# Optimizing a Trainium2 kernel written in Bass

```python
import numpy as np
import jax
import jax.numpy as jnp

def _softmax(x, axis=-1):
    return jax.nn.softmax(x, axis=axis)

def _gelu(x):
    return jax.nn.gelu(x, approximate=True)

def _silu(x):
    return jax.nn.silu(x)

def _sigmoid(x):
    return jax.nn.sigmoid(x)

def _layernorm(x, axis=-1, eps=1e-05):
    m = jnp.mean(x, axis=axis, keepdims=True)
    v = jnp.var(x, axis=axis, keepdims=True)
    return (x - m) / jnp.sqrt(v + eps)

def _scatter_add(tgt, idx, src, axis=0):
    return tgt.at[idx].add(src)

def _segment_sum(src, seg, n):
    return jax.ops.segment_sum(src, seg, n)
kernel_name = 'mk_gnn_preln_d2_gnn_r32_57039d'

def setup_inputs(seed: int=0):
    np.random.seed(seed)
    _w = jnp.asarray

    def _rec_inputs():
        import jax
        import jax.numpy as jnp
        _gk = jax.random.key(seed)
        x = -0.0003713 + 1 * jax.random.normal(jax.random.fold_in(_gk, 1), (3125, 128), jnp.float32)
        _s = jax.random.randint(jax.random.fold_in(_gk, 2), (50000,), 0, 3125, jnp.int32)
        _d = jax.random.randint(jax.random.fold_in(_gk, 3), (50000,), 0, 3125, jnp.int32)
        _loop = jnp.arange(3125, dtype=jnp.int32)
        src = jnp.concatenate([_s, _d, _loop])
        dst = jnp.concatenate([_d, _s, _loop])
        _o = jnp.argsort(dst, stable=True)
        src = src[_o]
        dst = dst[_o]
        edge_attr_16 = 0.000196303 + 1.00016 * jax.random.normal(jax.random.fold_in(_gk, 11), (103125, 16), jnp.float32)
        edge_weight = jax.random.uniform(jax.random.fold_in(_gk, 13), (103125,), jnp.float32, 0.0, 0.999999)
        return (x, src, dst, edge_attr_16, edge_weight)
    x, src, dst, edge_attr_16, edge_weight = _rec_inputs()

    def _L0_gnn_setup():
        import jax, jax.numpy as jnp
        import numpy as np
        N = 3125
        E = 50000
        D = 128
        NEG_SLOPE = 0.2
        LN_EPS = 1e-05
        key = jax.random.key(seed)
        ks = jax.random.split(key, 6)
        X = jax.random.normal(ks[0], (N, D), dtype=jnp.float32)
        M_ei = jax.random.randint(ks[1], (2, E), 0, N, dtype=jnp.int64)
        M_w = jax.random.uniform(ks[2], (E,), dtype=jnp.float32)
        W = jax.random.normal(ks[3], (D, D), dtype=jnp.float32) * 0.05
        a_src = jax.random.normal(ks[4], (D,), dtype=jnp.float32) * 0.05
        a_dst = jax.random.normal(ks[5], (D,), dtype=jnp.float32) * 0.05
        ln_gamma = jnp.ones((D,), dtype=jnp.float32)
        ln_beta = jnp.zeros((D,), dtype=jnp.float32)
        return {'X': X, 'M_ei': M_ei, 'M_w': M_w, 'W': W, 'a_src': a_src, 'a_dst': a_dst, 'ln_gamma': ln_gamma, 'ln_beta': ln_beta}
    _L0_gnn_all = _L0_gnn_setup()
    _L0_gnn_in = {k: v for k, v in _L0_gnn_all.items() if k in ('W', 'a_src', 'a_dst', 'ln_gamma', 'ln_beta')}
    del _L0_gnn_all

    def _L1_gnn_setup():
        import jax, jax.numpy as jnp
        import numpy as np
        N = 50000
        IN_DIM = 128
        OUT_DIM = 128
        EA_DIM = 16
        REQ_DIM = 16
        E_TOTAL = 50000

        def _directional_msg(x, src, dst, edge_attr, req, W1, b1, W2, b2, n_nodes):
            x_j = x[src]
            req_e = jnp.broadcast_to(req, (src.shape[0], req.shape[-1]))
            m = jnp.concatenate([x_j, edge_attr, req_e], axis=-1)
            h = jax.nn.relu(m @ W1 + b1) @ W2 + b2
            return jax.ops.segment_sum(h, dst, num_segments=n_nodes)
        key = jax.random.key(seed)
        ks = jax.random.split(key, 16)
        cat_dim = IN_DIM + EA_DIM + REQ_DIM
        s = 0.02
        return {'x': jax.random.normal(ks[0], (N, IN_DIM), dtype=jnp.float32), 'edge_index': jax.random.randint(ks[1], (2, E_TOTAL), 0, N, dtype=jnp.int32), 'edge_attr': jax.random.normal(ks[2], (E_TOTAL, EA_DIM), dtype=jnp.float32), 'req_emb': jax.random.normal(ks[3], (1, REQ_DIM), dtype=jnp.float32), 'W1f': jax.random.normal(ks[4], (cat_dim, OUT_DIM), dtype=jnp.float32) * s, 'b1f': jnp.zeros((OUT_DIM,), dtype=jnp.float32), 'W2f': jax.random.normal(ks[5], (OUT_DIM, OUT_DIM), dtype=jnp.float32) * s, 'b2f': jnp.zeros((OUT_DIM,), dtype=jnp.float32), 'W1b': jax.random.normal(ks[6], (cat_dim, OUT_DIM), dtype=jnp.float32) * s, 'b1b': jnp.zeros((OUT_DIM,), dtype=jnp.float32), 'W2b': jax.random.normal(ks[7], (OUT_DIM, OUT_DIM), dtype=jnp.float32) * s, 'b2b': jnp.zeros((OUT_DIM,), dtype=jnp.float32), 'Wu': jax.random.normal(ks[8], (OUT_DIM, OUT_DIM), dtype=jnp.float32) * s, 'bu': jnp.zeros((OUT_DIM,), dtype=jnp.float32), 'eps': jnp.zeros((1,), dtype=jnp.float32)}
    _L1_gnn_all = _L1_gnn_setup()
    _L1_gnn_in = {k: v for k, v in _L1_gnn_all.items() if k in ('req_emb', 'W1f', 'b1f', 'W2f', 'b2f', 'W1b', 'b1b', 'W2b', 'b2b', 'Wu', 'bu', 'eps')}
    del _L1_gnn_all
    return {'x': x, 'src': src, 'dst': dst, 'edge_attr_16': edge_attr_16, 'edge_weight': edge_weight, 'L0_gnn_W': _L0_gnn_in['W'], 'L0_gnn_a_src': _L0_gnn_in['a_src'], 'L0_gnn_a_dst': _L0_gnn_in['a_dst'], 'L0_gnn_ln_gamma': _L0_gnn_in['ln_gamma'], 'L0_gnn_ln_beta': _L0_gnn_in['ln_beta'], 'L1_gnn_req_emb': _L1_gnn_in['req_emb'], 'L1_gnn_W1f': _L1_gnn_in['W1f'], 'L1_gnn_b1f': _L1_gnn_in['b1f'], 'L1_gnn_W2f': _L1_gnn_in['W2f'], 'L1_gnn_b2f': _L1_gnn_in['b2f'], 'L1_gnn_W1b': _L1_gnn_in['W1b'], 'L1_gnn_b1b': _L1_gnn_in['b1b'], 'L1_gnn_W2b': _L1_gnn_in['W2b'], 'L1_gnn_b2b': _L1_gnn_in['b2b'], 'L1_gnn_Wu': _L1_gnn_in['Wu'], 'L1_gnn_bu': _L1_gnn_in['bu'], 'L1_gnn_eps': _L1_gnn_in['eps']}

def reference(x, src, dst, edge_attr_16, edge_weight, L0_gnn_W, L0_gnn_a_src, L0_gnn_a_dst, L0_gnn_ln_gamma, L0_gnn_ln_beta, L1_gnn_req_emb, L1_gnn_W1f, L1_gnn_b1f, L1_gnn_W2f, L1_gnn_b2f, L1_gnn_W1b, L1_gnn_b1b, L1_gnn_W2b, L1_gnn_b2b, L1_gnn_Wu, L1_gnn_bu, L1_gnn_eps):
    import jax
    import jax.numpy as jnp

    def _L0_gnn_ref(X, M_ei, M_w, W, a_src, a_dst, ln_gamma, ln_beta):
        import jax, jax.numpy as jnp
        import numpy as np
        N = 3125
        E = 50000
        D = 128
        NEG_SLOPE = 0.2
        LN_EPS = 1e-05
        n = X.shape[0]
        src, dst = (M_ei[0], M_ei[1])
        H = X @ W.T
        res = X
        e_src = H @ a_src
        e_dst = H @ a_dst
        e_ij = jax.nn.leaky_relu(e_src[src] + e_dst[dst], negative_slope=NEG_SLOPE)
        logits = M_w * e_ij
        seg_max = jax.ops.segment_max(logits, src, num_segments=n)
        ex = jnp.exp(logits - seg_max[src])
        denom = jax.ops.segment_sum(ex, src, num_segments=n)
        alpha = ex / denom[src]
        msg = H[dst] * alpha[:, None]
        Z = jax.ops.segment_sum(msg, src, num_segments=n)
        has_nb = jnp.zeros((n,), dtype=bool).at[src].set(True)
        Z = jnp.where(has_nb[:, None], Z, H)
        Zr = Z + res
        mu = jnp.mean(Zr, axis=-1, keepdims=True)
        var = jnp.mean(jnp.square(Zr - mu), axis=-1, keepdims=True)
        Zn = (Zr - mu) * jax.lax.rsqrt(var + LN_EPS) * ln_gamma + ln_beta
        return jax.nn.elu(Zn)

    def _L1_gnn_ref(x, edge_index, edge_attr, req_emb, W1f, b1f, W2f, b2f, W1b, b1b, W2b, b2b, Wu, bu, eps):
        import jax, jax.numpy as jnp
        import numpy as np
        N = 50000
        IN_DIM = 128
        OUT_DIM = 128
        EA_DIM = 16
        REQ_DIM = 16
        E_TOTAL = 50000

        def _directional_msg(x, src, dst, edge_attr, req, W1, b1, W2, b2, n_nodes):
            x_j = x[src]
            req_e = jnp.broadcast_to(req, (src.shape[0], req.shape[-1]))
            m = jnp.concatenate([x_j, edge_attr, req_e], axis=-1)
            h = jax.nn.relu(m @ W1 + b1) @ W2 + b2
            return jax.ops.segment_sum(h, dst, num_segments=n_nodes)
        n_nodes = x.shape[0]
        E = edge_index.shape[1] // 2
        req = req_emb.reshape(1, -1)
        x_self = x
        src_f, dst_f = (edge_index[0, :E], edge_index[1, :E])
        src_b, dst_b = (edge_index[0, E:], edge_index[1, E:])
        h_in = _directional_msg(x, src_f, dst_f, edge_attr[:E], req, W1f, b1f, W2f, b2f, n_nodes)
        h_out = _directional_msg(x, src_b, dst_b, edge_attr[E:], req, W1b, b1b, W2b, b2b, n_nodes)
        h = (1.0 + eps) * x_self + h_in + h_out
        return jax.nn.relu(h @ Wu + bu)
    edge_index = jnp.stack([src, dst])
    h = jnp.maximum(_layernorm(x, axis=-1), 0.0)
    x = x + _L0_gnn_ref(h, edge_index, edge_weight, L0_gnn_W, L0_gnn_a_src, L0_gnn_a_dst, L0_gnn_ln_gamma, L0_gnn_ln_beta)
    h = jnp.maximum(_layernorm(x, axis=-1), 0.0)
    x = x + _L1_gnn_ref(h, edge_index, edge_attr_16, L1_gnn_req_emb, L1_gnn_W1f, L1_gnn_b1f, L1_gnn_W2f, L1_gnn_b2f, L1_gnn_W1b, L1_gnn_b1b, L1_gnn_W2b, L1_gnn_b2b, L1_gnn_Wu, L1_gnn_bu, L1_gnn_eps)
    return x

_drawn_inputs = setup_inputs


def setup_inputs(seed=0):
    import zlib

    import numpy as np

    out = dict(_drawn_inputs(seed))
    spreads = {'L0_gnn_ln_gamma': (1.0, 0.2),
     'L0_gnn_ln_beta': (0.0, 0.1),
     'L1_gnn_b1f': (0.0, 0.276),
     'L1_gnn_b2f': (0.0, 0.1),
     'L1_gnn_b1b': (0.0, 0.391),
     'L1_gnn_b2b': (0.0, 0.1),
     'L1_gnn_bu': (0.0, 0.1)}
    factors = {'edge_attr_16': 8.0, 'edge_weight': 8.0, 'L0_gnn_a_src': 8.0, 'L0_gnn_a_dst': 8.0}
    for name, (base, spread) in spreads.items():
        noise = np.random.default_rng([zlib.crc32(name.encode()), seed]).standard_normal(out[name].shape)
        drawn = base * np.exp(spread * noise) if base else spread * noise
        out[name] = jnp.asarray(drawn.astype(out[name].dtype))
    for name, factor in factors.items():
        out[name] = (out[name] * factor).astype(out[name].dtype)
    return out
```

```python
from contextlib import ExitStack

import concourse.bass as bass
from concourse import mybir

ALU = mybir.AluOpType
ACT = mybir.ActivationFunctionType
AX = mybir.AxisListType
F32 = mybir.dt.float32
BF16 = mybir.dt.bfloat16
I32 = mybir.dt.int32

P = 128
D = 128
N = 3125
R = 125
NB = N // R
E = 103125
EH = (E // 2, E - E // 2)
B = 8
C = 3
TURN = B * C
HT = 17
NT = 2 * HT * TURN
Q = NT // B
ST = 35
NS = ST * TURN
RT = 7
RO = ST // RT
RING = RT * TURN
SW = NS + TURN
GW = D + 1
EA = 16
REQ = 16
TN = N + 1
WIN = 128
AW = N + WIN
EPS = 1e-5
SLOPE = 0.2
MAGIC = 12582912.0
FAR = 2.0 ** 55
NOMAX = 1e32
CH = 5

assert 2 * HT * TURN * P >= E and HT * TURN * P >= max(EH)
assert NS * P >= E + NB * (P - 1) and RO * RT == ST and NT % B == 0

C_ID, C_TRI, C_IOTA = 0, P, 2 * P
C_P = C_IOTA + NS
C_PB = C_P + 1
C_INC = C_PB + 1
C_W = C_INC + NB + 1


def turns(eng, count, body):
    body(0, True)
    with eng.Fori(1, count) as i:
        body(i, False)


def build(nc, a, out, scr):
    with ExitStack() as ctx:
        def sb(name, shape, dt):
            return ctx.enter_context(nc.sbuf_tensor(name, shape, dt))

        def sem(name):
            return ctx.enter_context(nc.semaphore(name))

        bank = [ctx.enter_context(nc.psum_tensor(f"bank{i}", [P, 512], F32)) for i in range(8)]

        cst = sb("cst", [P, C_W], F32)
        identb = sb("identb", [P, P], BF16)
        onesb = sb("onesb", [P, 1], BF16)
        onesf = sb("onesf", [P, P], F32)
        h0 = sb("h0", [R, NB, D], F32)
        hs = sb("hs", [P, NB, D], F32)
        maxes = sb("maxes", [P, (NB + 1) * R], F32)
        zacc = sb("zacc", [P, (NB + 1) * GW], F32)
        srt = sb("srt", [P, NS, 3], F32)
        sdst = sb("sdst", [P, NS], I32)
        far = sb("far", [P, NS], F32)
        srcg = sb("srcg", [P, NT], I32)
        rel = sb("rel", [P, NT], F32)
        offs = sb("offs", [1, 2, NS], I32)
        base = sb("base", [1, NT], I32)
        npass = sb("npass", [1, 1], I32)
        idxr = sb("idxr", [P, RING], I32)
        wt = sb("wt", [P, 7 * D], F32)
        small = sb("small", [P, 256], F32)
        arena = sb("arena", [P, RING * GW], F32)
        AR = RING * GW
        ring = arena[:, :].rearrange("p (s w) -> p s w", w=GW)

        ident = cst[:, C_ID:C_ID + P]
        tri = cst[:, C_TRI:C_TRI + P]
        iota = cst[:, C_IOTA:C_IOTA + NS]
        iota_p = cst[:, C_P:C_P + 1]
        iota_pb = cst[:, C_PB:C_PB + 1]
        inc = cst[:, C_INC:C_INC + NB + 1]

        def taker():
            at = [0]

            def take(n):
                n += n % 2
                v = arena[:, at[0]:at[0] + n]
                at[0] += n
                assert at[0] <= AR, at[0]
                return v
            return take

        take = taker()
        nat_i = take(2 * B * P).bitcast(I32)
        nat_r = take(B * P).bitcast(BF16)
        nat_b = take(B * P).bitcast(BF16)
        col_i = take(2 * NT).bitcast(I32)
        rec2 = take(2 * NT).rearrange("p (t a) -> p t a", a=2)
        cb = take(2 * NT)
        cr = take(2 * NT)
        cf = maxes[:, 0:2 * NT]
        ct = srt[:, :, :].rearrange("p s a -> p (s a)")[:, 0:2 * NT]
        wcol = take(NT)
        posf = take(NT)
        posi = take(NT).bitcast(I32)
        xin = maxes[:, 2 * NT:2 * NT + CH * D]
        xsq = maxes[:, 2 * NT + CH * D:2 * NT + 2 * CH * D]
        h0T = take(CH * P)
        recr = take(TURN * 3).rearrange("p (s a) -> p s a", a=3)
        posr = take(TURN).bitcast(I32)
        lk = take(B)
        oht = [take(256).bitcast(BF16) for _ in range(2)]
        vcp = [take(256).bitcast(BF16) for _ in range(2)]
        msk = [take(256).bitcast(BF16) for _ in range(2)]
        onehots = take(B * R + C * B * R // 2)
        nat_t = onehots[:, 0:2 * B * P]
        sqr = onehots[:, 0:B * R].rearrange("p (k r) -> p k r", r=R)
        ohr = [onehots[:, B * R + q * B * R // 2:B * R + (q + 1) * B * R // 2].bitcast(BF16).rearrange(
            "p (k r) -> p k r", r=R) for q in range(C)]
        ohb = [take(B * 2 * NB // 2).bitcast(BF16).rearrange("p (k r) -> p k r", r=2 * NB) for _ in range(C)]
        tb = take(3 * NB).bitcast(BF16).rearrange("p (a k) -> p a k", a=2)
        tf = take(2 * NB)
        brow = take(2 * NT)
        mcnt = take(R)[0:2 * NB, 0:R]
        fill2 = take(NS)
        ohb0 = take(NB).bitcast(BF16)[:, 0:2 * NB]
        fill_ = zacc[:, 0:SW * 3]
        fill = fill_.rearrange("p (s a) -> p s a", a=3)
        nat_f = fill_[:, 0:2 * B * P]
        cnt = take(NB + 1)
        laneoff = take(NB + 1)
        mv = take(4 * CH)
        sq_ = sb("sq_", [P, C * B * WIN], F32)
        sq = sq_[:, 0:TURN * R].rearrange("p (k r) -> p k r", r=R)
        sq2 = sb("sq2", [P, B, R], F32)
        junk = sb("junk", [P, B, R], BF16)
        me = sb("me", [P, TURN], F32)
        lm = sb("lm", [P, TURN], F32)
        mcol = sb("mcol", [R, NB], F32)
        take = taker()
        accT = [take(AW) for _ in range(2)]
        g1 = take(TURN * D).rearrange("p (c n) -> p c n", c=C)
        pre = take(TURN * D).rearrange("p (c n) -> p c n", c=C)
        eat = take(TURN * P).rearrange("p (c n) -> p c n", c=C)
        y1 = take(CH * D)
        y2 = take(CH * D)
        y3 = take(CH * D)
        y4 = take(CH * D)
        h1n = take(CH * D)
        pout = [take(2 * D) for _ in range(2)]
        gbc = take(2 * D)
        padrow = take(D)
        den = take(4 * NB)
        hT2 = take(512)
        mv2 = take(4 * CH)
        crow = take(2 * D)
        u2 = take(2 * D)
        oh1 = sq_[:, :].rearrange("p (c n) -> p c n", c=C)
        cntT = maxes[0:2, 0:N]
        h1T = hs[:, :, :].rearrange("p a b -> p (a b)")

        names = ("cst nati coli wcol x0 wl0 fill pat cols lanes laneoff rank tiles ends blkp blk H0T h0t Hp Hs Htab tq "
                 "nat xst lnv bcd ready ohtd vald vcpd mskd sumd logd ohr ohb cntd rfill turn sorted srtl sfar idx0 "
                 "sq mx mtr mred mbc mbcd g0turn lmd wd pvd fld med zdone x1l wl1 h1a h1b h1c Pp Pc pst cnp cns "
                 "cnr ea msg pso add gpre rels bases spd spr hw1 hf1 hf2 hf3 hf4 outd outs steps asteps c0 c1 u2d "
                 "dsteps onesd pass ohd sq2d cntc0 cntc1 counted nextw spturn zq ze r1 rr").split()
        s = {n: sem("s_" + n) for n in names}
        s_sc = [sem(f"s_sc{c}") for c in range(C)]
        s_g0 = [sem(f"s_g0_{c}") for c in range(C)]
        s_g1 = [sem(f"s_g1_{c}") for c in range(C)]
        s_pst = [sem(f"s_pst{k}") for k in range(2)]
        s_ld = [sem(f"s_ld{c}") for c in range(C)]
        block = ctx.enter_context(nc.Block())

        def c16(i, c):
            return C * i + c + 1

        @block.sync
        def _(sp):
            sp.dma_start(cst[:, :], a["cst"]).then_inc(s["cst"], 16)
            sp.dma_start(nat_i[0:Q, :], a["nat"]).then_inc(s["nati"], 16)
            sp.dma_start(col_i[:, :], a["col"]).then_inc(s["coli"], 16)
            sp.dma_start(wcol[:, :], a["w"]).then_inc(s["wcol"], 16)
            sp.dma_start(wt[:, 0:D], a["W"]).then_inc(s["wl0"], 16)
            sp.dma_start(wt[:, D:2 * D], a["WT"]).then_inc(s["wl0"], 16)
            sp.dma_start(wt[:, 2 * D:2 * D + 1], a["as"].rearrange("(p o) -> p o", o=1)).then_inc(s["wl0"], 16)
            sp.dma_start(wt[:, 2 * D + 1:2 * D + 2], a["ad"].rearrange("(p o) -> p o", o=1)).then_inc(s["wl0"], 16)
            xv = a["x"].rearrange("(b r) d -> r b d", r=R)
            for k in range(NB // CH):
                if k:
                    sp.wait_ge(s["lnv"], k)
                sp.dma_start(xin[0:R, :].rearrange("p (b d) -> p b d", d=D),
                             xv[:, CH * k:CH * (k + 1), :]).then_inc(s["x0"], 16)
            sp.wait_ge(s["pat"], 1)
            sp.dma_start(scr["rec"].rearrange("(p s) a -> p (s a)", p=P),
                         fill.rearrange("p s a -> p (s a)")).then_inc(s["fill"], 16)
            hv = scr["H"].rearrange("(b r) d -> r b d", r=R)
            for k in range(NB // CH):
                sp.wait_ge(s["Hs"], k + 1)
                sp.dma_start(hv[:, CH * k:CH * (k + 1), :], hs[0:R, CH * k:CH * (k + 1), :]).then_inc(s["Htab"], 16)
            sp.wait_ge(s["bases"], 1)
            sp.dma_start(scr["base"].rearrange("k (q c) -> q k c", q=Q),
                         small[0:Q, 0:2 * B].rearrange("p (k c) -> p k c", k=2)).then_inc(s["spd"], 16)
            sp.wait_ge(s["spd"], 16)
            sp.dma_start(rel[:, :], scr["base"][0:1, :].to_broadcast([P, NT])).then_inc(s["spr"], 16)
            sp.dma_start(brow[0:1, :], scr["base"].rearrange("(o k) t -> o (k t)", o=1)).then_inc(s["spr"], 16)

            sp.wait_ge(s["cnp"], 1)
            sp.dma_start(scr["cnt"].rearrange("(k r) -> k r", r=R), mcnt).then_inc(s["cns"], 16)

            for c in range(C):
                sp.wait_ge(s_sc[c], 16 * B * 2 * HT)
            sp.dma_start(srt[:, :, :].rearrange("p s a -> p (s a)"),
                         scr["rec"].rearrange("(p s) a -> p s a", p=P)[:, 0:NS, :].rearrange(
                             "p s a -> p (s a)")).then_inc(s["srtl"], 16)

            sp.wait_ge(s["sfar"], 1)
            def idx_round(o, first):
                for u in range(RT):
                    if not first:
                        for c in range(C):
                            sp.wait_ge(s_g0[c], o * (16 * B * RT) + 16 * B * (u + 1 - RT))
                            sp.sem_inc(s["spturn"], 1)
                    sp.dma_start(idxr[:, TURN * u:TURN * (u + 1)],
                                 sdst[:, bass.ds(o * RING + TURN * u, TURN)]).then_inc(s["idx0"], 16)
                    sp.wait_ge(s["idx0"], o * (16 * RT) + 16 * (u + 1))
                    sp.sem_inc(s["spturn"], 1)
            turns(sp, RO, idx_round)

            sp.wait_ge(s["zdone"], 1)
            sp.wait_ge(s["cns"], 16)
            sp.dma_start(cntT, scr["cnt"].rearrange("(h n) -> h n", h=2)).then_inc(s["cnr"], 16)
            for n_, c0_, w_ in (("W1f", 0, D), ("W1b", D, D), ("W2f", 2 * D, D), ("W2b", 3 * D, D), ("Wu", 4 * D, D)):
                sp.dma_start(wt[:, c0_:c0_ + w_], a[n_][0:D, :]).then_inc(s["wl1"], 16)
            sp.dma_start(wt[0:EA, 5 * D:6 * D], a["W1f"][D:D + EA, :]).then_inc(s["wl1"], 16)
            sp.dma_start(wt[0:EA, 6 * D:7 * D], a["W1b"][D:D + EA, :]).then_inc(s["wl1"], 16)
            sp.dma_start(y1[0:REQ, 0:D], a["W1f"][D + EA:D + EA + REQ, :]).then_inc(s["wl1"], 16)
            sp.dma_start(y1[0:REQ, D:2 * D], a["W1b"][D + EA:D + EA + REQ, :]).then_inc(s["wl1"], 16)
            sp.dma_start(small[0:REQ, 0:1], a["req"].rearrange("o p -> p o")).then_inc(s["wl1"], 16)
            sp.dma_start(crow[0:1, 0:D], a["b1f"].rearrange("(o p) -> o p", o=1)).then_inc(s["wl1"], 16)
            sp.dma_start(crow[0:1, D:2 * D], a["b1b"].rearrange("(o p) -> o p", o=1)).then_inc(s["wl1"], 16)
            sp.dma_start(small[:, 1:2], a["b2f"].rearrange("(p o) -> p o", o=1)).then_inc(s["wl1"], 16)
            sp.dma_start(small[:, 2:3], a["b2b"].rearrange("(p o) -> p o", o=1)).then_inc(s["wl1"], 16)
            sp.dma_start(small[:, 3:4], a["eps"].rearrange("(o p) -> o p", o=1).to_broadcast([P, 1])).then_inc(s["wl1"], 16)
            sp.dma_start(small[0:1, 128:256], a["bu"].rearrange("(o p) -> o p", o=1)).then_inc(s["wl1"], 16)
            sp.dma_start(gbc[:, 0:D], a["gamma"].rearrange("(o p) -> o p", o=1).to_broadcast([P, D])).then_inc(s["wl1"], 16)
            sp.dma_start(gbc[:, D:2 * D], a["beta"].rearrange("(o p) -> o p", o=1).to_broadcast([P, D])).then_inc(s["wl1"], 16)
            pv = scr["PP"].rearrange("(h n) d -> n h d", h=2)
            for k in range(NB // CH + 1):
                if k < NB // CH:
                    if k:
                        sp.wait_ge(s["h1a"], k)
                    sp.dma_start(y4[0:R, :].rearrange("p (b d) -> p b d", d=D),
                                 xv[:, CH * k:CH * (k + 1), :]).then_inc(s["x1l"], 16)
                if k:
                    for b in range(CH * (k - 1), CH * k):
                        sp.wait_ge(s["Pc"], b + 1)
                        sp.dma_start(pv[R * b:R * (b + 1), :, :],
                                     pout[b % 2][0:R, :].rearrange("p (h d) -> p h d", h=2)).then_inc(s_pst[b % 2], 16)
            sp.dma_start(pv[N:N + 1, :, :], padrow[0:2, :]).then_inc(s_pst[0], 16)

            passes = sp.value_load(npass[0:1, 0:1], min_val=1, max_val=NB)
            with sp.Fori(0, passes) as kp:
                for h in range(2):
                    def load_turn(i, first, h=h):
                        for c in range(C):
                            tt = kp * (2 * HT) + (h * HT + i)
                            t0 = i * TURN + (h * HT * TURN + B * c)
                            if not first:
                                sp.wait_ge(s_g1[c], tt * (16 * B))
                                sp.sem_inc(s["spturn"], 1)
                                sp.wait_ge(s["ea"], tt * C + (c + 1 - C))
                                sp.sem_inc(s["spturn"], 1)
                            sp.dma_start(eat[0:EA, c, :], a["eaT"][:, bass.ds(t0 * P, B * P)]).then_inc(s_ld[c], 16)
                            sp.dma_start(idxr[:, B * c:B * (c + 1)], srcg[:, bass.ds(t0, B)]).then_inc(s_ld[c], 16)
                    turns(sp, HT, load_turn)
                    sp.wait_ge(s["fld"], ((kp * 2 + (h + 1)) * HT) * TURN + NS)
                    sp.sem_inc(s["spturn"], 1)
            ov = out.rearrange("(b r) d -> r b d", r=R)
            for b in range(NB):
                sp.wait_ge(s["outd"], b + 1)
                sp.dma_start(ov[:, b, :], h0[:, b, :]).then_inc(s["outs"], 16)
            sp.wait_ge(s["outs"], 16 * NB)

        @block.gpsimd
        def _(pool):
            pool.wait_ge(s["fill"], 16)
            def scatter_turn(i, first):
                for c in range(C):
                    if not first:
                        pool.wait_ge(s_sc[c], i * (16 * B))
                    pool.wait_ge(s["rfill"], c16(i, c))
                    pool.wait_ge(s["logd"], c16(i, c))
                    pool.sem_inc(s["turn"], 1)
                    for k in range(B * c, B * (c + 1)):
                        pool.indirect_dma_start(scr["rec"], bass.IndirectOffsetOnAxis(ap=posr[:, k:k + 1], axis=0),
                                                recr[:, k, :], None).then_inc(s_sc[c], 16)
            turns(pool, 2 * HT, scatter_turn)

            pool.wait_ge(s["Htab"], 16 * (NB // CH))
            pool.wait_ge(s["onesd"], 1)
            def gather_round(o, first):
                for u in range(RT):
                    pool.wait_ge(s["idx0"], o * (16 * RT) + 16 * (u + 1))
                    for c in range(C):
                        if not (first and u == 0):
                            pool.wait_ge(s_g0[c], o * (16 * B * RT) + 16 * B * u)
                        if not first:
                            pool.wait_ge(s["pvd"], o * RING + (TURN * u + B * (c + 1) - RING))
                        pool.sem_inc(s["turn"], 1)
                        for k in range(TURN * u + B * c, TURN * u + B * (c + 1)):
                            pool.indirect_dma_start(ring[:, k, 0:D], None, scr["H"],
                                                    bass.IndirectOffsetOnAxis(ap=idxr[:, k:k + 1], axis=0)
                                                    ).then_inc(s_g0[c], 16)
            turns(pool, RO, gather_round)

            pool.wait_ge(s_pst[0], 16 * (NB // 2 + 2))
            pool.wait_ge(s_pst[1], 16 * (NB // 2))
            passes = pool.value_load(npass[0:1, 0:1], min_val=1, max_val=NB)
            with pool.Fori(0, passes) as kp:
                for h in range(2):
                    def msg_turn(i, first, h=h):
                        tt = kp * (2 * HT) + (h * HT + i)
                        for c in range(C):
                            pool.wait_ge(s_ld[c], tt * 32 + 32)
                            if not first:
                                pool.wait_ge(s["add"], tt * C + (c + 1 - C))
                            pool.sem_inc(s["turn"], 1)
                            for k in range(B):
                                pool.indirect_dma_start(g1[:, c, k * D:(k + 1) * D], None, scr["PP"],
                                                        bass.IndirectOffsetOnAxis(
                                                            ap=idxr[:, B * c + k:B * c + k + 1], axis=0)
                                                        ).then_inc(s_g1[c], 16)
                    turns(pool, HT, msg_turn)
                    pool.wait_ge(s["fld"], ((kp * 2 + (h + 1)) * HT) * TURN + NS)

        @block.scalar
        def _(act):
            n_step = [0]

            def link(ins):
                n_step[0] += 1
                ins.then_inc(s["asteps"], 1)
                act.wait_ge(s["asteps"], n_step[0])

            act.wait_ge(s["cst"], 16)
            link(act.copy(identb[:, :], ident))
            for k in range(NB // CH):
                act.wait_ge(s["xst"], 2 * k + 1)
                act.activation(xsq[0:R, :], h0[:, CH * k:CH * (k + 1), :].rearrange("p b d -> p (b d)"),
                               ACT.Square).then_inc(s["zq"], 1)
                act.wait_ge(s["xst"], 2 * k + 2)
                act.activation(mv[0:R, CH:2 * CH], mv[0:R, 0:CH], ACT.Sqrt).then_inc(s["zq"], 1)
            for b in range(NB):
                act.wait_ge(s["H0T"], b + 1)
                act.copy(h0T[:, (b % CH) * P:(b % CH) * P + R], bank[b % 2][:, 0:R]).then_inc(s["h0t"], 1)

            def fill_turn(i, first):
                for c in range(C):
                    t0 = i * TURN + B * c
                    if not first:
                        act.wait_ge(s_sc[c], i * (16 * B))
                    act.copy(recr[:, B * c:B * (c + 1), 0:2], rec2[:, bass.ds(t0, B), :]).then_inc(s["rr"], 1)
                    act.copy(posr[:, B * c:B * (c + 1)], posi[:, bass.ds(t0, B)]).then_inc(s["rr"], 1)
                    act.wait_ge(s["rr"], (C * i + c) * 2 + 2)
                    act.sem_inc(s["rfill"], 1)
                    if not first:
                        act.wait_ge(s["cntd"], C * i + (c + 1 - C))
                    if not (first and c == 0):
                        act.wait_ge(s["ohr"], C * i + c)
                    for k in range(B):
                        act.activation(sqr[:, k, :], iota[:, 0:R], ACT.Square,
                                       bias=cr[:, bass.ds(NT + t0 + k, 1)]).then_inc(s["r1"], 1)
                    act.wait_ge(s["r1"], i * TURN + B * (c + 1))
                    act.activation(ohr[c], sqr, ACT.Relu, scale=-1.0, bias=onesf[:, 0:1]).then_inc(s["ohr"], 1)
                    for j in range(B // 2):
                        m = (B // 2) * c + j
                        pr = i * (TURN // 2) + m
                        act.wait_ge(s["vald"], pr + 1)
                        if not (first and m < 2):
                            act.wait_ge(s["mskd"], pr - 1)
                        act.copy(vcp[m % 2][0:3 * NB, :], bank[4 + m % 2][0:3 * NB, :]).then_inc(s["vcpd"], 1)
            act.wait_ge(s["ready"], 1)
            turns(act, 2 * HT, fill_turn)

            act.wait_ge(s["sfar"], 1)
            def dist_turn(T, first):
                for k in range(TURN):
                    if not first:
                        act.wait_ge(s["mx"], T * TURN + (k + 1 - TURN))
                    act.activation(sq[:, k, :], iota[:, 0:R], ACT.Square, scale=FAR,
                                   bias=far[:, bass.ds(T * TURN + k, 1)]).then_inc(s["sq"], 1)
            turns(act, ST, dist_turn)
            for g in range((NB + 3) // 4):
                w = min(4, NB - 4 * g) * R
                act.wait_ge(s["mbc"], g + 1)
                act.copy(maxes[:, 4 * g * R:4 * g * R + w], bank[4 + g % 4][:, 0:w]).then_inc(s["mbcd"], 1)
            def exp_turn(T, first):
                for c in range(C):
                    if not (first and c == 0):
                        act.wait_ge(s["wd"], T * TURN + B * c)
                    for k in range(B):
                        act.activation(sq2[:, k, :], iota[:, 0:R], ACT.Square, scale=FAR,
                                       bias=far[:, bass.ds(T * TURN + B * c + k, 1)]).then_inc(s["sq2d"], 1)
                    act.wait_ge(s["sq2d"], T * TURN + B * (c + 1))
                    act.wait_ge(s["lmd"], c16(T, c))
                    if not first:
                        act.wait_ge(s["pvd"], T * TURN + (B * (c + 1) - TURN))
                    for k in range(B):
                        act.activation(sq[:, B * c + k, :], sq2[:, k, :], ACT.Exp, scale=-1.0,
                                       bias=lm[:, B * c + k:B * c + k + 1]).then_inc(s["wd"], 1)
            turns(act, ST, exp_turn)

            for k in range(NB // CH):
                act.wait_ge(s["h1b"], 3 * k + 1)
                act.activation(y2[0:R, :], y1[0:R, :], ACT.Square).then_inc(s["ze"], 1)
                act.wait_ge(s["h1b"], 3 * k + 2)
                act.activation(mv2[0:R, CH:2 * CH], mv2[0:R, 0:CH], ACT.Sqrt).then_inc(s["ze"], 1)
                act.wait_ge(s["h1b"], 3 * k + 3)
                act.activation(y2[0:R, :], y2[0:R, :], ACT.Exp).then_inc(s["ze"], 1)
                act.wait_ge(s["h1c"], 2 * k + 1)
                act.activation(y3[0:R, :], y1[0:R, :], ACT.Square).then_inc(s["ze"], 1)
                act.wait_ge(s["h1c"], 2 * k + 2)
                act.activation(mv2[0:R, CH:2 * CH], mv2[0:R, 0:CH], ACT.Sqrt).then_inc(s["ze"], 1)
                for b in range(CH * k, CH * (k + 1)):
                    act.wait_ge(s["hw1"], b + 1)
                    act.copy(h1T[:, R * b:R * (b + 1)], bank[b % 2][:, 0:R]).then_inc(s["hf1"], 1)
                    act.wait_ge(s["Pp"], b + 1)
                    if b >= 2:
                        act.wait_ge(s_pst[b % 2], 16 * (b // 2))
                    act.copy(pout[b % 2][0:R, :], bank[2 + b % 2][0:R, 0:2 * D]).then_inc(s["Pc"], 1)
            act.wait_ge(s["zdone"], 1)
            passes = act.value_load(npass[0:1, 0:1], min_val=1, max_val=NB)
            with act.Fori(0, passes) as kp:
                for h in range(2):
                    def relu_turn(i, first, h=h):
                        tt = kp * (2 * HT) + (h * HT + i)
                        for c in range(C):
                            act.wait_ge(s["add"], tt * C + (c + 1))
                            act.activation(pre[:, c, :], pre[:, c, :], ACT.Relu).then_inc(s["msg"], 1)
                    turns(act, HT, relu_turn)

        @block.tensor
        def _(pe):
            pe.wait_ge(s["cst"], 16)
            pe.wait_ge(s["wl0"], 64)
            pe.matmul(bank[2][:, 0:2], wt[:, 0:D], wt[:, 2 * D:2 * D + 2], start=True, stop=True).then_inc(s["c0"], 1)
            pe.wait_ge(s["c1"], 1)
            for k in range(NB // CH):
                pe.wait_ge(s["lnv"], k + 1)
                for b in range(CH * k, CH * (k + 1)):
                    if b >= 2:
                        pe.wait_ge(s["h0t"], b - 1)
                    pe.transpose(bank[b % 2][:, 0:R], h0[:, b, :], ident[0:R, 0:R]).then_inc(s["H0T"], 1)
                    pe.wait_ge(s["h0t"], b + 1)
                    if b >= 2:
                        pe.wait_ge(s["Hp"], b - 1)
                    pe.matmul(bank[2 + b % 2][0:R, 0:D + 2], h0T[:, (b % CH) * P:(b % CH) * P + R],
                              wt[:, D:2 * D + 2], start=True, stop=True).then_inc(s["tq"], 1)
            pe.wait_ge(s["lanes"], 1)
            pe.matmul(bank[6][0:NB + 1, 0:1], cnt, onesf[:, 0:1], start=True, stop=True).then_inc(s["cols"], 1)
            pe.wait_ge(s["tiles"], 1)
            pe.matmul(bank[6][0:NB + 1, 1:2], inc[0:NB + 1, :], small[0:NB + 1, 32:33],
                      start=True, stop=True).then_inc(s["ends"], 1)
            pe.matmul(bank[7][:, 0:NB + 1], small[0:NB + 1, 34:35].to_broadcast([NB + 1, P]), tri[0:NB + 1, 0:NB + 1],
                      start=True, stop=False)
            pe.matmul(bank[7][:, 0:NB + 1], tri, cnt, start=False, stop=True).then_inc(s["laneoff"], 1)
            pe.wait_ge(s["blkp"], 1)
            for g in range(2):
                pe.matmul(bank[2 + g][0:1, 0:NS // 2], onesf[0:NB, 0:1], fill2[0:NB, g * (NS // 2):(g + 1) * (NS // 2)],
                          start=True, stop=True).then_inc(s["blk"], 1)

            pe.wait_ge(s["ready"], 1)
            pe.wait_ge(s["asteps"], 1)
            zero = bank[7][0:R, 0:2 * NB]
            pe.matmul(zero, identb[:, 0:R], ohb0, start=True, stop=False)

            def spread(i, m):
                c, j = m // (B // 2), m % (B // 2)
                sel = identb[0:Q, bass.ds(C * i + c, 1)]
                for a_ in range(2):
                    o = a_ * B * P + 256 * j
                    pe.matmul(bank[m % 2][:, 256 * a_:256 * (a_ + 1)], sel.to_broadcast([Q, P]),
                              nat_r[0:Q, o:o + 256], start=True, stop=True)
                for a_ in range(2):
                    o = a_ * B * P + 256 * j
                    mm = pe.matmul(bank[2 + m % 2][0:3 * NB, 256 * a_:256 * (a_ + 1)], sel.to_broadcast([Q, 3 * NB]),
                                   nat_b[0:Q, o:o + 256], start=True, stop=True)
                mm.then_inc(s["bcd"], 1)

            spread(0, 0)

            def logit_turn(i, first):
                for m in range(TURN // 2):
                    c, j = m // (B // 2), m % (B // 2)
                    pr = i * (TURN // 2) + m
                    if not (first and m == 0):
                        pe.wait_ge(s["ohtd"], pr)
                        pe.wait_ge(s["mskd"], pr)
                    if m + 1 < TURN // 2:
                        spread(i, m + 1)
                    else:
                        spread(i + 1, 0)
                    pe.wait_ge(s["ohtd"], pr + 1)
                    if not (first and m < 2):
                        pe.wait_ge(s["vcpd"], pr - 1)
                    for a_ in range(2):
                        mm = pe.matmul(bank[4 + m % 2][0:3 * NB, 256 * a_:256 * (a_ + 1)], tb[0:R, a_, 0:3 * NB],
                                       oht[m % 2][0:R, 256 * a_:256 * (a_ + 1)], start=True, stop=True)
                    mm.then_inc(s["vald"], 1)
                    if j == 0:
                        pe.wait_ge(s["ohr"], c16(i, c))
                        pe.wait_ge(s["ohb"], c16(i, c))
                        for k in range(B):
                            mm = pe.matmul(zero, ohr[c][:, k, :], ohb[c][:, k, :], start=False, stop=False)
                        mm.then_inc(s["cntd"], 1)
                    pe.wait_ge(s["mskd"], pr + 1)
                    if j == 0 and not (first and c == 0):
                        pe.wait_ge(s["logd"], C * i + c)
                    for u in range(2):
                        col = bank[6][:, 2 * m + u:2 * m + u + 1]
                        for a_ in range(2):
                            mm = pe.matmul(col, msk[m % 2][0:3 * NB, 256 * a_ + P * u:256 * a_ + P * (u + 1)],
                                           onesb[0:3 * NB, 0:1], start=(a_ == 0), stop=(a_ == 1))
                    if j == B // 2 - 1:
                        mm.then_inc(s["sumd"], 1)
            turns(pe, 2 * HT, logit_turn)
            pe.matmul(zero, identb[:, 0:R], ohb0, start=False, stop=True).then_inc(s["counted"], 1)
            pe.wait_ge(s["cntc0"], 1)
            pe.wait_ge(s["logd"], 2 * HT * C)
            pe.transpose(bank[6][0:2 * NB, 128:128 + R], small[0:R, 64:64 + 2 * NB], ident[0:R, 0:R]
                         ).then_inc(s["cntc1"], 1)

            for b in range(NB):
                if b == 0:
                    pe.wait_ge(s["mx"], NS)
                    pe.wait_ge(s["cnp"], 1)
                if b >= 4:
                    pe.wait_ge(s["mred"], b - 3)
                pe.transpose(bank[b % 4][0:R, 0:P], maxes[:, R * b:R * (b + 1)], ident).then_inc(s["mtr"], 1)
            pe.wait_ge(s["mred"], NB + 1)
            for b in range(NB):
                g = b // 4
                if g >= 4 and b % 4 == 0:
                    pe.wait_ge(s["mbcd"], g - 3)
                mm = pe.matmul(bank[4 + g % 4][:, R * (b % 4):R * (b % 4 + 1)], mcol[:, b:b + 1].to_broadcast([R, P]),
                               ident[0:R, 0:R], start=True, stop=True)
                if b % 4 == 3 or b == NB - 1:
                    mm.then_inc(s["mbc"], 1)
            pe.wait_ge(s["mbcd"], (NB + 3) // 4)

            def sum_turn(T, first, o, u):
                for k in range(TURN):
                    if k % B == 0:
                        pe.wait_ge(s_g0[k // B], T * (16 * B) + 16 * B)
                    pe.wait_ge(s["wd"], T * TURN + (k + 1))
                    if not (first and k < 8):
                        pe.wait_ge(s["fld"], T * TURN + (k - 7))
                    pe.matmul(bank[k % 8][0:R, 0:GW], sq[:, k, :],
                              ring[:, bass.ds(u * TURN + k, 1), :].rearrange("p a w -> p (a w)"),
                              start=True, stop=True).then_inc(s["pvd"], 1)
            sum_turn(0, True, 0, 0)
            with pe.Fori(1, RT) as u:
                sum_turn(u, False, 0, u)
            with pe.Fori(1, RO) as o:
                with pe.Fori(0, RT) as u:
                    sum_turn(o * RT + u, False, o, u)

            pe.wait_ge(s["wl1"], 16 * 18)
            pe.wait_ge(s["fld"], NS)
            pe.matmul(bank[4][0:1, 0:2 * D], small[0:REQ, 0:1], y1[0:REQ, 0:2 * D],
                      start=True, stop=True)
            pe.matmul(bank[5][0:2, 0:D], small[:, 1:3], wt[:, 4 * D:5 * D], start=True, stop=True).then_inc(s["u2d"], 1)
            for k in range(NB // CH):
                pe.wait_ge(s["pass"], k + 1)
                for b in range(CH * k, CH * (k + 1)):
                    if b >= 2:
                        pe.wait_ge(s["hf1"], b - 1)
                        pe.wait_ge(s["Pc"], b - 1)
                    pe.transpose(bank[b % 2][:, 0:R], h1n[0:R, (b % CH) * D:(b % CH + 1) * D], ident[0:R, 0:R]
                                 ).then_inc(s["hw1"], 1)
                    pe.wait_ge(s["hf1"], b + 1)
                    pe.matmul(bank[2 + b % 2][0:R, 0:2 * D], h1T[:, R * b:R * (b + 1)], wt[:, 0:2 * D],
                              start=True, stop=False)
                    pe.matmul(bank[2 + b % 2][0:R, 0:2 * D], onesf[0:1, 0:R], crow[0:1, :],
                              start=False, stop=True).then_inc(s["Pp"], 1)
            pe.wait_ge(s["Pc"], NB)

            passes = pe.value_load(npass[0:1, 0:1], min_val=1, max_val=NB)
            with pe.Fori(0, passes) as kp:
                for h in range(2):
                    def seg(nb, c, skip):
                        pe.wait_ge(s["msg"], nb + 1)
                        pe.wait_ge(s["ohd"], nb + 1)
                        for k in range(B):
                            if k % 4 == 0 and not skip:
                                pe.wait_ge(s["fld"], nb * B + (NS + k + 4 - B))
                            pe.matmul(bank[6 + k // 4][:, P * (k % 4):P * (k % 4 + 1)], pre[:, c, k * D:(k + 1) * D],
                                      oh1[:, c, k * WIN:(k + 1) * WIN], start=True, stop=True).then_inc(s["pso"], 1)

                    def msg_turn(i, first, h=h):
                        tt = kp * (2 * HT) + (h * HT + i)
                        for c in range(C):
                            nb = tt * C + c
                            pe.wait_ge(s_ld[c], tt * 32 + 32)
                            if not first:
                                pe.wait_ge(s["add"], nb + (1 - C))
                            for k in range(B):
                                mm = pe.matmul(bank[2 * c + k // 4][:, P * (k % 4):P * (k % 4 + 1)],
                                               eat[0:EA, c, k * P:(k + 1) * P],
                                               wt[0:EA, (5 + h) * D:(6 + h) * D], start=True, stop=True)
                            mm.then_inc(s["ea"], 1)
                            if not (first and c == 0):
                                seg(nb - 1, (c - 1) % C, first and c == 1)
                    turns(pe, HT, msg_turn)
                    seg(kp * (2 * HT * C) + ((h + 1) * HT * C - 1), C - 1, False)
                    pe.wait_ge(s["fld"], ((kp * 2 + (h + 1)) * HT) * TURN + NS)

            pe.wait_ge(s["u2d"], 2)
            pe.wait_ge(s["cnr"], 16)
            for b in range(NB):
                n0 = R * b
                if b >= 2:
                    pe.wait_ge(s["hf3"], b - 1)
                pe.matmul(bank[b % 2][:, 0:R], wt[:, 2 * D:3 * D], accT[0][:, n0:n0 + R], start=True, stop=False)
                pe.matmul(bank[b % 2][:, 0:R], wt[:, 3 * D:4 * D], accT[1][:, n0:n0 + R],
                          start=False, stop=True).then_inc(s["hf2"], 1)
                pe.wait_ge(s["hf3"], b + 1)
                if b >= 2:
                    pe.wait_ge(s["outd"], b - 1)
                o = bank[2 + b % 2][0:R, 0:D]
                pe.matmul(o, hT2[:, P * (b % 4):P * (b % 4) + R], wt[:, 4 * D:5 * D], start=True, stop=False)
                pe.matmul(o, cntT[:, n0:n0 + R], u2[0:2, 0:D], start=False, stop=False)
                pe.matmul(o, onesf[0:1, 0:R], small[0:1, 128:256], start=False, stop=True).then_inc(s["hf4"], 1)

        @block.vector
        def _(dve):
            n_step = [0]

            def link(ins):
                n_step[0] += 1
                ins.then_inc(s["dsteps"], 1)
                dve.wait_ge(s["dsteps"], n_step[0])

            def signal(name, ins):
                link(ins)
                dve.sem_inc(s[name], 1)

            def divmod_r(v, t, b, r):
                link(dve.tensor_scalar(t, v, 0.5, 1.0 / R, ALU.add, ALU.mult))
                link(dve.tensor_scalar(t, t, -0.5, MAGIC, ALU.add, ALU.add))
                link(dve.tensor_scalar(t, t, -MAGIC, None, ALU.add))
                link(dve.scalar_tensor_tensor(r, t, -float(R), v, ALU.mult, ALU.add))
                link(dve.tensor_copy(b, t))

            def bc(v, d):
                return v.rearrange("p (b o) -> p b o", o=1).to_broadcast([R, CH, d])

            link(dve.memset(onesf[:, :], 1.0))
            link(dve.memset(onesb[:, :], 1.0))
            link(dve.memset(fill[:, :, 0:1], -1.0))
            signal("pat", dve.memset(fill[:, :, 1:3], 0.0))
            dve.wait_ge(s["c0"], 1)
            link(dve.tensor_copy(wt[:, 2 * D:2 * D + 2], bank[2][:, 0:2]))
            dve.sem_inc(s["c1"], 1)
            for k in range(NB // CH):
                hk = h0[:, CH * k:CH * (k + 1), :]
                hk2 = hk.rearrange("p b d -> p (b d)")
                x3 = xin[0:R, :].rearrange("p (b d) -> p b d", d=D)
                sq3 = xsq[0:R, :].rearrange("p (b d) -> p b d", d=D)
                m1, m2, m3 = mv[0:R, 0:CH], mv[0:R, CH:2 * CH], mv[0:R, 2 * CH:3 * CH]
                dve.wait_ge(s["x0"], 16 * (k + 1))
                link(dve.tensor_reduce(m3, x3, AX.X, ALU.add))
                link(dve.tensor_scalar(m3, m3, 1.0 / D, None, ALU.mult))
                signal("xst", dve.tensor_tensor(hk, x3, bc(m3, D), ALU.subtract))
                dve.wait_ge(s["zq"], 2 * k + 1)
                link(dve.tensor_reduce(m1, sq3, AX.X, ALU.add))
                signal("xst", dve.tensor_scalar(m1, m1, 1.0 / D, EPS, ALU.mult, ALU.add))
                dve.wait_ge(s["zq"], 2 * k + 2)
                link(dve.reciprocal(m3, m2))
                link(dve.tensor_tensor(hk, hk, bc(m3, D), ALU.mult))
                signal("lnv", dve.tensor_scalar(hk2, hk2, 0.0, None, ALU.max))
            for b in range(NB):
                dve.wait_ge(s["tq"], b + 1)
                link(dve.tensor_copy(hs[0:R, b, :], bank[2 + b % 2][0:R, 0:D]))
                signal("Hp", dve.tensor_copy(tf[0:R, :].rearrange("p (a k) -> p a k", a=2)[:, :, b],
                                             bank[2 + b % 2][0:R, D:D + 2]))
                if b % CH == CH - 1:
                    dve.sem_inc(s["Hs"], 1)
            for p_ in range(3):
                part = tb[0:R, :, NB * p_:NB * (p_ + 1)]
                t3 = tf[0:R, :].rearrange("p (a k) -> p a k", a=2)
                link(dve.tensor_copy(part, t3))
                if p_ < 2:
                    link(dve.tensor_tensor(t3, t3, part, ALU.subtract))
            dve.wait_ge(s["nati"], 16)
            dve.wait_ge(s["fill"], 16)
            link(dve.tensor_copy(nat_f[0:Q, :], nat_i[0:Q, :]))
            divmod_r(nat_f[0:Q, :], nat_t[0:Q, :], nat_b[0:Q, :], nat_r[0:Q, :])
            dn = nat_f[0:Q, B * P:2 * B * P].rearrange("p (c e) -> p c e", c=B)
            link(dve.tensor_reduce(small[0:Q, 0:B], dn, AX.X, ALU.min))
            link(dve.tensor_reduce(small[0:Q, B:2 * B], dn, AX.X, ALU.max))
            signal("bases", dve.tensor_tensor(small[0:Q, B:2 * B], small[0:Q, B:2 * B], small[0:Q, 0:B], ALU.subtract))
            dve.wait_ge(s["coli"], 16)
            link(dve.tensor_copy(cf[:, :], col_i[:, :]))
            divmod_r(cf[:, :], ct[:, :], cb[:, :], cr[:, :])
            link(dve.tensor_copy(rec2[:, :, 0], cr[:, 0:NT]))
            link(dve.tensor_copy(rec2[:, :, 1], cf[:, NT:2 * NT]))
            link(dve.tensor_scalar(cr[:, NT:2 * NT], cr[:, NT:2 * NT], -1.0, None, ALU.mult))
            link(dve.tensor_scalar(ct[:, 0:NT], cb[:, 0:NT], float(NB), 1000.0, ALU.is_equal, ALU.mult))
            link(dve.tensor_tensor(cb[:, NT:2 * NT], cb[:, NT:2 * NT], ct[:, 0:NT], ALU.add))
            hb = cb[:, NT + NT // 2:2 * NT]
            link(dve.tensor_scalar(hb, hb, float(NB), None, ALU.add))
            link(dve.tensor_copy(srcg[:, 0:NT // 2], col_i[:, 0:NT // 2]))
            link(dve.tensor_scalar(srcg[:, NT // 2:NT], col_i[:, NT // 2:NT], float(TN), None, ALU.add))
            m_, sc_ = ct[:, 0:NT], ct[:, NT:2 * NT]
            link(dve.memset(posf[:, :], 0.0))
            bs = cb[:, 0:NT]
            for k in range(NB + 1):
                link(dve.tensor_scalar(m_, bs, float(k), None, ALU.is_equal))
                link(dve.tensor_tensor_scan(sc_, m_, m_, 0.0, ALU.add, ALU.max))
                link(dve.tensor_copy(cnt[:, k:k + 1], sc_[:, NT - 1:NT]))
                link(dve.tensor_tensor(m_, m_, sc_, ALU.mult))
                link(dve.tensor_tensor(posf[:, :], posf[:, :], m_, ALU.add))
            dve.sem_inc(s["lanes"], 1)
            dve.wait_ge(s["cols"], 1)
            tl, te = small[0:NB + 1, 32:33], small[0:NB + 1, 33:34]
            link(dve.tensor_scalar(tl, bank[6][0:NB + 1, 0:1], float(P - 1), 1.0 / P, ALU.add, ALU.mult))
            link(dve.tensor_scalar(tl, tl, -(P - 1) / (2.0 * P), MAGIC, ALU.add, ALU.add))
            link(dve.tensor_scalar(tl, tl, -MAGIC, None, ALU.add))
            signal("tiles", dve.tensor_scalar(small[0:NB + 1, 34:35], tl, float(P), None, ALU.mult))
            dve.wait_ge(s["ends"], 1)
            link(dve.tensor_copy(te, bank[6][0:NB + 1, 1:2]))
            signal("blkp", dve.tensor_scalar(fill2[0:NB, :], iota[0:NB, :], te[0:NB, :], None, ALU.is_ge))
            dve.wait_ge(s["laneoff"], 1)
            link(dve.tensor_scalar(laneoff[:, :], bank[7][:, 0:NB + 1], -1.0, None, ALU.add))
            for k in range(NB + 1):
                link(dve.tensor_scalar(m_, bs, float(k), laneoff[:, k:k + 1], ALU.is_equal, ALU.mult))
                link(dve.tensor_tensor(posf[:, :], posf[:, :], m_, ALU.add))
            link(dve.tensor_scalar(m_, posf[:, :], 1.0 / P, -(P - 1) / (2.0 * P), ALU.mult, ALU.add))
            link(dve.tensor_scalar(m_, m_, MAGIC, -MAGIC, ALU.add, ALU.add))
            link(dve.scalar_tensor_tensor(sc_, m_, -float(P), posf[:, :], ALU.mult, ALU.add))
            link(dve.scalar_tensor_tensor(posi[:, :], sc_, float(SW), m_, ALU.mult, ALU.add))
            dve.wait_ge(s["blk"], 2)
            for g in range(2):
                w = NS // 2
                for a_, f in ((0, R), (1, GW)):
                    link(dve.tensor_scalar(offs[0:1, a_, g * w:(g + 1) * w], bank[2 + g][0:1, 0:w], float(f), None,
                                           ALU.mult))
            link(dve.memset(ohb0, 0.0))
            dve.wait_ge(s["wcol"], 16)
            dve.sem_inc(s["ready"], 1)

            def logit_turn(i, first):
                for c in range(C):
                    t0 = i * TURN + B * c
                    if not first:
                        dve.wait_ge(s["cntd"], C * i + (c + 1 - C))
                    dve.tensor_tensor(ohb[c], iota[:, 0:2 * NB].rearrange("p (o k) -> p o k", o=1).to_broadcast([P, B, 2 * NB]),
                                      cb[:, bass.ds(NT + t0, B)].rearrange("p (b o) -> p b o", o=1).to_broadcast([P, B, 2 * NB]),
                                      ALU.is_equal).then_inc(s["ohb"], 1)
                    for j in range(B // 2):
                        m = (B // 2) * c + j
                        pr = i * (TURN // 2) + m
                        dve.wait_ge(s["bcd"], pr + 1)
                        if not (first and m < 2):
                            dve.wait_ge(s["vald"], pr - 1)
                        dve.tensor_scalar(oht[m % 2][0:R, :], bank[m % 2][0:R, :], iota_p[0:R, :], None,
                                          ALU.is_equal).then_inc(s["ohtd"], 1)
                        dve.wait_ge(s["vcpd"], pr + 1)
                        if j == 2 and not (first and c == 0):
                            pass
                        dve.scalar_tensor_tensor(msk[m % 2][0:3 * NB, :], bank[2 + m % 2][0:3 * NB, :],
                                                 iota_pb[0:3 * NB, :], vcp[m % 2][0:3 * NB, :],
                                                 ALU.is_equal, ALU.mult).then_inc(s["mskd"], 1)
                    dve.wait_ge(s["sumd"], c16(i, c))
                    if not first:
                        dve.wait_ge(s_sc[c], i * (16 * B))
                    ps = bank[6][:, B * c:B * (c + 1)]
                    dve.tensor_scalar(lk, ps, SLOPE, None, ALU.mult).then_inc(s["med"], 1)
                    dve.wait_ge(s["med"], (C * i + c) * 2 + 1)
                    dve.tensor_tensor(lk, ps, lk, ALU.max).then_inc(s["med"], 1)
                    dve.wait_ge(s["med"], (C * i + c) * 2 + 2)
                    dve.tensor_tensor(recr[:, B * c:B * (c + 1), 2], lk, wcol[:, bass.ds(t0, B)],
                                      ALU.mult).then_inc(s["logd"], 1)
            turns(dve, 2 * HT, logit_turn)

            dve.wait_ge(s["counted"], 1)
            link(dve.tensor_copy(small[0:R, 64:64 + 2 * NB], bank[7][0:R, 0:2 * NB]))
            dve.sem_inc(s["cntc0"], 1)
            dve.wait_ge(s["cntc1"], 1)
            dve.wait_ge(s["logd"], 2 * HT * C)
            link(dve.tensor_copy(mcnt, bank[6][0:2 * NB, 128:128 + R]))
            dve.sem_inc(s["cnp"], 1)
            dve.wait_ge(s["spr"], 32)
            link(dve.tensor_tensor(rel[:, :], cf[:, NT:2 * NT], rel[:, :], ALU.subtract))
            link(dve.tensor_copy(base[:, :], brow[0:1, 0:NT]))
            link(dve.tensor_reduce(small[0:1, 40:41], brow[0:1, NT:2 * NT], AX.X, ALU.max))
            link(dve.tensor_scalar(small[0:1, 40:41], small[0:1, 40:41], 1.0 / WIN, -(WIN - 1) / (2.0 * WIN),
                                   ALU.mult, ALU.add))
            link(dve.tensor_scalar(small[0:1, 40:41], small[0:1, 40:41], MAGIC, 1.0 - MAGIC, ALU.add, ALU.add))
            link(dve.tensor_copy(npass[:, :], small[0:1, 40:41]))
            dve.wait_ge(s["rfill"], 2 * HT * C)
            for c in range(C):
                dve.wait_ge(s_sc[c], 16 * B * 2 * HT)
            dve.wait_ge(s["cns"], 16)
            signal("onesd", dve.memset(ring[:, :, D:GW], 1.0))
            link(dve.memset(maxes[:, :], 3e38))
            link(dve.memset(zacc[:, :], 0.0))
            dve.wait_ge(s["srtl"], 16)
            link(dve.tensor_copy(sdst[:, :], srt[:, :, 1]))
            signal("sfar", dve.tensor_scalar(far[:, :], srt[:, :, 0], -FAR, None, ALU.mult))

            def max_turn(T, first):
                for k in range(TURN):
                    o = dve.value_load(offs[0:1, 0, bass.ds(T * TURN + k, 1)], min_val=0, max_val=NB * R)
                    dve.wait_ge(s["sq"], T * TURN + (k + 1))
                    if not (first and k == 0):
                        dve.wait_ge(s["mx"], T * TURN + k)
                    mx = maxes[:, bass.ds(o, R)]
                    dve.scalar_tensor_tensor(mx, sq[:, k, :],
                                             srt[:, bass.ds(T * TURN + k, 1), 2:3].rearrange("p a b -> p (a b)"),
                                             mx, ALU.subtract, ALU.min).then_inc(s["mx"], 1)
            turns(dve, ST, max_turn)
            dve.wait_ge(s["mx"], NS)
            for b in range(NB):
                dve.wait_ge(s["mtr"], b + 1)
                dve.tensor_reduce(mcol[:, b:b + 1], bank[b % 4][0:R, 0:P], AX.X, ALU.min).then_inc(s["mred"], 1)
            dve.wait_ge(s["mred"], NB)
            dve.tensor_scalar(mcol[:, :], mcol[:, :], NOMAX, None, ALU.min).then_inc(s["mred"], 1)
            link(dve.memset(maxes[:, NB * R:(NB + 1) * R], 0.0))
            dve.wait_ge(s["mbcd"], (NB + 3) // 4)

            def guard(T, c, first):
                if not first:
                    dve.wait_ge(s["wd"], T * TURN + (B * (c + 1) - TURN))
                for k in range(B * c, B * (c + 1)):
                    o = dve.value_load(offs[0:1, 0, bass.ds(T * TURN + k, 1)], min_val=0, max_val=NB * R)
                    dve.scalar_tensor_tensor(junk[:, k % B, :], iota[:, 0:R],
                                             srt[:, bass.ds(T * TURN + k, 1), 0:1].rearrange("p a b -> p (a b)"),
                                             maxes[:, bass.ds(o, R)], ALU.is_equal, ALU.mult,
                                             accum_out=me[:, k:k + 1]).then_inc(s["gpre"], 1)
                dve.wait_ge(s["gpre"], T * TURN + B * (c + 1))
                dve.tensor_tensor(lm[:, B * c:B * (c + 1)], me[:, B * c:B * (c + 1)],
                                  srt[:, bass.ds(T * TURN + B * c, B), 2], ALU.add).then_inc(s["lmd"], 1)

            def add_sums(T, c, first):
                for k in range(B * c, B * (c + 1)):
                    o = dve.value_load(offs[0:1, 1, bass.ds(T * TURN + k, 1)], min_val=0, max_val=NB * GW)
                    dve.wait_ge(s["pvd"], T * TURN + (k + 1))
                    if not (first and k == 0):
                        dve.wait_ge(s["fld"], T * TURN + k)
                    z = zacc[0:R, bass.ds(o, GW)]
                    dve.tensor_tensor(z, z, bank[k % 8][0:R, 0:GW], ALU.add).then_inc(s["fld"], 1)

            def soft_turn(T, first):
                for c in range(C):
                    guard(T, c, first)
                    if c:
                        add_sums(T, c - 1, first)
                    elif not first:
                        add_sums(T - 1, C - 1, False)
            turns(dve, ST, soft_turn)
            add_sums(ST - 1, C - 1, False)
            dve.wait_ge(s["fld"], NS)
            dve.sem_inc(s["zdone"], 1)

            z3 = zacc[0:R, 0:NB * GW].rearrange("p (b w) -> p b w", w=GW)
            dsum, has, none, dinv = (den[0:R, NB * q_:NB * (q_ + 1)] for q_ in range(4))
            link(dve.memset(padrow[:, :], -1e30))
            link(dve.memset(accT[0], 0.0))
            link(dve.memset(accT[1], 0.0))
            link(dve.tensor_scalar(none, z3[:, :, D], 0.0, None, ALU.is_equal))
            link(dve.tensor_tensor(dsum, z3[:, :, D], none, ALU.add))
            link(dve.reciprocal(dinv, dsum))
            dve.wait_ge(s["wl1"], 16 * 18)
            dve.wait_ge(s["u2d"], 1)
            link(dve.tensor_tensor(crow[0:1, :], crow[0:1, :], bank[4][0:1, 0:2 * D], ALU.add))
            link(dve.tensor_copy(u2[0:2, 0:D], bank[5][0:2, 0:D]))
            dve.sem_inc(s["u2d"], 1)
            Y1, Y2, Y3, Y4 = (v[0:R, :] for v in (y1, y2, y3, y4))
            Y1b, Y2b, Y3b = (v.rearrange("p (b d) -> p b d", d=D) for v in (Y1, Y2, Y3))
            m1, m2, m3 = mv2[0:R, 0:CH], mv2[0:R, CH:2 * CH], mv2[0:R, 2 * CH:3 * CH]

            def row(q_):
                return gbc[0:R, D * q_:D * (q_ + 1)].rearrange("p (o d) -> p o d", o=1).to_broadcast([R, CH, D])

            for k in range(NB // CH):
                bl = slice(CH * k, CH * (k + 1))
                link(dve.tensor_tensor(Y1b, z3[:, bl, 0:D], bc(dinv[:, bl], D), ALU.mult))
                link(dve.tensor_tensor(Y2b, hs[0:R, bl, :], bc(none[:, bl], D), ALU.mult))
                link(dve.tensor_tensor(Y1, Y1, Y2, ALU.add))
                link(dve.tensor_tensor(Y1b, Y1b, h0[:, bl, :], ALU.add))
                link(dve.tensor_reduce(m3, Y1b, AX.X, ALU.add))
                link(dve.tensor_scalar(m3, m3, 1.0 / D, None, ALU.mult))
                signal("h1b", dve.tensor_tensor(Y1b, Y1b, bc(m3, D), ALU.subtract))
                dve.wait_ge(s["ze"], 5 * k + 1)
                link(dve.tensor_reduce(m1, Y2b, AX.X, ALU.add))
                signal("h1b", dve.tensor_scalar(m1, m1, 1.0 / D, EPS, ALU.mult, ALU.add))
                dve.wait_ge(s["ze"], 5 * k + 2)
                link(dve.reciprocal(m3, m2))
                link(dve.tensor_tensor(Y1b, Y1b, bc(m3, D), ALU.mult))
                link(dve.tensor_tensor(Y1b, Y1b, row(0), ALU.mult))
                link(dve.tensor_tensor(Y1b, Y1b, row(1), ALU.add))
                signal("h1b", dve.tensor_scalar(Y2, Y1, 0.0, None, ALU.min))
                dve.wait_ge(s["ze"], 5 * k + 3)
                link(dve.tensor_scalar(Y2, Y2, -1.0, None, ALU.add))
                link(dve.scalar_tensor_tensor(Y1, Y1, 0.0, Y2, ALU.max, ALU.add))
                dve.wait_ge(s["x1l"], 16 * (k + 1))
                link(dve.tensor_tensor(h0[:, bl, :], Y1b, Y4.rearrange("p (b d) -> p b d", d=D), ALU.add))
                dve.sem_inc(s["h1a"], 1)
                link(dve.tensor_reduce(m3, h0[:, bl, :], AX.X, ALU.add))
                link(dve.tensor_scalar(m3, m3, 1.0 / D, None, ALU.mult))
                signal("h1c", dve.tensor_tensor(Y1b, h0[:, bl, :], bc(m3, D), ALU.subtract))
                dve.wait_ge(s["ze"], 5 * k + 4)
                link(dve.tensor_reduce(m1, Y3b, AX.X, ALU.add))
                signal("h1c", dve.tensor_scalar(m1, m1, 1.0 / D, EPS, ALU.mult, ALU.add))
                dve.wait_ge(s["ze"], 5 * k + 5)
                link(dve.reciprocal(m3, m2))
                link(dve.tensor_tensor(Y1b, Y1b, bc(m3, D), ALU.mult))
                if k:
                    dve.wait_ge(s["hw1"], CH * k)
                signal("pass", dve.tensor_scalar(h1n[0:R, :], Y1, 0.0, None, ALU.max))

            passes = dve.value_load(npass[0:1, 0:1], min_val=1, max_val=NB)
            with dve.Fori(0, passes) as kp:
                for h in range(2):
                    def flush(nb, i, c, h=h):
                        for k in range(B):
                            t = i * TURN + (h * HT * TURN + B * c + k)
                            o = dve.value_load(base[0:1, bass.ds(t, 1)], min_val=0, max_val=N)
                            if k % 4 == 0:
                                dve.wait_ge(s["pso"], nb * B + (k + 4))
                            dve.wait_ge(s["fld"], nb * B + (NS + k))
                            w = accT[h][:, bass.ds(o, WIN)]
                            dve.tensor_tensor(w, w, bank[6 + k // 4][:, P * (k % 4):P * (k % 4 + 1)],
                                              ALU.add).then_inc(s["fld"], 1)

                    def msg_turn(i, first, h=h):
                        tt = kp * (2 * HT) + (h * HT + i)
                        for c in range(C):
                            nb = tt * C + c
                            t0 = i * TURN + (h * HT * TURN + B * c)
                            if not first:
                                dve.wait_ge(s["pso"], nb * B + (B - C * B))
                            dve.tensor_tensor(oh1[:, c, :].rearrange("p (k w) -> p k w", k=B),
                                              iota[:, 0:WIN].rearrange("p (o w) -> p o w", o=1).to_broadcast([P, B, WIN]),
                                              rel[:, bass.ds(t0, B)].rearrange("p (k o) -> p k o", o=1).to_broadcast([P, B, WIN]),
                                              ALU.is_equal).then_inc(s["ohd"], 1)
                            dve.wait_ge(s["ea"], nb + 1)
                            dve.wait_ge(s_g1[c], tt * (16 * B) + 16 * B)
                            for g in range(2):
                                w = slice(512 * g, 512 * (g + 1))
                                ins = dve.tensor_tensor(pre[:, c, w], bank[2 * c + g][:, :], g1[:, c, w], ALU.add)
                                ins.then_inc(s["rels"], 1)
                            dve.wait_ge(s["rels"], nb * 2 + 2)
                            dve.sem_inc(s["add"], 1)
                            if c:
                                flush(nb - 1, i, c - 1)
                            elif not first:
                                flush(nb - 1, i - 1, C - 1)
                    turns(dve, HT, msg_turn)
                    flush(kp * (2 * HT * C) + ((h + 1) * HT * C - 1), HT - 1, C - 1)
                    dve.wait_ge(s["fld"], ((kp * 2 + (h + 1)) * HT) * TURN + NS)
                dve.tensor_scalar(rel[:, :], rel[:, :], -float(WIN), None, ALU.add).then_inc(s["nextw"], 1)
                dve.tensor_scalar(base[:, :], base[:, :], float(WIN), float(N), ALU.add, ALU.min).then_inc(s["nextw"], 1)
                dve.wait_ge(s["nextw"], kp * 2 + 2)

            link(dve.tensor_scalar(small[:, 3:4], small[:, 3:4], 1.0, None, ALU.add))
            for b in range(NB):
                dve.wait_ge(s["hf2"], b + 1)
                if b >= 4:
                    dve.wait_ge(s["hf4"], b - 3)
                dve.scalar_tensor_tensor(hT2[:, P * (b % 4):P * (b % 4) + R], h1T[:, R * b:R * (b + 1)], small[:, 3:4],
                                         bank[b % 2][:, 0:R], ALU.mult, ALU.add).then_inc(s["hf3"], 1)
                dve.wait_ge(s["hf4"], b + 1)
                dve.scalar_tensor_tensor(h0[:, b, :], bank[2 + b % 2][0:R, 0:D], 0.0, h0[:, b, :],
                                         ALU.max, ALU.add).then_inc(s["outd"], 1)


def _lay(inputs):
    import numpy as np

    def slots(v, pad):
        halves = [v[:EH[0]], v[EH[0]:]]
        room = HT * TURN * P
        if pad is None:
            return np.concatenate([np.pad(x, (0, room - len(x)), mode="edge") for x in halves])
        return np.concatenate([np.pad(x, (0, room - len(x)), constant_values=pad) for x in halves])

    g = {k: np.asarray(v) for k, v in inputs.items()}
    src, dst = slots(g["src"], N), slots(g["dst"], None)
    w = slots(g["edge_weight"], 0)
    nat = np.concatenate([src.reshape(Q, B * P), dst.reshape(Q, B * P)], 1)
    col = np.concatenate([src.reshape(NT, P).T, dst.reshape(NT, P).T], 1)
    ea = g["edge_attr_16"].T
    eat = np.zeros((EA, NT * P), ea.dtype)
    eat[:, :EH[0]] = ea[:, :EH[0]]
    eat[:, HT * TURN * P:HT * TURN * P + EH[1]] = ea[:, EH[0]:]
    cst = np.zeros((P, C_W), np.float32)
    cst[:, C_ID:C_ID + P] = np.eye(P)
    cst[:, C_TRI:C_TRI + P] = np.triu(np.ones((P, P)), 1)
    cst[:, C_IOTA:C_IOTA + NS] = np.arange(NS)
    cst[:, C_P] = np.arange(P)
    cst[:, C_PB] = np.arange(P) % NB
    cst[:NB + 1, C_INC:] = np.triu(np.ones((NB + 1, NB + 1)))
    return {
        "cst": cst, "nat": nat, "col": col, "w": w.reshape(NT, P).T, "eaT": eat, "x": g["x"],
        "W": g["L0_gnn_W"], "WT": g["L0_gnn_W"].T, "as": g["L0_gnn_a_src"], "ad": g["L0_gnn_a_dst"],
        "gamma": g["L0_gnn_ln_gamma"], "beta": g["L0_gnn_ln_beta"], "req": g["L1_gnn_req_emb"],
        "W1f": g["L1_gnn_W1f"], "W1b": g["L1_gnn_W1b"], "b1f": g["L1_gnn_b1f"], "b1b": g["L1_gnn_b1b"],
        "W2f": g["L1_gnn_W2f"], "W2b": g["L1_gnn_W2b"], "b2f": g["L1_gnn_b2f"], "b2b": g["L1_gnn_b2b"],
        "Wu": g["L1_gnn_Wu"], "bu": g["L1_gnn_bu"], "eps": g["L1_gnn_eps"],
    }


def kernel(**inputs):
    import numpy as _np
    import concourse.bacc as _bacc
    from concourse import mybir as _mybir
    from concourse.bass_utils import run_bass_kernel_spmd as _run

    nc = _bacc.Bacc("TRN2", target_bir_lowering=False, num_devices=1)
    arrays, args = {}, {}
    for name, v in _lay(inputs).items():
        v = _np.ascontiguousarray(v)
        arrays[f"in_{name}"] = v
        args[name] = nc.dram_tensor(f"in_{name}", v.shape, _mybir.dt.from_np(v.dtype), kind="ExternalInput").ap()
    out = nc.dram_tensor("out_x", (N, D), F32, kind="ExternalOutput").ap()
    scratch = {
        "rec": nc.dram_tensor("scr_rec", (P * SW, 3), F32).ap(),
        "H": nc.dram_tensor("scr_H", (N, D), F32).ap(),
        "PP": nc.dram_tensor("scr_PP", (2 * TN, D), F32).ap(),
        "base": nc.dram_tensor("scr_base", (2, NT), F32).ap(),
        "cnt": nc.dram_tensor("scr_cnt", (2 * N,), F32).ap(),
    }
    build(nc, args, out, scratch)
    r = _run(nc, [arrays], core_ids=[0])
    return r.results[0]["out_x"]
```

```python
from contextlib import ExitStack

import concourse.bass as bass
from concourse import mybir

ALU = mybir.AluOpType
ACT = mybir.ActivationFunctionType
AX = mybir.AxisListType
F32 = mybir.dt.float32
BF16 = mybir.dt.bfloat16
I32 = mybir.dt.int32

P = 128
D = 128
N = 3125
R = 125
NB = N // R
E = 103125
EH = (E // 2, E - E // 2)
B = 8
C = 3
TURN = B * C
HT = 17
NT = 2 * HT * TURN
Q = NT // B
G0 = 2
ST = 36
NS = ST * TURN
RT = 9
RO = ST // RT
RING = RT * TURN
SW = NS + TURN
GW = D + 1
EA = 16
REQ = 16
TN = N + 1
GT = 4
WIN = 64
NPASS = -(-N // WIN)
AW = N + WIN
EPS = 1e-5
SLOPE = 0.2
MAGIC = 12582912.0
NG = NS // G0
FAR = 2.0 ** 110
NOMAX = 1e32
CH = 5
HB = 3
HW = D + 2
HALF = NT // 2

assert 2 * HT * TURN * P >= E and HT * TURN * P >= max(EH)
assert NG * G0 * P >= E + NB * (G0 * P - 1) and RO * RT == ST and NT % B == 0

C_ID, C_TRI, C_IOTA = 0, P, 2 * P
C_P = C_IOTA + NS // G0
C_PB = C_P + 1
C_INC = C_PB + 1
C_W = C_INC + NB + 1


def turns(eng, count, body):
    body(0, True)
    with eng.Fori(1, count) as i:
        body(i, False)


def build(nc, a, out, scr):
    with ExitStack() as ctx:
        def sb(name, shape, dt):
            return ctx.enter_context(nc.sbuf_tensor(name, shape, dt))

        def sem(name):
            return ctx.enter_context(nc.semaphore(name))

        bank = [ctx.enter_context(nc.psum_tensor(f"bank{i}", [P, 512], F32)) for i in range(8)]

        cst = sb("cst", [P, C_W], F32)
        identb = sb("identb", [P, 2, R], BF16)
        farb = sb("farb", [P, P], BF16)
        selb = sb("selb", [P, P], BF16)
        onesb = sb("onesb", [P, 1], BF16)
        onesf = sb("onesf", [P, P], F32)
        h0 = sb("h0", [R, NB, D], F32)
        hs = sb("hs", [P, NB, HW], F32)
        zacc = sb("zacc", [P, (NB + 1) * GW], F32)
        srt = sb("srt", [P, NS, 3], F32)
        sdst = sb("sdst", [P, NS], I32)
        srcg = sb("srcg", [P, NT], I32)
        rel = sb("rel", [P, NT], F32)
        offs = sb("offs", [1, NG], I32)
        newb = sb("newb", [R, NG + 1], F32)
        low = sb("low", [R, 3, NG], F32)
        guard = sb("guard", [R, 3, NG], BF16)
        base = sb("base", [1, NT // GT], I32)
        npass = sb("npass", [1, 1], I32)
        idxr = sb("idxr", [P, RING], I32)
        wt = sb("wt", [P, 7 * D], F32)
        small = sb("small", [P, 256], F32)
        arena = sb("arena", [P, RING * GW], F32)
        AR = RING * GW
        ring = arena[:, :].rearrange("p (s w) -> p s w", w=GW)

        ident = cst[:, C_ID:C_ID + P]
        tri = cst[:, C_TRI:C_TRI + P]
        iota = cst[:, C_IOTA:C_IOTA + NG]
        iota_p = cst[:, C_P:C_P + 1]
        iota_pb = cst[:, C_PB:C_PB + 1]
        inc = cst[:, C_INC:C_INC + NB + 1]

        at = [0]

        def taker():
            at[0] = 0

            def take(n):
                n += n % 2
                v = arena[:, at[0]:at[0] + n]
                at[0] += n
                assert at[0] <= AR, at[0]
                return v
            return take

        sq_ = sb("sq_", [P, C * B * P], F32)
        pen = sq_[:, 0:TURN * R].rearrange("p (c k r) -> p c k r", c=C, r=R)
        sqb = sb("sqb", [P, TURN, R], BF16)
        gring = sb("gring", [R, C, 3, B // G0], BF16)
        take = taker()
        nat_i = sq_[:, 0:2 * B * P].bitcast(I32)
        nat_r = take(B * P).bitcast(BF16)
        nat_b = take(B * P).bitcast(BF16)
        col_i = take(2 * NT).bitcast(I32)
        rec2 = take(2 * NT).rearrange("p (t a) -> p t a", a=2)
        cb = take(2 * NT)
        cr = take(2 * NT)
        cf = take(2 * NT)
        ct = srt[:, :, :].rearrange("p s a -> p (s a)")[:, 0:2 * NT]
        wcol = take(NT)
        posi = take(NT).bitcast(I32)
        h0T = [take(HB * R)[:, 0:HB * R] for _ in range(2)]
        tb = take(3 * NB).bitcast(BF16).rearrange("p (a k) -> p a k", a=2)
        tf = take(2 * NB)
        brow = newb[0:1, 0:2 * NT // GT]
        mcnt = take(R)[0:2 * NB, 0:R]
        starts = take(NG)
        zb = take(NB).bitcast(BF16)[:, 0:2 * NB]
        fill_ = zacc[:, 0:SW * 3]
        fill = fill_.rearrange("p (s a) -> p s a", a=3)
        nat_f = fill_[:, 0:2 * B * P]
        cnt = take(NB + 1)
        laneoff = take(NB + 1)
        bst = take(6 * NB).rearrange("p (b k) -> p b k", k=6)
        bmv = take(2 * NB).rearrange("p (b k) -> p b k", k=2)
        brs = take(NB + 1)
        bnm = take(NB + 1)
        scans = [take(NT) for _ in range(2)]
        prods = [take(NT) for _ in range(2)]
        winb = sdst[:, 0:NT // GT].bitcast(F32)
        nat_t = srt[:, :, :].rearrange("p s a -> p (s a)")[:, 0:2 * B * P]
        msqs = prods
        sorting = at[0]
        masks = take((NB + 1) * NT // 2).bitcast(BF16).rearrange("p (k t) -> p k t", t=NT)
        at[0] = sorting
        recr = take(TURN * 3).rearrange("p (s a) -> p s a", a=3)
        posr = take(TURN).bitcast(I32)
        lk = take(B)
        oht = [take(256).bitcast(BF16) for _ in range(2)]
        vcp = [take(256).bitcast(BF16) for _ in range(2)]
        msk = [take(256).bitcast(BF16) for _ in range(2)]
        sqr = take(B * R).rearrange("p (k r) -> p k r", r=R)
        ohr = [take(B * R // 2).bitcast(BF16).rearrange("p (k r) -> p k r", r=R) for _ in range(C)]
        ohb = [take(B * 2 * NB // 2).bitcast(BF16).rearrange("p (k r) -> p k r", r=2 * NB) for _ in range(C)]
        take = taker()
        accT = [take(AW) for _ in range(2)]
        g1 = take(TURN * D).rearrange("p (c n) -> p c n", c=C)
        pre = take(TURN * D).rearrange("p (c n) -> p c n", c=C)
        eat = take(TURN * P).rearrange("p (c n) -> p c n", c=C)
        at[0] -= 3 * TURN * D
        big = take(3 * NB * D)
        ya, yb, yc = (big[0:R, NB * D * q_:NB * D * (q_ + 1)] for q_ in range(3))
        padrow = take(D)
        den = take(4 * NB)
        crow = take(4 * D)
        u3 = take(D)
        pout = [take(4 * D) for _ in range(2)]
        gbc = take(2 * D)
        cntT = take(N)[0:3, 0:N]
        st2 = take(6 * NB).rearrange("p (b k) -> p b k", k=6)
        mv2 = take(2 * NB).rearrange("p (b k) -> p b k", k=2)
        rs2 = take(NB + 1)
        nm2 = take(NB + 1)
        w2u = take(3 * D)
        xagain = take(NB * D)[0:R, :]
        oh1 = sq_[:, 0:TURN * WIN].rearrange("p (c n) -> p c n", c=C)
        h1T = hs[:, :, :].rearrange("p a b -> p (a b)")

        names = (
            "cst nati coli wcol x wl fill pat asteps dsteps "
            "stat root norm tpd tcp hp hcp hst wa wac "
            "blocks sqm mask lanes totals tiles ends first scan prod rank slots ready "
            "rowb ohtd blkb vald vcpd mskd sumd lks logd ohr ohb cntd r1 rr rfill turn spturn "
            "counted cntc cntp cntw win winw winr "
            "ones srtl sfar idx sq pend mtr lowd guards grd xd wd pvd fld zdone "
            "wl1 xa none hn root1 norm1 mins exps root2 norm2 tp1 tc1 pp pc cm cmd u3d onesr "
            "ea addh msg ohd pso nextw pre q1 q2 qc hf out0 outd outs").split()
        s = {n: sem("s_" + n) for n in names}
        s_sc = [sem(f"s_sc{c}") for c in range(C)]
        s_g0 = [sem(f"s_g0_{c}") for c in range(C)]
        s_g1 = [sem(f"s_g1_{c}") for c in range(C)]
        s_pst = [sem(f"s_pst{k}") for k in range(2)]
        s_ld = [sem(f"s_ld{c}") for c in range(C)]
        block = ctx.enter_context(nc.Block())

        def c16(i, c):
            return C * i + c + 1

        @block.sync
        def _(sp):
            sp.dma_start(col_i[:, :], a["col"]).then_inc(s["coli"], 16)
            sp.dma_start(cst[:, :], a["cst"]).then_inc(s["cst"], 16)
            xv = a["x"].rearrange("(b r) d -> r b d", r=R)
            sp.dma_start(h0[:, :, :], xv).then_inc(s["x"], 16)
            sp.dma_start(nat_i[0:Q, :], a["nat"]).then_inc(s["nati"], 16)
            sp.dma_start(wt[:, 0:D], a["W"]).then_inc(s["wl"], 16)
            sp.dma_start(wt[:, D:2 * D], a["WT"]).then_inc(s["wl"], 16)
            sp.dma_start(wt[:, 2 * D:2 * D + 1], a["as"].rearrange("(p o) -> p o", o=1)).then_inc(s["wl"], 16)
            sp.dma_start(wt[:, 2 * D + 1:2 * D + 2], a["ad"].rearrange("(p o) -> p o", o=1)).then_inc(s["wl"], 16)
            sp.dma_start(wcol[:, :], a["w"]).then_inc(s["wcol"], 16)
            sp.wait_ge(s["pat"], 1)
            sp.dma_start(scr["rec"].rearrange("(p s) a -> p (s a)", p=P),
                         fill.rearrange("p s a -> p (s a)")).then_inc(s["fill"], 16)
            sp.wait_ge(s["win"], 1)
            sp.dma_start(scr["base"].rearrange("k (q c) -> q k c", q=Q),
                         small[0:Q, 0:4].rearrange("p (k c) -> p k c", k=2)).then_inc(s["winw"], 16)
            sp.wait_ge(s["winw"], 16)
            sp.dma_start(brow[0:1, :], scr["base"].rearrange("(o k) t -> o (k t)", o=1)).then_inc(s["winr"], 16)
            sp.dma_start(winb, scr["base"][0:1, :].to_broadcast([P, NT // GT])).then_inc(s["winr"], 16)
            sp.wait_ge(s["hcp"], (NB + HB - 1) // HB)
            sp.dma_start(scr["H"].rearrange("(b r) d -> r b d", r=R), hs[0:R, :, 0:D]).then_inc(s["hst"], 16)

            sp.wait_ge(s["cntp"], 1)
            sp.dma_start(scr["cnt"].rearrange("(k r) -> k r", r=R), mcnt).then_inc(s["cntw"], 16)
            for c in range(C):
                sp.wait_ge(s_sc[c], 16 * B * 2 * HT)
            sp.dma_start(srt[:, :, :].rearrange("p s a -> p (s a)"),
                         scr["rec"].rearrange("(p s) a -> p s a", p=P)[:, 0:NS, :].rearrange(
                             "p s a -> p (s a)")).then_inc(s["srtl"], 16)

            sp.wait_ge(s["sfar"], 1)

            def idx_round(o, first):
                for u in range(RT):
                    if not first:
                        for c in range(C):
                            sp.wait_ge(s_g0[c], o * (16 * B * RT) + 16 * B * (u + 1 - RT))
                            sp.sem_inc(s["spturn"], 1)
                    sp.dma_start(idxr[:, TURN * u:TURN * (u + 1)],
                                 sdst[:, bass.ds(o * RING + TURN * u, TURN)]).then_inc(s["idx"], 16)
                    sp.wait_ge(s["idx"], o * (16 * RT) + 16 * (u + 1))
                    sp.sem_inc(s["spturn"], 1)
            turns(sp, RO, idx_round)

            sp.wait_ge(s["zdone"], 1)

            def row(name):
                return a[name].rearrange("(o p) -> o p", o=1)

            def col(name):
                return a[name].rearrange("(p o) -> p o", o=1)

            sp.dma_start(xagain.rearrange("p (b d) -> p b d", d=D), xv).then_inc(s["xa"], 16)
            for dst, src in (
                (gbc[:, 0:D], row("gamma").to_broadcast([P, D])), (gbc[:, D:2 * D], row("beta").to_broadcast([P, D])),
                (wt[:, 0:D], a["W1f"][0:D, :]), (wt[:, D:2 * D], a["W1b"][0:D, :]),
                (wt[:, 2 * D:3 * D], a["W2fT"]), (wt[:, 3 * D:4 * D], a["W2bT"]), (wt[:, 4 * D:5 * D], a["Wu"]),
                (wt[0:EA, 5 * D:6 * D], a["W1f"][D:D + EA, :]), (wt[0:EA, 6 * D:7 * D], a["W1b"][D:D + EA, :]),
                (pout[0][0:REQ, 0:D], a["W1f"][D + EA:D + EA + REQ, :]),
                (pout[0][0:REQ, D:2 * D], a["W1b"][D + EA:D + EA + REQ, :]),
                (small[0:REQ, 0:1], a["req"].rearrange("o p -> p o")),
                (pout[1][0:1, 0:D], row("b1f")), (pout[1][0:1, D:2 * D], row("b1b")),
                (small[:, 1:2], col("b2f")), (small[:, 2:3], col("b2b")),
                (small[:, 3:4], row("eps").to_broadcast([P, 1])), (u3[2:3, :], row("bu")),
            ):
                sp.dma_start(dst, src).then_inc(s["wl1"], 16)
            sp.wait_ge(s["onesr"], 1)
            sp.wait_ge(s["cntw"], 16)
            sp.dma_start(cntT[0:2, :], scr["cnt"].rearrange("(h n) -> h n", h=2)).then_inc(s["wl1"], 16)
            pv = scr["PP"].rearrange("(h n) d -> n h d", h=2)
            sp.wait_ge(s["none"], 1)
            sp.dma_start(pv[N:N + 1, :, :], padrow[0:2, :]).then_inc(s_pst[0], 16)
            for g in range((NB + 1) // 2):
                sp.wait_ge(s["pc"], g + 1)
                for b in range(2 * g, min(2 * g + 2, NB)):
                    o = 2 * D * (b % 2)
                    sp.dma_start(pv[R * b:R * (b + 1), :, :],
                                 pout[g % 2][0:R, o:o + 2 * D].rearrange("p (h d) -> p h d", h=2)
                                 ).then_inc(s_pst[g % 2], 16)

            passes = sp.value_load(npass[0:1, 0:1], min_val=1, max_val=NPASS)
            with sp.Fori(0, passes) as kp:
                for h in range(2):
                    def load_turn(i, first, h=h):
                        for c in range(C):
                            tt = kp * (2 * HT) + (h * HT + i)
                            t0 = i * TURN + (h * HALF + B * c)
                            if not first:
                                sp.wait_ge(s_g1[c], tt * (16 * B))
                                sp.sem_inc(s["spturn"], 1)
                                sp.wait_ge(s["ea"], tt * C + (c + 1 - C))
                                sp.sem_inc(s["spturn"], 1)
                            sp.dma_start(eat[0:EA, c, :], a["eaT"][:, bass.ds(t0 * P, B * P)]).then_inc(s_ld[c], 16)
                            sp.dma_start(idxr[:, B * c:B * (c + 1)], srcg[:, bass.ds(t0, B)]).then_inc(s_ld[c], 16)
                    turns(sp, HT, load_turn)
                    sp.wait_ge(s["fld"], ((kp * 2 + (h + 1)) * HT) * (TURN // GT) + NG)
                    sp.sem_inc(s["spturn"], 1)
            ov = out.rearrange("(b r) d -> r b d", r=R)
            for g in range((NB + 3) // 4):
                b0, b1 = 4 * g, min(4 * g + 4, NB)
                sp.wait_ge(s["outd"], g + 1)
                sp.dma_start(ov[:, b0:b1, :], h0[:, b0:b1, :]).then_inc(s["outs"], 16)
            sp.wait_ge(s["outs"], 16 * ((NB + 3) // 4))

        @block.gpsimd
        def _(pool):
            for k in range(NB + 1):
                pool.wait_ge(s["scan"], k + 1)
                if k >= 2:
                    pool.wait_ge(s["rank"], k - 1)
                pool.tensor_tensor(prods[k % 2], masks[:, k, :], scans[k % 2], ALU.mult).then_inc(s["prod"], 1)
            pool.wait_ge(s["fill"], 16)

            def scatter_turn(i, first):
                for c in range(C):
                    if not first:
                        pool.wait_ge(s_sc[c], i * (16 * B))
                    pool.wait_ge(s["rfill"], c16(i, c))
                    pool.wait_ge(s["logd"], c16(i, c))
                    pool.sem_inc(s["turn"], 1)
                    for k in range(B * c, B * (c + 1)):
                        pool.indirect_dma_start(scr["rec"], bass.IndirectOffsetOnAxis(ap=posr[:, k:k + 1], axis=0),
                                                recr[:, k, :], None).then_inc(s_sc[c], 16)
            turns(pool, 2 * HT, scatter_turn)

            pool.wait_ge(s["hst"], 16)
            pool.wait_ge(s["ones"], 1)

            def gather_round(o, first):
                for u in range(RT):
                    pool.wait_ge(s["idx"], o * (16 * RT) + 16 * (u + 1))
                    for c in range(C):
                        if not (first and u == 0):
                            pool.wait_ge(s_g0[c], o * (16 * B * RT) + 16 * B * u)
                        if not first:
                            pool.wait_ge(s["pvd"], o * (RING // G0) + (TURN * u + B * (c + 1) - RING) // G0)
                        pool.sem_inc(s["turn"], 1)
                        for k in range(TURN * u + B * c, TURN * u + B * (c + 1)):
                            pool.indirect_dma_start(ring[:, k, 0:D], None, scr["H"],
                                                    bass.IndirectOffsetOnAxis(ap=idxr[:, k:k + 1], axis=0)
                                                    ).then_inc(s_g0[c], 16)
            turns(pool, RO, gather_round)

            pool.wait_ge(s["zdone"], 1)
            pool.memset(cntT, 1.0).then_inc(s["onesr"], 1)
            pool.wait_ge(s["none"], 1)
            for k in range(NB // CH):
                bl = slice(CH * k, CH * (k + 1))
                y = yb[:, CH * D * k:CH * D * (k + 1)].rearrange("p (b d) -> p b d", d=D)
                no = den[0:R, CH * k:CH * (k + 1)].rearrange("p (b o) -> p b o", o=1).to_broadcast([R, CH, D])
                pool.tensor_tensor(y, hs[0:R, bl, 0:D], no, ALU.mult).then_inc(s["hn"], 1)
                pool.wait_ge(s["hn"], 2 * k + 1)
                pool.tensor_tensor(y, y, h0[:, bl, :], ALU.add).then_inc(s["hn"], 1)

            pool.wait_ge(s_pst[0], 16 * (1 + NB // 4 * 2 + 1))
            pool.wait_ge(s_pst[1], 16 * (NB // 4 * 2))
            passes = pool.value_load(npass[0:1, 0:1], min_val=1, max_val=NPASS)
            with pool.Fori(0, passes) as kp:
                for h in range(2):
                    def msg_turn(i, first, h=h):
                        tt = kp * (2 * HT) + (h * HT + i)
                        for c in range(C):
                            pool.wait_ge(s_ld[c], tt * 32 + 32)
                            if not first:
                                pool.wait_ge(s["addh"], (tt * C + (c + 1 - C)) * 2)
                            pool.sem_inc(s["turn"], 1)
                            for k in range(B):
                                pool.indirect_dma_start(g1[:, c, k * D:(k + 1) * D], None, scr["PP"],
                                                        bass.IndirectOffsetOnAxis(
                                                            ap=idxr[:, B * c + k:B * c + k + 1], axis=0)
                                                        ).then_inc(s_g1[c], 16)
                    turns(pool, HT, msg_turn)
                    pool.wait_ge(s["fld"], ((kp * 2 + (h + 1)) * HT) * (TURN // GT) + NG)

        @block.scalar
        def _(act):
            n_step = [0]

            def link(ins):
                n_step[0] += 1
                ins.then_inc(s["asteps"], 1)
                act.wait_ge(s["asteps"], n_step[0])

            act.wait_ge(s["cst"], 16)
            for q_ in range(2):
                act.copy(identb[:, q_, :], ident[:, 0:R]).then_inc(s["asteps"], 1)
            act.copy(selb[:, :], ident).then_inc(s["asteps"], 1)
            act.activation(farb[:, :], ident, ACT.Copy, scale=FAR).then_inc(s["asteps"], 1)
            n_step[0] = 4
            act.wait_ge(s["blocks"], 1)
            for k in range(NB + 1):
                if k >= 2:
                    act.wait_ge(s["mask"], k - 1)
                act.activation(msqs[k % 2], cb[:, 0:NT], ACT.Square, scale=-1.0,
                               bias=iota[:, k:k + 1]).then_inc(s["sqm"], 1)
                act.wait_ge(s["sqm"], k + 1)
                act.activation(masks[:, k, :], msqs[k % 2], ACT.Relu, scale=-1.0, bias=onesf[:, 0:1],
                               accum_out=cnt[:, k:k + 1]).then_inc(s["mask"], 1)
            act.wait_ge(s["stat"], 1)
            act.activation(brs[0:R, 0:NB], brs[0:R, 0:NB], ACT.Sqrt).then_inc(s["root"], 1)
            act.wait_ge(s["stat"], 2)
            for b in range(NB):
                act.activation(h0[:, b, :], h0[:, b, :], ACT.Relu, scale=brs[0:R, b:b + 1],
                               bias=bnm[0:R, b:b + 1]).then_inc(s["norm"], 1)

            def h_out(g):
                b0, b1 = HB * g, min(HB * g + HB, NB)
                act.wait_ge(s["hp"], g + 1)
                act.copy(hs[0:R, b0:b1, :].rearrange("p b w -> p (b w)"),
                         bank[2 + g % 2][0:R, 0:HW * (b1 - b0)]).then_inc(s["hcp"], 1)

            ng = (NB + HB - 1) // HB
            for g in range(ng):
                b0, b1 = HB * g, min(HB * g + HB, NB)
                act.wait_ge(s["tpd"], g + 1)
                if g >= 2:
                    act.wait_ge(s["hp"], g - 1)
                act.copy(h0T[g % 2][:, 0:R * (b1 - b0)], bank[g % 2][:, 0:R * (b1 - b0)]).then_inc(s["tcp"], 1)
                if g:
                    h_out(g - 1)
            h_out(ng - 1)

            def fill_turn(i, first):
                for c in range(C):
                    t0 = i * TURN + B * c
                    if not first:
                        act.wait_ge(s_sc[c], i * (16 * B))
                    act.copy(recr[:, B * c:B * (c + 1), 0:2], rec2[:, bass.ds(t0, B), :]).then_inc(s["rr"], 1)
                    act.copy(posr[:, B * c:B * (c + 1)], posi[:, bass.ds(t0, B)]).then_inc(s["rr"], 1)
                    act.wait_ge(s["rr"], (C * i + c) * 2 + 2)
                    act.sem_inc(s["rfill"], 1)
                    for j in range(B // 2):
                        m = (B // 2) * c + j
                        pr = i * (TURN // 2) + m
                        act.wait_ge(s["vald"], pr + 1)
                        if not (first and m < 2):
                            act.wait_ge(s["mskd"], pr - 1)
                        act.copy(vcp[m % 2][0:3 * NB, :], bank[4 + m % 2][0:3 * NB, :]).then_inc(s["vcpd"], 1)
                        if j == 0 and not (first and c == 0):
                            act.wait_ge(s["ohr"], C * i + c)
                        for k in (2 * j, 2 * j + 1):
                            act.activation(sqr[:, k, :], iota[:, 0:R], ACT.Square, scale=-1.0,
                                           bias=cr[:, bass.ds(NT + t0 + k, 1)]).then_inc(s["r1"], 1)
                    act.wait_ge(s["r1"], i * TURN + B * (c + 1))
                    if not first:
                        act.wait_ge(s["cntd"], C * i + (c + 1 - C))
                    act.activation(ohr[c], sqr, ACT.Relu, scale=-1.0, bias=onesf[:, 0:1]).then_inc(s["ohr"], 1)
            act.wait_ge(s["ready"], 1)
            turns(act, 2 * HT, fill_turn)

            def distances(T, ks, n0):
                for k in ks:
                    act.activation(sqb[:, k, :], iota[:, 0:R], ACT.Square, scale=-1.0,
                                   bias=srt[:, bass.ds(T * TURN + k, 1), 0:1].rearrange("p a b -> p (a b)")
                                   ).then_inc(s["sq"], 1)

            act.wait_ge(s["sfar"], 1)

            def dist_turn(T, first):
                for c in range(C):
                    if not first:
                        act.wait_ge(s["pend"], C * T + (c + 1 - C))
                    distances(T, range(B * c, B * (c + 1)), 0)
            turns(act, ST, dist_turn)

            def weights(T, q_):
                act.wait_ge(s["xd"], T * (TURN // 4) + (q_ + 1))
                for k in range(4 * q_, 4 * q_ + 4):
                    act.activation(pen[:, k // B, k % B, :], bank[q_ % 3][:, R * (k % 4):R * (k % 4 + 1)], ACT.Exp,
                                   scale=-1.0, bias=srt[:, bass.ds(T * TURN + k, 1), 2:3].rearrange("p a b -> p (a b)")
                                   ).then_inc(s["wd"], 1)

            act.wait_ge(s["guards"], 1)

            def exp_turn(T, peeled):
                for q_ in range(TURN // 4):
                    if peeled:
                        act.wait_ge(s["xd"], T * (TURN // 4) + (q_ + 1 - TURN // 4))
                    distances(T, range(4 * q_, 4 * q_ + 4), NS)
                    if peeled == 0 and q_ == 0:
                        continue
                    if peeled > 1 or (peeled == 1 and q_):
                        act.wait_ge(s["pvd"], T * (TURN // G0) + (4 * q_ - TURN) // G0)
                    if q_:
                        weights(T, q_ - 1)
                    else:
                        weights(T - 1, TURN // 4 - 1)
            exp_turn(0, 0)
            exp_turn(1, 1)
            with act.Fori(2, ST) as T:
                exp_turn(T, 2)
            weights(ST - 1, TURN // 4 - 1)

            act.wait_ge(s["root1"], 1)
            act.activation(rs2[0:R, 0:NB], rs2[0:R, 0:NB], ACT.Sqrt).then_inc(s["root1"], 1)
            act.wait_ge(s["root1"], 3)

            def exps(k):
                act.wait_ge(s["mins"], k + 1)
                v = yb[:, CH * D * k:CH * D * (k + 1)]
                act.activation(v, v, ACT.Exp).then_inc(s["exps"], 1)

            for k in range(NB // CH):
                for b in range(CH * k, CH * (k + 1)):
                    act.activation(ya[:, D * b:D * (b + 1)], ya[:, D * b:D * (b + 1)], ACT.Identity,
                                   scale=rs2[0:R, b:b + 1], bias=nm2[0:R, b:b + 1]).then_inc(s["norm1"], 1)
                if k:
                    exps(k - 1)
            exps(NB // CH - 1)
            act.wait_ge(s["root2"], 1)
            act.activation(rs2[0:R, 0:NB], rs2[0:R, 0:NB], ACT.Sqrt).then_inc(s["root2"], 1)
            act.wait_ge(s["root2"], 3)
            ngh = (NB + 3) // 4
            for g in range(ngh + 1):
                if g < ngh:
                    for b in range(4 * g, min(4 * g + 4, NB)):
                        act.activation(yc[:, D * b:D * (b + 1)], h0[:, b, :], ACT.Relu, scale=rs2[0:R, b:b + 1],
                                       bias=nm2[0:R, b:b + 1]).then_inc(s["norm2"], 1)
                if g:
                    w = R * (min(4 * g, NB) - 4 * (g - 1))
                    act.wait_ge(s["tp1"], g)
                    act.copy(h1T[:, R * 4 * (g - 1):R * 4 * (g - 1) + w], bank[g % 2][:, 0:w]).then_inc(s["tc1"], 1)
            for g in range(ngh):
                w = D * (min(4 * g + 4, NB) - 4 * g)
                act.wait_ge(s["q1"], g + 1)
                act.copy(xagain[:, 4 * D * g:4 * D * g + w], bank[4 + g % 2][0:R, 0:w]).then_inc(s["q2"], 1)
            passes = act.value_load(npass[0:1, 0:1], min_val=1, max_val=NPASS)
            with act.Fori(0, passes) as kp:
                for h in range(2):
                    def relu_turn(i, first, h=h):
                        tt = kp * (2 * HT) + (h * HT + i)
                        for c in range(C):
                            act.wait_ge(s["addh"], (tt * C + (c + 1)) * 2)
                            act.activation(pre[:, c, :], pre[:, c, :], ACT.Relu).then_inc(s["msg"], 1)
                    turns(act, HT, relu_turn)

        @block.tensor
        def _(pe):
            pe.wait_ge(s["cst"], 16)
            pe.wait_ge(s["wl"], 64)
            pe.matmul(bank[2][:, 0:2], wt[:, 0:D], wt[:, 2 * D:2 * D + 2], start=True, stop=True).then_inc(s["wa"], 1)
            pe.wait_ge(s["mask"], NB + 1)
            pe.wait_ge(s["lanes"], 1)
            pe.matmul(bank[6][0:NB + 1, 0:1], cnt, onesf[:, 0:1], start=True, stop=True).then_inc(s["totals"], 1)
            pe.wait_ge(s["tiles"], 1)
            pe.matmul(bank[7][:, 0:NB + 1], small[0:NB + 1, 34:35].to_broadcast([NB + 1, P]), tri[0:NB + 1, 0:NB + 1],
                      start=True, stop=False)
            pe.matmul(bank[7][:, 0:NB + 1], tri, cnt, start=False, stop=True).then_inc(s["first"], 1)
            pe.matmul(bank[6][0:NB + 1, 1:2], inc[0:NB + 1, :], small[0:NB + 1, 32:33],
                      start=True, stop=True).then_inc(s["ends"], 1)
            pe.wait_ge(s["wac"], 1)
            ng = (NB + HB - 1) // HB

            def h_rows(g):
                b0, b1 = HB * g, min(HB * g + HB, NB)
                pe.wait_ge(s["tcp"], g + 1)
                if g >= 2:
                    pe.wait_ge(s["hcp"], g - 1)
                for b in range(b0, b1):
                    mm = pe.matmul(bank[2 + g % 2][0:R, HW * (b - b0):HW * (b - b0 + 1)],
                                   h0T[g % 2][:, R * (b - b0):R * (b - b0 + 1)], wt[:, D:2 * D + 2],
                                   start=True, stop=True)
                mm.then_inc(s["hp"], 1)

            for k in range(NB + 1):
                if k < ng:
                    b0, b1 = HB * k, min(HB * k + HB, NB)
                    pe.wait_ge(s["norm"], b1)
                    if k >= 2:
                        pe.wait_ge(s["tcp"], k - 1)
                    for b in range(b0, b1):
                        mm = pe.transpose(bank[k % 2][:, R * (b - b0):R * (b - b0 + 1)], h0[:, b, :], ident[0:R, 0:R])
                    mm.then_inc(s["tpd"], 1)
                if 1 <= k <= ng:
                    h_rows(k - 1)
                pe.wait_ge(s["prod"], k + 1)
                for q_ in range(2):
                    mm = pe.matmul(bank[4 + q_][:, 0:HALF], ident, prods[k % 2][:, HALF * q_:HALF * (q_ + 1)],
                                   start=(k == 0), stop=(k == NB))
                mm.then_inc(s["rank"], 1)
            pe.wait_ge(s["slots"], 1)
            pe.matmul(bank[7][0:R, 0:NG], onesf[0:NB, 0:R], starts[0:NB, :], start=True, stop=True).then_inc(s["slots"], 1)

            pe.wait_ge(s["ready"], 1)
            counts = bank[7][0:R, 0:2 * NB]
            pe.matmul(counts, identb[:, 0, :], zb, start=True, stop=False)

            def spread(i, m, what, where, rows, name):
                c, j = m // (B // 2), m % (B // 2)
                sel = selb[0:Q, bass.ds(C * i + c, 1)]
                for a_ in range(2):
                    o = a_ * B * P + 256 * j
                    mm = pe.matmul(bank[where + m % 2][0:rows, 256 * a_:256 * (a_ + 1)], sel.to_broadcast([Q, rows]),
                                   what[0:Q, o:o + 256], start=True, stop=True)
                mm.then_inc(s[name], 1)

            def sums(i, m):
                for u in range(2):
                    col = bank[6][:, 2 * m + u:2 * m + u + 1]
                    for a_ in range(2):
                        mm = pe.matmul(col, msk[m % 2][0:3 * NB, 256 * a_ + P * u:256 * a_ + P * (u + 1)],
                                       onesb[0:3 * NB, 0:1], start=(a_ == 0), stop=(a_ == 1))
                if m % (B // 2) == B // 2 - 1:
                    mm.then_inc(s["sumd"], 1)

            spread(0, 0, nat_r, 0, P, "rowb")
            spread(0, 0, nat_b, 2, 3 * NB, "blkb")

            def logit_turn(i, first):
                for m in range(TURN // 2):
                    c, j = m // (B // 2), m % (B // 2)
                    pr = i * (TURN // 2) + m
                    nxt = (i, m + 1) if m + 1 < TURN // 2 else (i + 1, 0)
                    if not (first and m == 0):
                        pe.wait_ge(s["ohtd"], pr)
                    spread(*nxt, nat_r, 0, P, "rowb")
                    pe.wait_ge(s["ohtd"], pr + 1)
                    if not (first and m < 2):
                        pe.wait_ge(s["vcpd"], pr - 1)
                    for a_ in range(2):
                        mm = pe.matmul(bank[4 + m % 2][0:3 * NB, 256 * a_:256 * (a_ + 1)], tb[0:R, a_, 0:3 * NB],
                                       oht[m % 2][0:R, 256 * a_:256 * (a_ + 1)], start=True, stop=True)
                    mm.then_inc(s["vald"], 1)
                    if j == 0 and not (first and c == 0):
                        cb_ = (c - 1) % C
                        pe.wait_ge(s["ohr"], C * i + c)
                        pe.wait_ge(s["ohb"], C * i + c)
                        for k in range(B):
                            mm = pe.matmul(counts, ohr[cb_][:, k, :], ohb[cb_][:, k, :], start=False, stop=False)
                        mm.then_inc(s["cntd"], 1)
                    if not (first and m == 0):
                        pe.wait_ge(s["mskd"], pr)
                        if j == 1 and not (first and c == 0):
                            pe.wait_ge(s["logd"], C * i + c)
                        sums(*((i, m - 1) if m else (i - 1, TURN // 2 - 1)))
                    spread(*nxt, nat_b, 2, 3 * NB, "blkb")
            turns(pe, 2 * HT, logit_turn)
            pe.wait_ge(s["mskd"], HT * TURN)
            sums(2 * HT - 1, TURN // 2 - 1)
            pe.wait_ge(s["ohr"], 2 * HT * C)
            pe.wait_ge(s["ohb"], 2 * HT * C)
            for k in range(B):
                mm = pe.matmul(counts, ohr[C - 1][:, k, :], ohb[C - 1][:, k, :], start=False, stop=(k == B - 1))
            mm.then_inc(s["counted"], 1)
            pe.wait_ge(s["cntc"], 1)
            pe.wait_ge(s["logd"], 2 * HT * C)
            pe.transpose(bank[6][0:2 * NB, 128:128 + R], small[0:R, 64:64 + 2 * NB], ident[0:R, 0:R]
                         ).then_inc(s["cntc"], 1)

            def low_turn(T, first):
                for c in range(C):
                    pe.wait_ge(s["pend"], C * T + (c + 1))
                    for k in range(B):
                        if k % 4 == 0 and not first:
                            pe.wait_ge(s["lowd"], (C * T + c) * 2 + (k // 4 + 1 - 2 * C))
                        mm = pe.transpose(bank[2 * c + k // 4][0:R, P * (k % 4):P * (k % 4 + 1)],
                                          pen[:, c, k, :], ident)
                        if k % 4 == 3:
                            mm.then_inc(s["mtr"], 1)
            pe.wait_ge(s["cntp"], 1)
            turns(pe, ST, low_turn)
            pe.wait_ge(s["guards"], 1)

            def exponents(T, q_, first):
                bk = bank[q_ % 3]
                pe.wait_ge(s["sq"], T * TURN + (NS + 4 * q_ + 4))
                if q_ % 2 == 0:
                    pe.wait_ge(s["grd"], C * T + (q_ // 2 + 1))
                if not (first and q_ < 3):
                    pe.wait_ge(s["wd"], T * TURN + (4 * q_ - 8))
                pe.matmul(bk[:, 0:4 * R], farb[:, :], sqb[:, 4 * q_:4 * q_ + 4, :].rearrange("p k r -> p (k r)"),
                          start=True, stop=False)
                for g in range(2):
                    for p_ in range(3):
                        n_ = 2 * (q_ % 2) + g
                        mm = pe.matmul(bk[:, 2 * R * g:2 * R * (g + 1)],
                                       gring[:, q_ // 2, p_, n_:n_ + 1].to_broadcast([R, P]),
                                       identb[0:R, :, :].rearrange("p a r -> p (a r)"),
                                       start=False, stop=(p_ == 2 and g == 1))
                mm.then_inc(s["xd"], 1)

            def products(T, q_, first, u):
                for k in range(4 * q_, 4 * q_ + 4):
                    if k % B == 0:
                        pe.wait_ge(s_g0[k // B], T * (16 * B) + 16 * B)
                    pe.wait_ge(s["wd"], T * TURN + (k + 1))
                    g = k // G0
                    if k % G0 == 0 and not (first and g < 4):
                        pe.wait_ge(s["fld"], T * (TURN // G0) + (g - 3))
                    mm = pe.matmul(bank[3 + g % 4][0:R, 0:GW], pen[:, k // B, k % B, :],
                                   ring[:, bass.ds(u * TURN + k, 1), :].rearrange("p a w -> p (a w)"),
                                   start=(k % G0 == 0), stop=(k % G0 == G0 - 1))
                    if k % G0 == G0 - 1:
                        mm.then_inc(s["pvd"], 1)

            def sum_turn(T, first, u, Tp, up, second=False):
                for q_ in range(TURN // 4):
                    exponents(T, q_, first)
                    if q_:
                        products(T, q_ - 1, first, u)
                    elif not first:
                        products(Tp, TURN // 4 - 1, False, up)
            last = TURN // 4 - 1
            sum_turn(0, True, 0, 0, 0)
            with pe.Fori(1, RT) as u:
                sum_turn(u, False, u, u - 1, u - 1)
            with pe.Fori(1, RO) as o:
                sum_turn(o * RT, False, 0, o * RT - 1, RT - 1)
                with pe.Fori(1, RT) as u:
                    sum_turn(o * RT + u, False, u, o * RT + (u - 1), u - 1)
            products(ST - 1, last, False, RT - 1)

            pe.wait_ge(s["wl1"], 16 * 19)
            pe.wait_ge(s["fld"], NG)
            pe.matmul(bank[2][0:R, 0:2 * D], small[0:REQ, 0:1].to_broadcast([REQ, R]), pout[0][0:REQ, 0:2 * D],
                      start=True, stop=False)
            pe.matmul(bank[2][0:R, 0:2 * D], onesf[0:1, 0:R], pout[1][0:1, 0:2 * D], start=False, stop=True)
            pe.matmul(bank[3][:, 0:D], wt[:, 2 * D:3 * D], wt[:, 4 * D:5 * D], start=True, stop=True)
            pe.matmul(bank[3][:, D:2 * D], wt[:, 3 * D:4 * D], wt[:, 4 * D:5 * D], start=True, stop=True)
            pe.matmul(bank[3][0:2, 2 * D:3 * D], small[:, 1:3], wt[:, 4 * D:5 * D], start=True, stop=True
                      ).then_inc(s["cm"], 1)
            pe.wait_ge(s["cmd"], 1)
            ngh = (NB + 3) // 4
            for g in range(ngh + 1):
                if g < ngh:
                    b0, b1 = 4 * g, min(4 * g + 4, NB)
                    pe.wait_ge(s["norm2"], b1)
                    if g >= 2:
                        pe.wait_ge(s["tc1"], g - 1)
                    for b in range(b0, b1):
                        mm = pe.transpose(bank[(g + 1) % 2][:, R * (b - b0):R * (b - b0 + 1)], yc[:, D * b:D * (b + 1)],
                                          ident[0:R, 0:R])
                    mm.then_inc(s["tp1"], 1)
                if g:
                    pe.wait_ge(s["tc1"], g)
                    for b in range(4 * (g - 1), min(4 * g, NB)):
                        if b % 2 == 0 and b >= 4:
                            pe.wait_ge(s["pc"], b // 2 - 1)
                        mm = pe.matmul(bank[2 + b // 2 % 2][0:R, 2 * D * (b % 2):2 * D * (b % 2 + 1)],
                                       h1T[:, R * b:R * (b + 1)], wt[:, 0:2 * D], start=True, stop=True)
                        if b % 2 == 1 or b == NB - 1:
                            mm.then_inc(s["pp"], 1)
            pe.wait_ge(s["u3d"], 1)
            for b in range(NB):
                g = b // 4
                if b % 4 == 0 and g >= 2:
                    pe.wait_ge(s["q2"], g - 1)
                o = bank[4 + g % 2][0:R, D * (b % 4):D * (b % 4 + 1)]
                pe.matmul(o, h1T[:, R * b:R * (b + 1)], w2u[:, 2 * D:3 * D], start=True, stop=False)
                mm = pe.matmul(o, cntT[:, R * b:R * (b + 1)], u3[0:3, 0:D], start=False, stop=True)
                if b % 4 == 3 or b == NB - 1:
                    mm.then_inc(s["q1"], 1)
            pe.wait_ge(s["pc"], (NB + 1) // 2)
            pe.wait_ge(s["q2"], ngh)

            passes = pe.value_load(npass[0:1, 0:1], min_val=1, max_val=NPASS)
            with pe.Fori(0, passes) as kp:
                for h in range(2):
                    def seg(nb, c, skip):
                        pe.wait_ge(s["msg"], nb + 1)
                        pe.wait_ge(s["ohd"], nb + 1)
                        for k in range(B):
                            if k % GT == 0 and not skip:
                                pe.wait_ge(s["fld"], nb * 2 + (NG + k // GT - 1))
                            mm = pe.matmul(bank[6 + k // GT][:, 0:WIN], pre[:, c, k * D:(k + 1) * D],
                                           oh1[:, c, k * WIN:(k + 1) * WIN], start=(k % GT == 0), stop=(k % GT == GT - 1))
                            if k % GT == GT - 1:
                                mm.then_inc(s["pso"], 1)

                    def msg_turn(i, first, h=h):
                        tt = kp * (2 * HT) + (h * HT + i)
                        for c in range(C):
                            nb = tt * C + c
                            pe.wait_ge(s_ld[c], tt * 32 + 32)
                            if not first:
                                pe.wait_ge(s["addh"], nb * 2 + (2 - 2 * C))
                            for k in range(B):
                                mm = pe.matmul(bank[2 * c + k // 4][:, P * (k % 4):P * (k % 4 + 1)],
                                               eat[0:EA, c, k * P:(k + 1) * P],
                                               wt[0:EA, (5 + h) * D:(6 + h) * D], start=True, stop=True)
                            mm.then_inc(s["ea"], 1)
                            if not (first and c == 0):
                                seg(nb - 1, (c - 1) % C, first and c == 1)
                    turns(pe, HT, msg_turn)
                    seg(kp * (2 * HT * C) + ((h + 1) * HT * C - 1), C - 1, False)
                    pe.wait_ge(s["fld"], ((kp * 2 + (h + 1)) * HT) * (TURN // GT) + NG)

            for b in range(NB):
                g = b // 4
                if b % 4 == 0 and g >= 3:
                    pe.wait_ge(s["hf"], g - 2)
                o = bank[g % 3][0:R, D * (b % 4):D * (b % 4 + 1)]
                pe.matmul(o, accT[0][:, R * b:R * (b + 1)], w2u[:, 0:D], start=True, stop=False)
                mm = pe.matmul(o, accT[1][:, R * b:R * (b + 1)], w2u[:, D:2 * D], start=False, stop=True)
                if b % 4 == 3 or b == NB - 1:
                    mm.then_inc(s["out0"], 1)

        @block.vector
        def _(dve):
            n_step = [0]

            def link(ins):
                n_step[0] += 1
                ins.then_inc(s["dsteps"], 1)
                dve.wait_ge(s["dsteps"], n_step[0])

            def signal(name, ins):
                link(ins)
                dve.sem_inc(s[name], 1)

            def divmod_r(v, t, b, r):
                link(dve.tensor_scalar(t, v, 0.5, 1.0 / R, ALU.add, ALU.mult))
                link(dve.tensor_scalar(t, t, -0.5, MAGIC, ALU.add, ALU.add))
                link(dve.tensor_scalar(b, t, -MAGIC, None, ALU.add))
                link(dve.scalar_tensor_tensor(r, b, -float(R), v, ALU.mult, ALU.add))

            def floor_div(v, t, by):
                link(dve.tensor_scalar(t, v, 1.0 / by, -(by - 1) / (2.0 * by), ALU.mult, ALU.add))
                link(dve.tensor_scalar(t, t, MAGIC, -MAGIC, ALU.add, ALU.add))

            src, dst = slice(0, NT), slice(NT, 2 * NT)
            dve.wait_ge(s["coli"], 16)
            dve.memset(onesf[:, :], 1.0).then_inc(s["dsteps"], 1)
            n_step[0] += 1
            link(dve.tensor_copy(cf[:, src], col_i[:, src]))
            divmod_r(cf[:, src], ct[:, src], cb[:, src], cr[:, src])
            dve.sem_inc(s["blocks"], 1)
            link(dve.memset(fill[:, :, 0:1], -1.0))
            signal("pat", dve.memset(fill[:, :, 1:3], 0.0))
            link(dve.memset(onesb[:, :], 1.0))
            link(dve.memset(zb, 0.0))
            dve.wait_ge(s["x"], 16)
            for b in range(NB):
                dve.bn_stats(bst[0:R, b, :], h0[:, b, :]).then_inc(s["dsteps"], 1)
            n_step[0] += NB
            dve.wait_ge(s["dsteps"], n_step[0])
            for b in range(NB):
                dve.bn_aggr(bmv[0:R, b, :], bst[0:R, b, :]).then_inc(s["dsteps"], 1)
            n_step[0] += NB
            dve.wait_ge(s["dsteps"], n_step[0])
            signal("stat", dve.tensor_scalar(brs[0:R, 0:NB], bmv[0:R, :, 1], EPS, None, ALU.add))
            dve.wait_ge(s["wa"], 1)
            signal("wac", dve.tensor_copy(wt[:, 2 * D:2 * D + 2], bank[2][:, 0:2]))
            link(dve.tensor_copy(cf[:, dst], col_i[:, dst]))
            divmod_r(cf[:, dst], ct[:, dst], cb[:, dst], cr[:, dst])
            link(dve.tensor_copy(rec2[:, :, 0], cr[:, src]))
            link(dve.tensor_copy(rec2[:, :, 1], cf[:, dst]))
            link(dve.tensor_scalar(ct[:, src], cb[:, src], float(NB), 1000.0, ALU.is_equal, ALU.mult))
            link(dve.tensor_tensor(cb[:, dst], cb[:, dst], ct[:, src], ALU.add))
            hb = cb[:, NT + HALF:2 * NT]
            link(dve.tensor_scalar(hb, hb, float(NB), None, ALU.add))
            link(dve.tensor_copy(srcg[:, 0:HALF], col_i[:, 0:HALF]))
            link(dve.tensor_scalar(srcg[:, HALF:NT], col_i[:, HALF:NT], float(TN), None, ALU.add))
            dve.wait_ge(s["nati"], 16)
            dve.wait_ge(s["fill"], 16)
            link(dve.tensor_copy(nat_f[0:Q, :], nat_i[0:Q, :]))
            divmod_r(nat_f[0:Q, :], nat_t[0:Q, :], nat_b[0:Q, :], nat_r[0:Q, :])
            dn = nat_f[0:Q, B * P:2 * B * P].rearrange("p (c e) -> p c e", c=B // GT)
            link(dve.tensor_reduce(small[0:Q, 0:2], dn, AX.X, ALU.min))
            link(dve.tensor_reduce(small[0:Q, 2:4], dn, AX.X, ALU.max))
            signal("win", dve.tensor_tensor(small[0:Q, 2:4], small[0:Q, 2:4], small[0:Q, 0:2], ALU.subtract))
            dve.wait_ge(s["mask"], NB + 1)
            dve.sem_inc(s["lanes"], 1)
            dve.wait_ge(s["root"], 1)
            link(dve.reciprocal(brs[0:R, 0:NB], brs[0:R, 0:NB]))
            signal("stat", dve.scalar_tensor_tensor(bnm[0:R, 0:NB], bmv[0:R, :, 0], -1.0, brs[0:R, 0:NB],
                                                    ALU.mult, ALU.mult))
            dve.wait_ge(s["totals"], 1)
            tl, te, t0_ = (small[0:NB + 1, k:k + 1] for k in (32, 33, 35))
            link(dve.tensor_scalar(t0_, bank[6][0:NB + 1, 0:1], float(G0 * P - 1), None, ALU.add))
            floor_div(t0_, tl, float(G0 * P))
            signal("tiles", dve.tensor_scalar(small[0:NB + 1, 34:35], tl, float(G0 * P), None, ALU.mult))
            dve.wait_ge(s["first"], 1)
            link(dve.tensor_copy(laneoff[:, :], bank[7][:, 0:NB + 1]))
            for k in range(NB + 1):
                if k >= 2:
                    dve.wait_ge(s["prod"], k - 1)
                dve.tensor_tensor_scan(scans[k % 2], masks[:, k, :], masks[:, k, :], laneoff[:, k:k + 1],
                                       ALU.add, ALU.max).then_inc(s["scan"], 1)
            dve.wait_ge(s["ends"], 1)
            link(dve.tensor_copy(te, bank[6][0:NB + 1, 1:2]))
            signal("slots", dve.tensor_scalar(starts[0:NB, :], iota[0:NB, 0:NG], te[0:NB, :], None, ALU.is_ge))
            dve.wait_ge(s["hcp"], (NB + HB - 1) // HB)
            t3 = tf[0:R, :].rearrange("p (a k) -> p a k", a=2)
            link(dve.tensor_copy(t3, hs[0:R, :, D:HW].rearrange("p b a -> p a b")))
            for p_ in range(3):
                part = tb[0:R, :, NB * p_:NB * (p_ + 1)]
                link(dve.tensor_copy(part, t3))
                if p_ < 2:
                    link(dve.tensor_tensor(t3, t3, part, ALU.subtract))
            dve.wait_ge(s["rank"], NB + 1)
            for q_ in range(2):
                w = slice(HALF * q_, HALF * (q_ + 1))
                link(dve.tensor_scalar(scans[0][:, w], bank[4 + q_][:, 0:HALF], -1.0, None, ALU.add))
            floor_div(scans[0], scans[1], float(P))
            link(dve.scalar_tensor_tensor(scans[0], scans[1], -float(P), scans[0], ALU.mult, ALU.add))
            link(dve.scalar_tensor_tensor(posi[:, :], scans[0], float(SW), scans[1], ALU.mult, ALU.add))
            dve.wait_ge(s["wcol"], 16)
            dve.wait_ge(s["slots"], 2)
            link(dve.tensor_scalar(offs[0:1, :], bank[7][0:1, 0:NG], float(GW), None, ALU.mult))
            link(dve.tensor_copy(low[:, 0, :], bank[7][0:R, 0:NG]))
            dve.sem_inc(s["ready"], 1)

            def logits(i, c, first):
                dve.wait_ge(s["sumd"], c16(i, c))
                if not first:
                    dve.wait_ge(s_sc[c], i * (16 * B))
                ps = bank[6][:, B * c:B * (c + 1)]
                dve.tensor_scalar(lk, ps, SLOPE, None, ALU.mult).then_inc(s["lks"], 1)
                dve.wait_ge(s["lks"], (C * i + c) * 2 + 1)
                dve.tensor_tensor(lk, ps, lk, ALU.max).then_inc(s["lks"], 1)
                dve.wait_ge(s["lks"], (C * i + c) * 2 + 2)
                dve.tensor_tensor(recr[:, B * c:B * (c + 1), 2], lk, wcol[:, bass.ds(i * TURN + B * c, B)],
                                  ALU.mult).then_inc(s["logd"], 1)

            def own_block(i, m):
                pr = i * (TURN // 2) + m
                dve.wait_ge(s["blkb"], pr + 1)
                dve.wait_ge(s["vcpd"], pr + 1)
                dve.scalar_tensor_tensor(msk[m % 2][0:3 * NB, :], bank[2 + m % 2][0:3 * NB, :],
                                         iota_pb[0:3 * NB, :], vcp[m % 2][0:3 * NB, :],
                                         ALU.is_equal, ALU.mult).then_inc(s["mskd"], 1)

            def logit_turn(i, first):
                for m in range(TURN // 2):
                    c, j = m // (B // 2), m % (B // 2)
                    pr = i * (TURN // 2) + m
                    t0 = i * TURN + B * c
                    if j == 1 and not (first and c == 0):
                        if c:
                            logits(i, c - 1, first)
                        else:
                            logits(i - 1, C - 1, False) if not first1[0] else logits(i - 1, C - 1, True)
                    dve.wait_ge(s["rowb"], pr + 1)
                    if not (first and m < 2):
                        dve.wait_ge(s["vald"], pr - 1)
                    dve.tensor_scalar(oht[m % 2][0:R, :], bank[m % 2][0:R, :], iota_p[0:R, :], None,
                                      ALU.is_equal).then_inc(s["ohtd"], 1)
                    if j == 2:
                        if not first:
                            dve.wait_ge(s["cntd"], C * i + (c + 1 - C))
                        dve.tensor_tensor(
                            ohb[c], iota[:, 0:2 * NB].rearrange("p (o k) -> p o k", o=1).to_broadcast([P, B, 2 * NB]),
                            cb[:, bass.ds(NT + t0, B)].rearrange("p (b o) -> p b o", o=1).to_broadcast([P, B, 2 * NB]),
                            ALU.is_equal).then_inc(s["ohb"], 1)
                    if m:
                        own_block(i, m - 1)
                    elif not first:
                        own_block(i - 1, TURN // 2 - 1)
            first1 = [True]
            logit_turn(0, True)
            logit_turn(1, False)
            first1[0] = False
            with dve.Fori(2, 2 * HT) as i:
                logit_turn(i, False)
            own_block(2 * HT - 1, TURN // 2 - 1)
            logits(2 * HT - 1, C - 1, False)

            dve.wait_ge(s["counted"], 1)
            signal("cntc", dve.tensor_copy(small[0:R, 64:64 + 2 * NB], bank[7][0:R, 0:2 * NB]))
            dve.wait_ge(s["cntc"], 2)
            signal("cntp", dve.tensor_copy(mcnt, bank[6][0:2 * NB, 128:128 + R]))
            dve.wait_ge(s["winr"], 32)
            link(dve.tensor_tensor(rel[:, :].rearrange("p (g k) -> p g k", k=GT),
                                   cf[:, dst].rearrange("p (g k) -> p g k", k=GT),
                                   winb.rearrange("p (g o) -> p g o", o=1).to_broadcast([P, NT // GT, GT]),
                                   ALU.subtract))
            link(dve.tensor_copy(base[:, :], brow[0:1, 0:NT // GT]))
            sp_, sq1 = small[0:1, 40:41], small[0:1, 41:42]
            link(dve.tensor_reduce(sp_, brow[0:1, NT // GT:2 * NT // GT], AX.X, ALU.max))
            floor_div(sp_, sq1, float(WIN))
            link(dve.tensor_scalar(npass[:, :], sq1, 1.0, None, ALU.add))
            link(dve.tensor_tensor(newb[:, 1:NG], low[:, 0, 1:NG], low[:, 0, 0:NG - 1], ALU.not_equal))
            link(dve.tensor_scalar(newb[:, 1:NG], newb[:, 1:NG], 6e38 / 2, -1.5e38, ALU.mult, ALU.add))
            link(dve.memset(newb[:, 0:1], 1.5e38))
            link(dve.memset(newb[:, NG:NG + 1], 1.5e38))
            dve.wait_ge(s["rfill"], 2 * HT * C)
            dve.wait_ge(s["cntw"], 16)
            for c in range(C):
                dve.wait_ge(s_sc[c], 16 * B * 2 * HT)
            signal("ones", dve.memset(ring[:, :, D:GW], 1.0))
            link(dve.memset(zacc[:, :], 0.0))
            dve.wait_ge(s["srtl"], 16)
            signal("sfar", dve.tensor_copy(sdst[:, :], srt[:, :, 1]))

            def lowest(T, c):
                for q_ in range(2):
                    dve.wait_ge(s["mtr"], (C * T + c) * 2 + (q_ + 1))
                    dve.tensor_reduce(low[:, 0, bass.ds(T * (TURN // G0) + (B * c // G0 + 2 * q_), 2)],
                                      bank[2 * c + q_][0:R, :].rearrange("p (g e) -> p g e", g=2), AX.X,
                                      ALU.min).then_inc(s["lowd"], 1)

            def penal_turn(T, first):
                for c in range(C):
                    dve.wait_ge(s["sq"], T * TURN + B * (c + 1))
                    if not first:
                        dve.wait_ge(s["mtr"], (C * T + c) * 2 + (2 - 2 * C))
                    lg = srt[:, bass.ds(T * TURN + B * c, B), 2:3].to_broadcast([P, B, R])
                    dve.scalar_tensor_tensor(pen[:, c, :, :], sqb[:, B * c:B * (c + 1), :], FAR, lg,
                                             ALU.mult, ALU.subtract).then_inc(s["pend"], 1)
                    if c:
                        lowest(T, c - 1)
                    elif not first:
                        lowest(T - 1, C - 1)
            turns(dve, ST, penal_turn)
            lowest(ST - 1, C - 1)
            dve.wait_ge(s["lowd"], NG // 2)
            link(dve.tensor_tensor_scan(low[:, 1, :], newb[:, 0:NG], low[:, 0, :], 3e38, ALU.max, ALU.min))
            link(dve.tensor_tensor_scan(low[:, 2, ::-1], newb[:, 1:NG + 1][:, ::-1], low[:, 0, ::-1], 3e38,
                                        ALU.max, ALU.min))
            link(dve.tensor_tensor(low[:, 0, :], low[:, 1, :], low[:, 2, :], ALU.min))
            link(dve.tensor_scalar(low[:, 0, :], low[:, 0, :], NOMAX, -1.0, ALU.min, ALU.mult))
            for p_ in range(3):
                link(dve.tensor_copy(guard[:, p_, :], low[:, 0, :]))
                if p_ < 2:
                    link(dve.tensor_tensor(low[:, 0, :], low[:, 0, :], guard[:, p_, :], ALU.subtract))
            dve.sem_inc(s["guards"], 1)

            def add_sums(T, c, first):
                for g in range(B // G0 * c, B // G0 * (c + 1)):
                    o = dve.value_load(offs[0:1, bass.ds(T * (TURN // G0) + g, 1)], min_val=0, max_val=NB * GW)
                    dve.wait_ge(s["pvd"], T * (TURN // G0) + (g + 1))
                    if not (first and g == 0):
                        dve.wait_ge(s["fld"], T * (TURN // G0) + g)
                    z = zacc[0:R, bass.ds(o, GW)]
                    dve.tensor_tensor(z, z, bank[3 + g % 4][0:R, 0:GW], ALU.add).then_inc(s["fld"], 1)

            def soft_turn(T, first):
                for c in range(C):
                    if not first:
                        dve.wait_ge(s["xd"], T * (TURN // 4) + (2 * (c + 1) - TURN // 4))
                    dve.tensor_copy(gring[:, c, :, :], guard[:, :, bass.ds(T * (TURN // G0) + B // G0 * c, B // G0)]
                                    ).then_inc(s["grd"], 1)
                    if c:
                        add_sums(T, c - 1, first)
                    elif not first:
                        add_sums(T - 1, C - 1, False)
            turns(dve, ST, soft_turn)
            add_sums(ST - 1, C - 1, False)
            dve.wait_ge(s["fld"], NG)
            dve.sem_inc(s["zdone"], 1)

            z3 = zacc[0:R, 0:NB * GW].rearrange("p (b w) -> p b w", w=GW)
            none, dsum, dinv = (den[0:R, NB * q_:NB * (q_ + 1)] for q_ in range(3))
            link(dve.tensor_scalar(none, z3[:, :, D], 0.0, None, ALU.is_equal))
            link(dve.memset(padrow[:, :], -1e30))
            dve.sem_inc(s["none"], 1)
            link(dve.tensor_tensor(dsum, z3[:, :, D], none, ALU.add))
            link(dve.reciprocal(dinv, dsum))

            def bc(v, d):
                return v.rearrange("p (b o) -> p b o", o=1).to_broadcast([R, CH, d])

            def row(q_):
                return gbc[0:R, D * q_:D * (q_ + 1)].rearrange("p (o d) -> p o d", o=1).to_broadcast([R, CH, D])

            def chunk(v, k):
                return v[:, CH * D * k:CH * D * (k + 1)]

            def by_block(v):
                return v.rearrange("p (b d) -> p b d", d=D)

            def stats(k, v):
                for b in range(CH * k, CH * (k + 1)):
                    dve.bn_stats(st2[0:R, b, :], v(b)).then_inc(s["dsteps"], 1)
                n_step[0] += CH
                dve.wait_ge(s["dsteps"], n_step[0])
                for b in range(CH * k, CH * (k + 1)):
                    dve.bn_aggr(mv2[0:R, b, :], st2[0:R, b, :]).then_inc(s["dsteps"], 1)
                n_step[0] += CH
                dve.wait_ge(s["dsteps"], n_step[0])

            def norms(name):
                signal(name, dve.tensor_scalar(rs2[0:R, 0:NB], mv2[0:R, :, 1], EPS, None, ALU.add))
                dve.wait_ge(s[name], 2)
                link(dve.reciprocal(rs2[0:R, 0:NB], rs2[0:R, 0:NB]))
                signal(name, dve.scalar_tensor_tensor(nm2[0:R, 0:NB], mv2[0:R, :, 0], -1.0, rs2[0:R, 0:NB],
                                                      ALU.mult, ALU.mult))

            for k in range(NB // CH):
                bl = slice(CH * k, CH * (k + 1))
                link(dve.tensor_tensor(by_block(chunk(ya, k)), z3[:, bl, 0:D], bc(dinv[:, bl], D), ALU.mult))
                dve.wait_ge(s["hn"], 2 * (k + 1))
                link(dve.tensor_tensor(chunk(ya, k), chunk(ya, k), chunk(yb, k), ALU.add))
                stats(k, lambda b: ya[:, D * b:D * (b + 1)])
            norms("root1")
            dve.wait_ge(s["wl1"], 16 * 19)
            dve.wait_ge(s["xa"], 16)

            def elu(k):
                dve.wait_ge(s["exps"], k + 1)
                y = chunk(ya, k)
                link(dve.scalar_tensor_tensor(y, y, 0.0, chunk(yb, k), ALU.max, ALU.add))
                link(dve.scalar_tensor_tensor(h0[:, CH * k:CH * (k + 1), :].rearrange("p b d -> p (b d)"), y, -1.0,
                                              chunk(xagain, k), ALU.add, ALU.add))
                stats(k, lambda b: h0[:, b, :])

            for k in range(NB // CH):
                y = chunk(ya, k)
                dve.wait_ge(s["norm1"], CH * (k + 1))
                link(dve.tensor_tensor(by_block(y), by_block(y), row(0), ALU.mult))
                link(dve.tensor_tensor(by_block(y), by_block(y), row(1), ALU.add))
                signal("mins", dve.tensor_scalar(chunk(yb, k), y, 0.0, None, ALU.min))
                if k:
                    elu(k - 1)
            elu(NB // CH - 1)
            norms("root2")
            dve.wait_ge(s["cm"], 1)
            link(dve.tensor_copy(crow[0:R, 0:2 * D], bank[2][0:R, 0:2 * D]))
            link(dve.tensor_copy(crow[0:R, 2 * D:4 * D], bank[2][0:R, 0:2 * D]))
            link(dve.tensor_copy(w2u[:, 0:2 * D], bank[3][:, 0:2 * D]))
            link(dve.tensor_copy(u3[0:2, :], bank[3][0:2, 2 * D:3 * D]))
            link(dve.tensor_scalar(small[:, 3:4], small[:, 3:4], 1.0, None, ALU.add))
            link(dve.tensor_scalar(w2u[:, 2 * D:3 * D], wt[:, 4 * D:5 * D], small[:, 3:4], None, ALU.mult))
            dve.sem_inc(s["cmd"], 1)
            dve.sem_inc(s["u3d"], 1)
            for g in range((NB + 1) // 2):
                w = 2 * D * (min(2 * g + 2, NB) - 2 * g)
                dve.wait_ge(s["pp"], g + 1)
                if g >= 2:
                    dve.wait_ge(s_pst[g % 2], 16 * (g - g % 2 + (g % 2 == 0)))
                signal("pc", dve.tensor_tensor(pout[g % 2][0:R, 0:w], bank[2 + g % 2][0:R, 0:w], crow[0:R, 0:w],
                                               ALU.add))
            link(dve.memset(accT[0], 0.0))
            link(dve.memset(accT[1], 0.0))

            passes = dve.value_load(npass[0:1, 0:1], min_val=1, max_val=NPASS)
            with dve.Fori(0, passes) as kp:
                for h in range(2):
                    def flush(nb, i, c, h=h):
                        for g in range(B // GT):
                            t = i * (TURN // GT) + ((h * HALF + B * c) // GT + g)
                            o = dve.value_load(base[0:1, bass.ds(t, 1)], min_val=0, max_val=N)
                            dve.wait_ge(s["pso"], nb * 2 + (g + 1))
                            dve.wait_ge(s["fld"], nb * 2 + (NG + g))
                            w = accT[h][:, bass.ds(o, WIN)]
                            dve.tensor_tensor(w, w, bank[6 + g][:, 0:WIN], ALU.add).then_inc(s["fld"], 1)

                    def msg_turn(i, first, h=h):
                        tt = kp * (2 * HT) + (h * HT + i)
                        for c in range(C):
                            nb = tt * C + c
                            t0 = i * TURN + (h * HALF + B * c)
                            if not first:
                                dve.wait_ge(s["pso"], nb * 2 + (2 - 2 * C))
                            dve.tensor_tensor(oh1[:, c, :].rearrange("p (k w) -> p k w", k=B),
                                              iota[:, 0:WIN].rearrange("p (o w) -> p o w", o=1).to_broadcast([P, B, WIN]),
                                              rel[:, bass.ds(t0, B)].rearrange("p (k o) -> p k o", o=1).to_broadcast([P, B, WIN]),
                                              ALU.is_equal).then_inc(s["ohd"], 1)
                            dve.wait_ge(s["ea"], nb + 1)
                            dve.wait_ge(s_g1[c], tt * (16 * B) + 16 * B)
                            for g in range(2):
                                w = slice(512 * g, 512 * (g + 1))
                                dve.tensor_tensor(pre[:, c, w], bank[2 * c + g][:, :], g1[:, c, w],
                                                  ALU.add).then_inc(s["addh"], 1)
                            if c:
                                flush(nb - 1, i, c - 1)
                            elif not first:
                                flush(nb - 1, i - 1, C - 1)
                    turns(dve, HT, msg_turn)
                    flush(kp * (2 * HT * C) + ((h + 1) * HT * C - 1), HT - 1, C - 1)
                    dve.wait_ge(s["fld"], ((kp * 2 + (h + 1)) * HT) * (TURN // GT) + NG)
                dve.tensor_scalar(rel[:, :], rel[:, :], -float(WIN), None, ALU.add).then_inc(s["nextw"], 1)
                dve.tensor_scalar(base[:, :], base[:, :], float(WIN), float(N), ALU.add, ALU.min).then_inc(s["nextw"], 1)
                dve.wait_ge(s["nextw"], kp * 2 + 2)

            for g in range((NB + 3) // 4):
                b0, b1 = 4 * g, min(4 * g + 4, NB)
                w = D * (b1 - b0)
                q = xagain[:, D * b0:D * b1]
                dve.wait_ge(s["out0"], g + 1)
                dve.tensor_tensor(q, q, bank[g % 3][0:R, 0:w], ALU.add).then_inc(s["hf"], 1)
                dve.wait_ge(s["hf"], g + 1)
                x1 = h0[:, b0:b1, :].rearrange("p b d -> p (b d)")
                dve.scalar_tensor_tensor(x1, q, 0.0, x1, ALU.max, ALU.add).then_inc(s["outd"], 1)


def _lay(inputs):
    import numpy as np

    def slots(v, pad):
        halves = [v[:EH[0]], v[EH[0]:]]
        room = HT * TURN * P
        if pad is None:
            return np.concatenate([np.pad(x, (0, room - len(x)), mode="edge") for x in halves])
        return np.concatenate([np.pad(x, (0, room - len(x)), constant_values=pad) for x in halves])

    g = {k: np.asarray(v) for k, v in inputs.items()}
    src, dst = slots(g["src"], N), slots(g["dst"], None)
    w = slots(g["edge_weight"], 0)
    nat = np.concatenate([src.reshape(Q, B * P), dst.reshape(Q, B * P)], 1)
    col = np.concatenate([src.reshape(NT, P).T, dst.reshape(NT, P).T], 1)
    ea = g["edge_attr_16"].T
    eat = np.zeros((EA, NT * P), ea.dtype)
    eat[:, :EH[0]] = ea[:, :EH[0]]
    eat[:, HT * TURN * P:HT * TURN * P + EH[1]] = ea[:, EH[0]:]
    cst = np.zeros((P, C_W), np.float32)
    cst[:, C_ID:C_ID + P] = np.eye(P)
    cst[:, C_TRI:C_TRI + P] = np.triu(np.ones((P, P)), 1)
    cst[:, C_IOTA:C_IOTA + NG] = np.arange(NG)
    cst[:, C_P] = np.arange(P)
    cst[:, C_PB] = np.arange(P) % NB
    cst[:NB + 1, C_INC:] = np.triu(np.ones((NB + 1, NB + 1)))
    return {
        "cst": cst, "nat": nat, "col": col, "w": w.reshape(NT, P).T, "eaT": eat, "x": g["x"],
        "W": g["L0_gnn_W"], "WT": g["L0_gnn_W"].T, "as": g["L0_gnn_a_src"], "ad": g["L0_gnn_a_dst"],
        "gamma": g["L0_gnn_ln_gamma"], "beta": g["L0_gnn_ln_beta"], "req": g["L1_gnn_req_emb"],
        "W1f": g["L1_gnn_W1f"], "W1b": g["L1_gnn_W1b"], "b1f": g["L1_gnn_b1f"], "b1b": g["L1_gnn_b1b"],
        "W2fT": g["L1_gnn_W2f"].T, "W2bT": g["L1_gnn_W2b"].T, "b2f": g["L1_gnn_b2f"], "b2b": g["L1_gnn_b2b"],
        "Wu": g["L1_gnn_Wu"], "bu": g["L1_gnn_bu"], "eps": g["L1_gnn_eps"],
    }


def kernel(**inputs):
    import numpy as _np
    import concourse.bacc as _bacc
    from concourse import mybir as _mybir
    from concourse.bass_utils import run_bass_kernel_spmd as _run

    nc = _bacc.Bacc("TRN2", target_bir_lowering=False, num_devices=1)
    arrays, args = {}, {}
    for name, v in _lay(inputs).items():
        v = _np.ascontiguousarray(v)
        arrays[f"in_{name}"] = v
        args[name] = nc.dram_tensor(f"in_{name}", v.shape, _mybir.dt.from_np(v.dtype), kind="ExternalInput").ap()
    out = nc.dram_tensor("out_x", (N, D), F32, kind="ExternalOutput").ap()
    scratch = {
        "rec": nc.dram_tensor("scr_rec", (P * SW, 3), F32).ap(),
        "H": nc.dram_tensor("scr_H", (N, D), F32).ap(),
        "PP": nc.dram_tensor("scr_PP", (2 * TN, D), F32).ap(),
        "base": nc.dram_tensor("scr_base", (2, NT // GT), F32).ap(),
        "cnt": nc.dram_tensor("scr_cnt", (2 * N,), F32).ap(),
    }
    build(nc, args, out, scratch)
    r = _run(nc, [arrays], core_ids=[0])
    return r.results[0]["out_x"]
```

```python
from contextlib import ExitStack

import concourse.bass as bass
from concourse import mybir

ALU = mybir.AluOpType
ACT = mybir.ActivationFunctionType
AX = mybir.AxisListType
F32 = mybir.dt.float32
BF16 = mybir.dt.bfloat16
I32 = mybir.dt.int32

P = 128
D = 128
N = 3125
R = 125
NB = N // R
E = 103125
EH = (E // 2, E - E // 2)
B = 8
C = 3
TURN = B * C
HT = 17
NT = 2 * HT * TURN
Q = NT // B
G0 = 2
ST = 36
NS = ST * TURN
RT = 9
RO = ST // RT
RING = RT * TURN
SW = NS + TURN
GW = D + 1
EA = 16
REQ = 16
TN = N + 1
GT = 4
WIN = 64
NPASS = -(-N // WIN)
AW = N + WIN
EPS = 1e-5
SLOPE = 0.2
MAGIC = 12582912.0
NG = NS // G0
FAR = 2.0 ** 110
NOMAX = 1e32
CH = 5
HB = 3
HW = D + 2
HALF = NT // 2
NPA = 6

BA = 7
KD = 20
assert NB + 1 - KD <= (NB + HB - 1) // HB - 2
assert 2 * HT * TURN * P >= E and HT * TURN * P >= max(EH)
assert NG * G0 * P >= E + NB * (G0 * P - 1) and RO * RT == ST and NT % B == 0

C_ID, C_TRI, C_IOTA = 0, P, 2 * P
C_P = C_IOTA + NS // G0
C_PB = C_P + 1
C_INC = C_PB + 1
C_S3 = C_INC + NB + 1
C_W = C_S3 + TURN


def turns(eng, count, body):
    body(0, True)
    with eng.Fori(1, count) as i:
        body(i, False)


def half_turns(eng, h, body):
    if h == 0:
        turns(eng, HT, body)
    else:
        with eng.Fori(0, HT) as i:
            body(i, False)


def build(nc, a, out, scr):
    with ExitStack() as ctx:
        def sb(name, shape, dt):
            return ctx.enter_context(nc.sbuf_tensor(name, shape, dt))

        def sem(name):
            return ctx.enter_context(nc.semaphore(name))

        bank = [ctx.enter_context(nc.psum_tensor(f"bank{i}", [P, 512], F32)) for i in range(8)]

        cst = sb("cst", [P, C_W], F32)
        identb = sb("identb", [P, 2, R], BF16)
        farb = sb("farb", [P, P], BF16)
        selb = sb("selb", [P, P], BF16)
        onesb = sb("onesb", [P, 1], BF16)
        sel3 = sb("sel3", [P, TURN], BF16)
        onesf = sb("onesf", [P, P], F32)
        h0 = sb("h0", [R, NB, D], F32)
        hs = sb("hs", [P, NB, HW], F32)
        zacc = sb("zacc", [P, (NB + 1) * GW], F32)
        srt = sb("srt", [P, NS, 3], F32)
        sdst = sb("sdst", [P, NS], I32)
        srcg = sb("srcg", [P, NT], I32)
        rel = sb("rel", [P, NT], F32)
        offs = sb("offs", [1, NG], I32)
        newb = sb("newb", [R, NG + 1], F32)
        low = sb("low", [R, 3, NG], F32)
        guard = sb("guard", [R, 3, NG], BF16)
        base = sb("base", [1, NT // GT], I32)
        npass = sb("npass", [1, 1], I32)
        idxr = sb("idxr", [P, RING], I32)
        wt = sb("wt", [P, 7 * D], F32)
        small = sb("small", [P, 256], F32)
        arena = sb("arena", [P, RING * GW], F32)
        AR = RING * GW
        ring = arena[:, :].rearrange("p (s w) -> p s w", w=GW)

        ident = cst[:, C_ID:C_ID + P]
        tri = cst[:, C_TRI:C_TRI + P]
        iota = cst[:, C_IOTA:C_IOTA + NG]
        iota_p = cst[:, C_P:C_P + 1]
        iota_pb = cst[:, C_PB:C_PB + 1]
        inc = cst[:, C_INC:C_INC + NB + 1]

        at = [0]

        def taker():
            at[0] = 0

            def take(n):
                n += n % 2
                v = arena[:, at[0]:at[0] + n]
                at[0] += n
                assert at[0] <= AR, at[0]
                return v
            return take

        sq_ = sb("sq_", [P, C * B * P], F32)
        pen = sq_[:, 0:TURN * R].rearrange("p (c k r) -> p c k r", c=C, r=R)
        sqb = sb("sqb", [P, TURN, R], BF16)
        lrow = sq_[:, 0:ST * P // 2].bitcast(BF16)
        gring = sb("gring", [R, C, 3, B // G0], BF16)
        take = taker()
        nat_i = sq_[:, 0:2 * B * P].bitcast(I32)
        nat_r = take(B * P).bitcast(BF16)
        nat_b = take(B * P).bitcast(BF16)
        col_i = take(2 * NT).bitcast(I32)
        rec2 = take(2 * NT).rearrange("p (t a) -> p t a", a=2)
        cb = take(2 * NT)
        cr = take(2 * NT)
        cf = take(2 * NT)
        ct = srt[:, :, :].rearrange("p s a -> p (s a)")[:, 0:2 * NT]
        wcol = take(NT)
        posi = take(NT).bitcast(I32)
        h0T = [take(HB * R)[:, 0:HB * R] for _ in range(2)]
        tb = take(3 * NB).bitcast(BF16).rearrange("p (a k) -> p a k", a=2)
        tf = take(2 * NB)
        brow = newb[0:1, 0:2 * NT // GT]
        mcnt = take(R)[0:2 * NB, 0:R]
        starts = take(NG)
        zb = take(NB).bitcast(BF16)[:, 0:2 * NB]
        fill_ = zacc[:, 0:SW * 3]
        lpart = zacc[:, 0:3 * NS // 2].bitcast(BF16).rearrange("p (t a k) -> p t a k", a=3, k=TURN)
        lrest = zacc[:, 3 * NS // 2:3 * NS // 2 + NS].rearrange("p (t k) -> p t k", k=TURN)
        fill = fill_.rearrange("p (s a) -> p s a", a=3)
        nat_f = fill_[:, 0:2 * B * P]
        cnt = take(NB + 1)
        laneoff = take(NB + 1)
        bst = take(6 * NB).rearrange("p (b k) -> p b k", k=6)
        bmv = take(2 * NB).rearrange("p (b k) -> p b k", k=2)
        brs = take(NB + 1)
        bnm = take(NB + 1)
        scans = [take(NT) for _ in range(2)]
        prods = [take(NT) for _ in range(2)]
        winb = sdst[:, 0:NT // GT].bitcast(F32)
        nat_t = srt[:, :, :].rearrange("p s a -> p (s a)")[:, 0:2 * B * P]
        msqs = [hs[:, :, :].rearrange("p a b -> p (a b)")[:, NT * k:NT * (k + 1)] for k in range(2)]
        sorting = at[0]
        masks = take((NB + 1) * NT // 2).bitcast(BF16).rearrange("p (k t) -> p k t", t=NT)
        at[0] = sorting
        recr = take(TURN * 3).rearrange("p (s a) -> p s a", a=3)
        posr = take(TURN).bitcast(I32)
        lk = take(B)
        oht = [take(256).bitcast(BF16) for _ in range(2)]
        vcp = [take(256).bitcast(BF16) for _ in range(2)]
        msk = [take(256).bitcast(BF16) for _ in range(2)]
        sqr = take(B * R).rearrange("p (k r) -> p k r", r=R)
        ohr = [take(B * R // 2).bitcast(BF16).rearrange("p (k r) -> p k r", r=R) for _ in range(C)]
        ohb = [take(B * 2 * NB // 2).bitcast(BF16).rearrange("p (k r) -> p k r", r=2 * NB) for _ in range(C)]
        take = taker()
        accT = [take(AW) for _ in range(2)]
        g1 = take(TURN * D).rearrange("p (c n) -> p c n", c=C)
        pre = take(TURN * D).rearrange("p (c n) -> p c n", c=C)
        eat = take(TURN * P).rearrange("p (c n) -> p c n", c=C)
        at[0] -= 3 * TURN * D
        big = take(3 * NB * D)
        ya, yb, yc = (big[0:R, NB * D * q_:NB * D * (q_ + 1)] for q_ in range(3))
        padrow = take(D)
        den = take(4 * NB)
        u3 = take(D)
        pout = [take(4 * D) for _ in range(3)]
        gbc = take(2 * D)
        cntT = take(N)[0:3, 0:N]
        st2 = take(6 * NB).rearrange("p (b k) -> p b k", k=6)
        mv2 = take(2 * NB).rearrange("p (b k) -> p b k", k=2)
        rs1 = take(NB + 1)
        nm1 = take(NB + 1)
        rs2 = take(NB + 1)
        nm2 = take(NB + 1)
        w2u = take(3 * D)
        xagain = take(NB * D)[0:R, :]
        oh1 = sq_[:, 0:TURN * WIN].rearrange("p (c n) -> p c n", c=C)
        h1T = hs[:, :, :].rearrange("p a b -> p (a b)")

        names = (
            "cst nati coli wcol x wl fill pat asteps dsteps "
            "stat root norm tpd tcp hp hcp hst wa wac "
            "blocks sqm mask laneoff lprod totals tiles ends first scan prod rank slots ready "
            "rowb ohtd blkb vald vcpd mskd sumd lks logd ohr ohb cntd r1 rr rfill turn spturn "
            "counted cntc cntp cntw win winw winr "
            "ones srtl sfar lpart ltr lrow idx sq sqd mtr lowd guards grd xd wd pvd fld zdone "
            "wl1 xa xm none hn root1 norm1 gam bet exps var2 dev2 root2 norm2 tp1 tc1 pp pca pcd cm u3d onesr "
            "ea addh msg ohd pso nextw pre q1 q2 qc hf out0 outd outs").split()
        s = {n: sem("s_" + n) for n in names}
        s_sc = [sem(f"s_sc{c}") for c in range(C)]
        s_g0 = [sem(f"s_g0_{c}") for c in range(C)]
        s_g1 = [sem(f"s_g1_{c}") for c in range(C)]
        s_pst = [sem(f"s_pst{k}") for k in range(3)]
        s_ld = [sem(f"s_ld{c}") for c in range(C)]
        block = ctx.enter_context(nc.Block())

        def tables(k, g):
            return 16 * ((k == 0) + sum(min(2, NB - 2 * q_) for q_ in range(g) if q_ % 3 == k))

        def table_out(eng, copy, q_):
            w = 2 * D * (min(2 * q_ + 2, NB) - 2 * q_)
            eng.wait_ge(s["pp"], q_ + 1)
            if q_ >= 3:
                eng.wait_ge(s_pst[q_ % 3], tables(q_ % 3, q_))
            else:
                eng.wait_ge(s["cm"], 1)
            copy(pout[q_ % 3][0:R, 0:w], bank[2 + q_ % 2][0:R, 0:w]).then_inc(s["pca" if q_ < NPA else "pcd"], 1)

        def table_is_out(eng, q_):
            if q_ < NPA:
                eng.wait_ge(s["pca"], q_ + 1)
            else:
                eng.wait_ge(s["pcd"], q_ + 1 - NPA)

        def c16(i, c):
            return C * i + c + 1

        @block.sync
        def _(sp):
            sp.dma_start(col_i[:, :], a["col"]).then_inc(s["coli"], 16)
            sp.dma_start(cst[:, :], a["cst"]).then_inc(s["cst"], 16)
            xv = a["x"].rearrange("(b r) d -> r b d", r=R)
            sp.dma_start(h0[:, :, :], xv).then_inc(s["x"], 16)
            sp.dma_start(nat_i[0:Q, :], a["nat"]).then_inc(s["nati"], 16)
            sp.dma_start(wt[:, 0:D], a["W"]).then_inc(s["wl"], 16)
            sp.dma_start(wt[:, D:2 * D], a["WT"]).then_inc(s["wl"], 16)
            sp.dma_start(wt[:, 2 * D:2 * D + 1], a["as"].rearrange("(p o) -> p o", o=1)).then_inc(s["wl"], 16)
            sp.dma_start(wt[:, 2 * D + 1:2 * D + 2], a["ad"].rearrange("(p o) -> p o", o=1)).then_inc(s["wl"], 16)
            sp.dma_start(wcol[:, :], a["w"]).then_inc(s["wcol"], 16)
            sp.wait_ge(s["pat"], 1)
            sp.dma_start(scr["rec"].rearrange("(p s) a -> p (s a)", p=P),
                         fill.rearrange("p s a -> p (s a)")).then_inc(s["fill"], 16)
            sp.wait_ge(s["win"], 1)
            sp.dma_start(scr["base"].rearrange("k (q c) -> q k c", q=Q),
                         small[0:Q, 0:4].rearrange("p (k c) -> p k c", k=2)).then_inc(s["winw"], 16)
            sp.wait_ge(s["winw"], 16)
            sp.dma_start(brow[0:1, :], scr["base"].rearrange("(o k) t -> o (k t)", o=1)).then_inc(s["winr"], 16)
            sp.dma_start(winb, scr["base"][0:1, :].to_broadcast([P, NT // GT])).then_inc(s["winr"], 16)
            sp.wait_ge(s["hcp"], (NB + HB - 1) // HB)
            sp.dma_start(scr["H"].rearrange("(b r) d -> r b d", r=R), hs[0:R, :, 0:D]).then_inc(s["hst"], 16)

            sp.wait_ge(s["cntp"], 1)
            sp.dma_start(scr["cnt"].rearrange("(k r) -> k r", r=R), mcnt).then_inc(s["cntw"], 16)
            for c in range(C):
                sp.wait_ge(s_sc[c], 16 * B * 2 * HT)
            sp.dma_start(srt[:, :, :].rearrange("p s a -> p (s a)"),
                         scr["rec"].rearrange("(p s) a -> p s a", p=P)[:, 0:NS, :].rearrange(
                             "p s a -> p (s a)")).then_inc(s["srtl"], 16)

            sp.wait_ge(s["sfar"], 1)

            def idx_round(o, first):
                for u in range(RT):
                    if not first:
                        for c in range(C):
                            sp.wait_ge(s_g0[c], o * (16 * B * RT) + 16 * B * (u + 1 - RT))
                            sp.sem_inc(s["spturn"], 1)
                    sp.dma_start(idxr[:, TURN * u:TURN * (u + 1)],
                                 sdst[:, bass.ds(o * RING + TURN * u, TURN)]).then_inc(s["idx"], 16)
                    sp.wait_ge(s["idx"], o * (16 * RT) + 16 * (u + 1))
                    sp.sem_inc(s["spturn"], 1)
            turns(sp, RO, idx_round)

            sp.wait_ge(s["zdone"], 1)

            def row(name):
                return a[name].rearrange("(o p) -> o p", o=1)

            def col(name):
                return a[name].rearrange("(p o) -> p o", o=1)

            sp.dma_start(xagain.rearrange("p (b d) -> p b d", d=D), xv).then_inc(s["xa"], 16)
            for dst, src in (
                (gbc[:, 0:D], row("gamma").to_broadcast([P, D])), (gbc[:, D:2 * D], row("beta").to_broadcast([P, D])),
                (wt[:, 0:D], a["W1f"][0:D, :]), (wt[:, D:2 * D], a["W1b"][0:D, :]),
                (wt[:, 2 * D:3 * D], a["W2fT"]), (wt[:, 3 * D:4 * D], a["W2bT"]), (wt[:, 4 * D:5 * D], a["Wu"]),
                (wt[1:EA + 1, 5 * D:6 * D], a["W1f"][D:D + EA, :]), (wt[1:EA + 1, 6 * D:7 * D], a["W1b"][D:D + EA, :]),
                (pout[0][0:REQ, 0:D], a["W1f"][D + EA:D + EA + REQ, :]),
                (pout[0][0:REQ, D:2 * D], a["W1b"][D + EA:D + EA + REQ, :]),
                (small[0:REQ, 0:1], a["req"].rearrange("o p -> p o")),
                (pout[1][0:1, 0:D], row("b1f")), (pout[1][0:1, D:2 * D], row("b1b")),
                (small[:, 1:2], col("b2f")), (small[:, 2:3], col("b2b")),
                (small[:, 3:4], row("eps").to_broadcast([P, 1])), (u3[2:3, :], row("bu")),
            ):
                sp.dma_start(dst, src).then_inc(s["wl1"], 16)
            sp.wait_ge(s["onesr"], 1)
            sp.wait_ge(s["cntw"], 16)
            sp.dma_start(cntT[0:2, :], scr["cnt"].rearrange("(h n) -> h n", h=2)).then_inc(s["wl1"], 16)
            pv = scr["PP"].rearrange("(h n) d -> n h d", h=2)
            sp.wait_ge(s["none"], 1)
            sp.dma_start(pv[N:N + 1, :, :], padrow[0:2, :]).then_inc(s_pst[0], 16)
            for g in range((NB + 1) // 2):
                table_is_out(sp, g)
                for b in range(2 * g, min(2 * g + 2, NB)):
                    o = 2 * D * (b % 2)
                    sp.dma_start(pv[R * b:R * (b + 1), :, :],
                                 pout[g % 3][0:R, o:o + 2 * D].rearrange("p (h d) -> p h d", h=2)
                                 ).then_inc(s_pst[g % 3], 16)

            passes = sp.value_load(npass[0:1, 0:1], min_val=1, max_val=NPASS)
            with sp.Fori(0, passes) as kp:
                for h in range(2):
                    def load_turn(i, first, h=h):
                        for c in range(C):
                            tt = kp * (2 * HT) + (h * HT + i)
                            t0 = i * TURN + (h * HALF + B * c)
                            if not first:
                                sp.wait_ge(s_g1[c], tt * (16 * B))
                                sp.sem_inc(s["spturn"], 1)
                                sp.wait_ge(s["ea"], tt * C + (c + 1 - C))
                                sp.sem_inc(s["spturn"], 1)
                            sp.dma_start(eat[0:EA + 1, c, :], a["eaT"][:, bass.ds(t0 * P, B * P)]).then_inc(s_ld[c], 16)
                            sp.dma_start(idxr[:, B * c:B * (c + 1)], srcg[:, bass.ds(t0, B)]).then_inc(s_ld[c], 16)
                    half_turns(sp, h, load_turn)
                sp.wait_ge(s["fld"], (kp + 1) * (2 * HT * TURN // GT) + NG)
                sp.sem_inc(s["spturn"], 1)
            ov = out.rearrange("(b r) d -> r b d", r=R)
            for g in range((NB + 3) // 4):
                b0, b1 = 4 * g, min(4 * g + 4, NB)
                sp.wait_ge(s["outd"], g + 1)
                sp.dma_start(ov[:, b0:b1, :], h0[:, b0:b1, :]).then_inc(s["outs"], 16)
            sp.wait_ge(s["outs"], 16 * ((NB + 3) // 4))

        @block.gpsimd
        def _(pool):
            for k in range(NB + 1):
                pool.wait_ge(s["scan"], k + 1)
                if k >= 2:
                    pool.wait_ge(s["rank"], k - 1)
                pool.tensor_tensor(prods[k % 2], masks[:, k, :], scans[k % 2], ALU.mult).then_inc(s["prod"], 1)
            pool.wait_ge(s["fill"], 16)

            def scatter_turn(i, first):
                for c in range(C):
                    if not first:
                        pool.wait_ge(s_sc[c], i * (16 * B))
                    pool.wait_ge(s["rfill"], c16(i, c))
                    pool.wait_ge(s["logd"], c16(i, c))
                    pool.sem_inc(s["turn"], 1)
                    for k in range(B * c, B * (c + 1)):
                        pool.indirect_dma_start(scr["rec"], bass.IndirectOffsetOnAxis(ap=posr[:, k:k + 1], axis=0),
                                                recr[:, k, :], None).then_inc(s_sc[c], 16)
            turns(pool, 2 * HT, scatter_turn)

            pool.wait_ge(s["hst"], 16)
            pool.wait_ge(s["ones"], 1)

            def gather_round(o, first):
                for u in range(RT):
                    pool.wait_ge(s["idx"], o * (16 * RT) + 16 * (u + 1))
                    for c in range(C):
                        if not (first and u == 0):
                            pool.wait_ge(s_g0[c], o * (16 * B * RT) + 16 * B * u)
                        if not first:
                            pool.wait_ge(s["pvd"], o * (RING // G0) + (TURN * u + B * (c + 1) - RING) // G0)
                        pool.sem_inc(s["turn"], 1)
                        for k in range(TURN * u + B * c, TURN * u + B * (c + 1)):
                            pool.indirect_dma_start(ring[:, k, 0:D], None, scr["H"],
                                                    bass.IndirectOffsetOnAxis(ap=idxr[:, k:k + 1], axis=0)
                                                    ).then_inc(s_g0[c], 16)
            turns(pool, RO, gather_round)

            pool.wait_ge(s["zdone"], 1)
            pool.wait_ge(s["none"], 1)

            def rest(k):
                bl = slice(CH * k, CH * (k + 1))
                y = yb[:, CH * D * k:CH * D * (k + 1)].rearrange("p (b d) -> p b d", d=D)
                no = den[0:R, CH * k:CH * (k + 1)].rearrange("p (b o) -> p b o", o=1).to_broadcast([R, CH, D])
                pool.tensor_tensor(y, hs[0:R, bl, 0:D], no, ALU.mult).then_inc(s["hn"], 1)
                pool.wait_ge(s["hn"], 2 * k + 1)
                pool.tensor_tensor(y, y, h0[:, bl, :], ALU.add).then_inc(s["hn"], 1)

            def plus_beta(k):
                y = ya[:, CH * D * k:CH * D * (k + 1)].rearrange("p (b d) -> p b d", d=D)
                be = gbc[0:R, D:2 * D].rearrange("p (o d) -> p o d", o=1).to_broadcast([R, CH, D])
                pool.wait_ge(s["gam"], k + 1)
                pool.tensor_tensor(y, y, be, ALU.add).then_inc(s["bet"], 1)

            for k in range(NB // CH):
                rest(k)
            pool.memset(cntT, 1.0).then_inc(s["onesr"], 1)
            for k in range(NB // CH):
                plus_beta(k)

            for k in range(3):
                pool.wait_ge(s_pst[k], tables(k, (NB + 1) // 2))
            passes = pool.value_load(npass[0:1, 0:1], min_val=1, max_val=NPASS)
            with pool.Fori(0, passes) as kp:
                for h in range(2):
                    def msg_turn(i, first, h=h):
                        tt = kp * (2 * HT) + (h * HT + i)
                        for c in range(C):
                            pool.wait_ge(s_ld[c], tt * 32 + 32)
                            if not first:
                                pool.wait_ge(s["addh"], (tt * C + (c + 1 - C)) * 2)
                            pool.sem_inc(s["turn"], 1)
                            for k in range(B):
                                pool.indirect_dma_start(g1[:, c, k * D:(k + 1) * D], None, scr["PP"],
                                                        bass.IndirectOffsetOnAxis(
                                                            ap=idxr[:, B * c + k:B * c + k + 1], axis=0)
                                                        ).then_inc(s_g1[c], 16)
                    half_turns(pool, h, msg_turn)
                pool.wait_ge(s["fld"], (kp + 1) * (2 * HT * TURN // GT) + NG)

        @block.scalar
        def _(act):
            n_step = [0]

            def link(ins):
                n_step[0] += 1
                ins.then_inc(s["asteps"], 1)
                act.wait_ge(s["asteps"], n_step[0])

            act.wait_ge(s["cst"], 16)
            for q_ in range(2):
                act.copy(identb[:, q_, :], ident[:, 0:R]).then_inc(s["asteps"], 1)
            act.copy(selb[:, :], ident).then_inc(s["asteps"], 1)
            act.activation(farb[:, :], ident, ACT.Copy, scale=FAR).then_inc(s["asteps"], 1)
            act.copy(sel3[:, :], cst[:, C_S3:C_W]).then_inc(s["asteps"], 1)
            n_step[0] = 5
            act.wait_ge(s["blocks"], 1)
            for k in range(NB + 1):
                if k >= 2:
                    act.wait_ge(s["mask"], k - 1)
                act.activation(msqs[k % 2], cb[:, 0:NT], ACT.Square, scale=-1.0,
                               bias=iota[:, k:k + 1]).then_inc(s["sqm"], 1)
                act.wait_ge(s["sqm"], k + 1)
                act.activation(masks[:, k, :], msqs[k % 2], ACT.Relu, scale=-1.0, bias=onesf[:, 0:1],
                               accum_out=cnt[:, k:k + 1]).then_inc(s["mask"], 1)
                if k == 10:
                    act.wait_ge(s["stat"], 1)
                    act.activation(brs[0:R, 0:NB], brs[0:R, 0:NB], ACT.Sqrt).then_inc(s["root"], 1)
                if k >= 14:
                    act.wait_ge(s["stat"], 2)
                    for b in range(min(NB, 3 * (k - 14)), min(NB, 3 * (k - 13))):
                        act.activation(h0[:, b, :], h0[:, b, :], ACT.Relu, scale=brs[0:R, b:b + 1],
                                       bias=bnm[0:R, b:b + 1]).then_inc(s["norm"], 1)
            act.wait_ge(s["mask"], NB + 1)

            def first_slots(k):
                if k == KD:
                    act.wait_ge(s["laneoff"], 1)
                act.wait_ge(s["rank"], k - KD + NB)
                act.activation(prods[(k - KD) % 2], masks[:, k, :], ACT.Copy,
                               scale=laneoff[:, k:k + 1]).then_inc(s["lprod"], 1)

            def h_out(g):
                b0, b1 = HB * g, min(HB * g + HB, NB)
                act.wait_ge(s["hp"], g + 1)
                act.copy(hs[0:R, b0:b1, :].rearrange("p b w -> p (b w)"),
                         bank[2 + g % 2][0:R, 0:HW * (b1 - b0)]).then_inc(s["hcp"], 1)

            ng = (NB + HB - 1) // HB
            for g in range(ng):
                b0, b1 = HB * g, min(HB * g + HB, NB)
                act.wait_ge(s["tpd"], g + 1)
                if g >= 2:
                    act.wait_ge(s["hp"], g - 1)
                act.copy(h0T[g % 2][:, 0:R * (b1 - b0)], bank[g % 2][:, 0:R * (b1 - b0)]).then_inc(s["tcp"], 1)
                if g:
                    h_out(g - 1)
                if 2 <= g < 2 + NB + 1 - KD:
                    first_slots(KD + g - 2)
            h_out(ng - 1)

            def fill_turn(i, first):
                for c in range(C):
                    t0 = i * TURN + B * c
                    if not first:
                        act.wait_ge(s_sc[c], i * (16 * B))
                    act.copy(recr[:, B * c:B * (c + 1), 0:2], rec2[:, bass.ds(t0, B), :]).then_inc(s["rr"], 1)
                    act.copy(posr[:, B * c:B * (c + 1)], posi[:, bass.ds(t0, B)]).then_inc(s["rr"], 1)
                    act.wait_ge(s["rr"], (C * i + c) * 2 + 2)
                    act.sem_inc(s["rfill"], 1)
                    for j in range(B // 2):
                        m = (B // 2) * c + j
                        pr = i * (TURN // 2) + m
                        act.wait_ge(s["vald"], pr + 1)
                        if not (first and m < 2):
                            act.wait_ge(s["mskd"], pr - 1)
                        act.copy(vcp[m % 2][0:3 * NB, :], bank[4 + m % 2][0:3 * NB, :]).then_inc(s["vcpd"], 1)
                        if j == 0 and not (first and c == 0):
                            act.wait_ge(s["ohr"], C * i + c)
                        for k in (2 * j, 2 * j + 1):
                            act.activation(sqr[:, k, :], iota[:, 0:R], ACT.Square, scale=-1.0,
                                           bias=cr[:, bass.ds(NT + t0 + k, 1)]).then_inc(s["r1"], 1)
                    act.wait_ge(s["r1"], i * TURN + B * (c + 1))
                    if not first:
                        act.wait_ge(s["cntd"], C * i + (c + 1 - C))
                    act.activation(ohr[c], sqr, ACT.Relu, scale=-1.0, bias=onesf[:, 0:1]).then_inc(s["ohr"], 1)
            act.wait_ge(s["ready"], 1)
            turns(act, 2 * HT, fill_turn)

            def distances(T, ks, n0):
                for k in ks:
                    act.activation(sqb[:, k, :], iota[:, 0:R], ACT.Square, scale=-1.0,
                                   bias=srt[:, bass.ds(T * TURN + k, 1), 0:1].rearrange("p a b -> p (a b)")
                                   ).then_inc(s["sq"], 1)

            act.wait_ge(s["sfar"], 1)

            def dist_turn(T, first):
                for c in range(C):
                    if not first:
                        act.wait_ge(s["mtr"], (C * T + c) * 2 + (2 - 2 * C))
                    distances(T, range(B * c, B * c + BA), 0)
            turns(act, ST, dist_turn)

            def weights(T, q_):
                act.wait_ge(s["xd"], T * (TURN // 4) + (q_ + 1))
                for k in range(4 * q_, 4 * q_ + 4):
                    act.activation(pen[:, k // B, k % B, :], bank[q_ % 3][:, R * (k % 4):R * (k % 4 + 1)], ACT.Exp,
                                   scale=-1.0, bias=srt[:, bass.ds(T * TURN + k, 1), 2:3].rearrange("p a b -> p (a b)")
                                   ).then_inc(s["wd"], 1)

            act.wait_ge(s["guards"], 1)

            def exp_turn(T, peeled):
                for q_ in range(TURN // 4):
                    if peeled:
                        act.wait_ge(s["xd"], T * (TURN // 4) + (q_ + 1 - TURN // 4))
                    distances(T, range(4 * q_, 4 * q_ + 4), NS)
                    if peeled == 0 and q_ == 0:
                        continue
                    if peeled > 1 or (peeled == 1 and q_):
                        act.wait_ge(s["pvd"], T * (TURN // G0) + (4 * q_ - TURN) // G0)
                    if q_:
                        weights(T, q_ - 1)
                    else:
                        weights(T - 1, TURN // 4 - 1)
            exp_turn(0, 0)
            exp_turn(1, 1)
            with act.Fori(2, ST) as T:
                exp_turn(T, 2)
            weights(ST - 1, TURN // 4 - 1)

            act.wait_ge(s["xa"], 16)

            def less_one(k):
                v = xagain[:, CH * D * k:CH * D * (k + 1)]
                act.activation(v, v, ACT.Copy, bias=-1.0).then_inc(s["xm"], 1)

            def norm1(k):
                for b in range(CH * k, CH * (k + 1)):
                    act.activation(ya[:, D * b:D * (b + 1)], ya[:, D * b:D * (b + 1)], ACT.Identity,
                                   scale=rs1[0:R, b:b + 1], bias=nm1[0:R, b:b + 1]).then_inc(s["norm1"], 1)

            def exps(k):
                act.wait_ge(s["bet"], k + 1)
                w = slice(CH * D * k, CH * D * (k + 1))
                act.activation(yb[:, w], ya[:, w], ACT.Exp).then_inc(s["exps"], 1)

            def norm2(k):
                act.wait_ge(s["root2"], 1 if k < 3 else 2)
                for b in range(CH * k, CH * (k + 1)):
                    act.activation(yc[:, D * b:D * (b + 1)], h0[:, b, :], ACT.Relu, scale=rs2[0:R, b:b + 1],
                                   bias=nm2[0:R, b:b + 1]).then_inc(s["norm2"], 1)

            ngh = (NB + 3) // 4

            def transposed(g):
                w = R * (min(4 * g + 4, NB) - 4 * g)
                act.wait_ge(s["tp1"], g + 1)
                act.copy(h1T[:, R * 4 * g:R * 4 * g + w], bank[g % 2][:, 0:w]).then_inc(s["tc1"], 1)

            def table(g):
                for q_ in range(2 * g, min(2 * g + 2, NPA)):
                    table_out(act, act.copy, q_)

            for k in range(NB // CH):
                less_one(k)
            act.wait_ge(s["root1"], 1)
            act.activation(rs1[0:R, 0:NB], rs1[0:R, 0:NB], ACT.Sqrt).then_inc(s["root1"], 1)
            act.wait_ge(s["root1"], 3)
            for k in range(NB // CH):
                norm1(k)
                if k >= 2:
                    exps(k - 2)
            exps(NB // CH - 2)
            exps(NB // CH - 1)
            g = 0
            for k in range(NB // CH):
                if k in (0, 2):
                    b = slice(0, 3 * CH) if k == 0 else slice(3 * CH, NB)
                    act.wait_ge(s["var2"], 3 if k == 0 else NB // CH)
                    act.activation(rs2[0:R, b], rs2[0:R, b], ACT.Sqrt).then_inc(s["dev2"], 1)
                norm2(k)
                while g < ngh and min(4 * g + 4, NB) <= CH * (k + 1):
                    transposed(g)
                    if g:
                        table(g - 1)
                    g += 1
            table(ngh - 1)
            for g in range(ngh):
                w = D * (min(4 * g + 4, NB) - 4 * g)
                act.wait_ge(s["q1"], g + 1)
                act.copy(xagain[:, 4 * D * g:4 * D * g + w], bank[4 + g % 2][0:R, 0:w]).then_inc(s["q2"], 1)
            passes = act.value_load(npass[0:1, 0:1], min_val=1, max_val=NPASS)
            with act.Fori(0, passes) as kp:
                for h in range(2):
                    def relu_turn(i, first, h=h):
                        tt = kp * (2 * HT) + (h * HT + i)
                        for c in range(C):
                            act.wait_ge(s["addh"], (tt * C + (c + 1)) * 2)
                            act.activation(pre[:, c, :], pre[:, c, :], ACT.Relu).then_inc(s["msg"], 1)
                    half_turns(act, h, relu_turn)

        @block.tensor
        def _(pe):
            pe.wait_ge(s["cst"], 16)
            pe.wait_ge(s["wl"], 64)
            pe.matmul(bank[2][:, 0:2], wt[:, 0:D], wt[:, 2 * D:2 * D + 2], start=True, stop=True).then_inc(s["wa"], 1)
            def rank_add(j, start, last):
                for q_ in range(2):
                    mm = pe.matmul(bank[4 + q_][:, 0:HALF], ident, prods[j % 2][:, HALF * q_:HALF * (q_ + 1)],
                                   start=start, stop=last)
                mm.then_inc(s["rank"], 1)

            for k in range(NB + 1):
                pe.wait_ge(s["prod"], k + 1)
                rank_add(k, k == 0, False)
            pe.wait_ge(s["mask"], NB + 1)
            pe.matmul(bank[6][0:NB + 1, 0:1], cnt, onesf[:, 0:1], start=True, stop=True).then_inc(s["totals"], 1)
            pe.wait_ge(s["tiles"], 1)
            pe.matmul(bank[7][:, 0:NB + 1], small[0:NB + 1, 34:35].to_broadcast([NB + 1, P]), tri[0:NB + 1, 0:NB + 1],
                      start=True, stop=False)
            pe.matmul(bank[7][:, 0:NB + 1], tri, cnt, start=False, stop=True).then_inc(s["first"], 1)
            pe.matmul(bank[6][0:NB + 1, 1:2], inc[0:NB + 1, :], small[0:NB + 1, 32:33],
                      start=True, stop=True).then_inc(s["ends"], 1)
            pe.wait_ge(s["wac"], 1)
            ng = (NB + HB - 1) // HB

            def h_rows(g):
                b0, b1 = HB * g, min(HB * g + HB, NB)
                pe.wait_ge(s["tcp"], g + 1)
                if g >= 2:
                    pe.wait_ge(s["hcp"], g - 1)
                for b in range(b0, b1):
                    mm = pe.matmul(bank[2 + g % 2][0:R, HW * (b - b0):HW * (b - b0 + 1)],
                                   h0T[g % 2][:, R * (b - b0):R * (b - b0 + 1)], wt[:, D:2 * D + 2],
                                   start=True, stop=True)
                mm.then_inc(s["hp"], 1)

            for k in range(ng + 1):
                if k < ng:
                    b0, b1 = HB * k, min(HB * k + HB, NB)
                    pe.wait_ge(s["norm"], b1)
                    if k >= 2:
                        pe.wait_ge(s["tcp"], k - 1)
                    for b in range(b0, b1):
                        mm = pe.transpose(bank[k % 2][:, R * (b - b0):R * (b - b0 + 1)], h0[:, b, :], ident[0:R, 0:R])
                    mm.then_inc(s["tpd"], 1)
                if k >= 1:
                    h_rows(k - 1)
                if 2 <= k < 2 + NB + 1 - KD:
                    pe.wait_ge(s["lprod"], k - 1)
                    rank_add(k - 2, False, k - 2 + KD == NB)
            pe.wait_ge(s["slots"], 1)
            pe.matmul(bank[7][0:R, 0:NG], onesf[0:NB, 0:R], starts[0:NB, :], start=True, stop=True).then_inc(s["slots"], 1)

            pe.wait_ge(s["ready"], 1)
            counts = bank[7][0:R, 0:2 * NB]
            pe.matmul(counts, identb[:, 0, :], zb, start=True, stop=False)

            def spread(i, m, what, where, rows, name):
                c, j = m // (B // 2), m % (B // 2)
                sel = selb[0:Q, bass.ds(C * i + c, 1)]
                for a_ in range(2):
                    o = a_ * B * P + 256 * j
                    mm = pe.matmul(bank[where + m % 2][0:rows, 256 * a_:256 * (a_ + 1)], sel.to_broadcast([Q, rows]),
                                   what[0:Q, o:o + 256], start=True, stop=True)
                mm.then_inc(s[name], 1)

            def sums(i, m):
                for u in range(2):
                    col = bank[6][:, 2 * m + u:2 * m + u + 1]
                    for a_ in range(2):
                        mm = pe.matmul(col, msk[m % 2][0:3 * NB, 256 * a_ + P * u:256 * a_ + P * (u + 1)],
                                       onesb[0:3 * NB, 0:1], start=(a_ == 0), stop=(a_ == 1))
                if m % (B // 2) == B // 2 - 1:
                    mm.then_inc(s["sumd"], 1)

            spread(0, 0, nat_r, 0, P, "rowb")
            spread(0, 0, nat_b, 2, 3 * NB, "blkb")

            def logit_turn(i, first):
                for m in range(TURN // 2):
                    c, j = m // (B // 2), m % (B // 2)
                    pr = i * (TURN // 2) + m
                    nxt = (i, m + 1) if m + 1 < TURN // 2 else (i + 1, 0)
                    if not (first and m == 0):
                        pe.wait_ge(s["ohtd"], pr)
                    spread(*nxt, nat_r, 0, P, "rowb")
                    pe.wait_ge(s["ohtd"], pr + 1)
                    if not (first and m < 2):
                        pe.wait_ge(s["vcpd"], pr - 1)
                    for a_ in range(2):
                        mm = pe.matmul(bank[4 + m % 2][0:3 * NB, 256 * a_:256 * (a_ + 1)], tb[0:R, a_, 0:3 * NB],
                                       oht[m % 2][0:R, 256 * a_:256 * (a_ + 1)], start=True, stop=True)
                    mm.then_inc(s["vald"], 1)
                    if j == 1 and not (first and c == 0):
                        cb_ = (c - 1) % C
                        pe.wait_ge(s["ohr"], C * i + c)
                        pe.wait_ge(s["ohb"], C * i + c)
                        for k in range(B):
                            mm = pe.matmul(counts, ohr[cb_][:, k, :], ohb[cb_][:, k, :], start=False, stop=False)
                        mm.then_inc(s["cntd"], 1)
                    if not (first and m == 0):
                        pe.wait_ge(s["mskd"], pr)
                        if j == 1 and not (first and c == 0):
                            pe.wait_ge(s["logd"], C * i + c)
                        sums(*((i, m - 1) if m else (i - 1, TURN // 2 - 1)))
                    spread(*nxt, nat_b, 2, 3 * NB, "blkb")
            turns(pe, 2 * HT, logit_turn)
            pe.wait_ge(s["mskd"], HT * TURN)
            sums(2 * HT - 1, TURN // 2 - 1)
            pe.wait_ge(s["ohr"], 2 * HT * C)
            pe.wait_ge(s["ohb"], 2 * HT * C)
            for k in range(B):
                mm = pe.matmul(counts, ohr[C - 1][:, k, :], ohb[C - 1][:, k, :], start=False, stop=(k == B - 1))
            mm.then_inc(s["counted"], 1)
            pe.wait_ge(s["cntc"], 1)
            pe.wait_ge(s["logd"], 2 * HT * C)
            pe.transpose(bank[6][0:2 * NB, 128:128 + R], small[0:R, 64:64 + 2 * NB], ident[0:R, 0:R]
                         ).then_inc(s["cntc"], 1)

            for g in range(ST // 4):
                pe.wait_ge(s["lpart"], 1)
                if g >= 6:
                    pe.wait_ge(s["lrow"], g - 5)
                for u in range(4):
                    mm = pe.matmul(bank[g % 6][0:3 * TURN, P * u:P * (u + 1)],
                                   lpart[:, 4 * g + u, :, :].rearrange("p a k -> p (a k)"), selb[:, :],
                                   start=True, stop=True)
                mm.then_inc(s["ltr"], 1)
            pe.wait_ge(s["lrow"], ST // 4)

            def low_turn(T, first):
                for c in range(C):
                    pe.wait_ge(s["sq"], T * (C * BA) + BA * (c + 1))
                    pe.wait_ge(s["sqd"], C * T + (c + 1))
                    for k in range(B):
                        if k % 4 == 0 and not first:
                            pe.wait_ge(s["lowd"], (C * T + c) * 2 + (k // 4 + 1 - 2 * C))
                        o = bank[2 * c + k // 4][0:R, P * (k % 4):P * (k % 4 + 1)]
                        n_ = B * c + k
                        pe.matmul(o, sqb[:, n_, :], farb[:, :], start=True, stop=False)
                        mm = pe.matmul(o, sel3[0:3 * TURN, n_:n_ + 1].to_broadcast([3 * TURN, R]),
                                       lrow[0:3 * TURN, bass.ds(T * P, P)], start=False, stop=True)
                        if k % 4 == 3:
                            mm.then_inc(s["mtr"], 1)
            pe.wait_ge(s["cntp"], 1)
            turns(pe, ST, low_turn)
            pe.wait_ge(s["guards"], 1)

            def exponents(T, q_, first):
                bk = bank[q_ % 3]
                pe.wait_ge(s["sq"], T * TURN + (NS * BA // B + 4 * q_ + 4))
                if q_ % 2 == 0:
                    pe.wait_ge(s["grd"], C * T + (q_ // 2 + 1))
                if not (first and q_ < 3):
                    pe.wait_ge(s["wd"], T * TURN + (4 * q_ - 8))
                pe.matmul(bk[:, 0:4 * R], farb[:, :], sqb[:, 4 * q_:4 * q_ + 4, :].rearrange("p k r -> p (k r)"),
                          start=True, stop=False)
                for g in range(2):
                    for p_ in range(3):
                        n_ = 2 * (q_ % 2) + g
                        mm = pe.matmul(bk[:, 2 * R * g:2 * R * (g + 1)],
                                       gring[:, q_ // 2, p_, n_:n_ + 1].to_broadcast([R, P]),
                                       identb[0:R, :, :].rearrange("p a r -> p (a r)"),
                                       start=False, stop=(p_ == 2 and g == 1))
                mm.then_inc(s["xd"], 1)

            def products(T, q_, first, u):
                for k in range(4 * q_, 4 * q_ + 4):
                    if k % B == 0:
                        pe.wait_ge(s_g0[k // B], T * (16 * B) + 16 * B)
                    pe.wait_ge(s["wd"], T * TURN + (k + 1))
                    g = k // G0
                    if k % G0 == 0 and not (first and g < 4):
                        pe.wait_ge(s["fld"], T * (TURN // G0) + (g - 3))
                    mm = pe.matmul(bank[3 + g % 4][0:R, 0:GW], pen[:, k // B, k % B, :],
                                   ring[:, bass.ds(u * TURN + k, 1), :].rearrange("p a w -> p (a w)"),
                                   start=(k % G0 == 0), stop=(k % G0 == G0 - 1))
                    if k % G0 == G0 - 1:
                        mm.then_inc(s["pvd"], 1)

            def sum_turn(T, first, u, Tp, up, second=False):
                for q_ in range(TURN // 4):
                    exponents(T, q_, first)
                    if q_:
                        products(T, q_ - 1, first, u)
                    elif not first:
                        products(Tp, TURN // 4 - 1, False, up)
            last = TURN // 4 - 1
            sum_turn(0, True, 0, 0, 0)
            with pe.Fori(1, RT) as u:
                sum_turn(u, False, u, u - 1, u - 1)
            with pe.Fori(1, RO) as o:
                sum_turn(o * RT, False, 0, o * RT - 1, RT - 1)
                with pe.Fori(1, RT) as u:
                    sum_turn(o * RT + u, False, u, o * RT + (u - 1), u - 1)
            products(ST - 1, last, False, RT - 1)

            pe.wait_ge(s["wl1"], 16 * 19)
            pe.wait_ge(s["fld"], NG)
            pe.matmul(bank[6][0:1, 0:2 * D], small[0:REQ, 0:1], pout[0][0:REQ, 0:2 * D], start=True, stop=False)
            pe.matmul(bank[6][0:1, 0:2 * D], onesf[0:1, 0:1], pout[1][0:1, 0:2 * D], start=False, stop=True)
            pe.matmul(bank[7][:, 0:D], wt[:, 2 * D:3 * D], wt[:, 4 * D:5 * D], start=True, stop=True)
            pe.matmul(bank[7][:, D:2 * D], wt[:, 3 * D:4 * D], wt[:, 4 * D:5 * D], start=True, stop=True)
            pe.matmul(bank[7][0:2, 2 * D:3 * D], small[:, 1:3], wt[:, 4 * D:5 * D], start=True, stop=True
                      ).then_inc(s["cm"], 1)
            ngh = (NB + 3) // 4
            for g in range(ngh):
                b0, b1 = 4 * g, min(4 * g + 4, NB)
                pe.wait_ge(s["norm2"], b1)
                for b in range(b0, b1):
                    mm = pe.transpose(bank[g % 2][:, R * (b - b0):R * (b - b0 + 1)], yc[:, D * b:D * (b + 1)],
                                      ident[0:R, 0:R])
                mm.then_inc(s["tp1"], 1)
                pe.wait_ge(s["tc1"], g + 1)
                for b in range(b0, b1):
                    if b % 2 == 0 and b >= 4:
                        table_is_out(pe, b // 2 - 2)
                    mm = pe.matmul(bank[2 + b // 2 % 2][0:R, 2 * D * (b % 2):2 * D * (b % 2 + 1)],
                                   h1T[:, R * b:R * (b + 1)], wt[:, 0:2 * D], start=True, stop=True)
                    if b % 2 == 1 or b == NB - 1:
                        mm.then_inc(s["pp"], 1)
            pe.wait_ge(s["u3d"], 1)
            for b in range(NB):
                g = b // 4
                if b % 4 == 0 and g >= 2:
                    pe.wait_ge(s["q2"], g - 1)
                o = bank[4 + g % 2][0:R, D * (b % 4):D * (b % 4 + 1)]
                pe.matmul(o, h1T[:, R * b:R * (b + 1)], w2u[:, 2 * D:3 * D], start=True, stop=False)
                mm = pe.matmul(o, cntT[:, R * b:R * (b + 1)], u3[0:3, 0:D], start=False, stop=True)
                if b % 4 == 3 or b == NB - 1:
                    mm.then_inc(s["q1"], 1)
            table_is_out(pe, NPA - 1)
            table_is_out(pe, (NB + 1) // 2 - 1)
            pe.wait_ge(s["q2"], ngh)

            passes = pe.value_load(npass[0:1, 0:1], min_val=1, max_val=NPASS)
            with pe.Fori(0, passes) as kp:
                for h in range(2):
                    def seg(nb, c, skip):
                        pe.wait_ge(s["msg"], nb + 1)
                        pe.wait_ge(s["ohd"], nb + 1)
                        for k in range(B):
                            if k % GT == 0 and not skip:
                                pe.wait_ge(s["fld"], nb * 2 + (NG + k // GT - 1))
                            mm = pe.matmul(bank[6 + k // GT][:, 0:WIN], pre[:, c, k * D:(k + 1) * D],
                                           oh1[:, c, k * WIN:(k + 1) * WIN], start=(k % GT == 0), stop=(k % GT == GT - 1))
                            if k % GT == GT - 1:
                                mm.then_inc(s["pso"], 1)

                    def msg_turn(i, first, h=h):
                        tt = kp * (2 * HT) + (h * HT + i)
                        for c in range(C):
                            nb = tt * C + c
                            pe.wait_ge(s_ld[c], tt * 32 + 32)
                            if not first:
                                pe.wait_ge(s["addh"], nb * 2 + (2 - 2 * C))
                            for k in range(B):
                                mm = pe.matmul(bank[2 * c + k // 4][:, P * (k % 4):P * (k % 4 + 1)],
                                               eat[0:EA + 1, c, k * P:(k + 1) * P],
                                               wt[0:EA + 1, (5 + h) * D:(6 + h) * D], start=True, stop=True)
                            mm.then_inc(s["ea"], 1)
                            if not (first and c == 0):
                                seg(nb - 1, (c - 1) % C, first and c == 1)
                    half_turns(pe, h, msg_turn)
                seg(kp * (2 * HT * C) + (2 * HT * C - 1), C - 1, False)
                pe.wait_ge(s["fld"], (kp + 1) * (2 * HT * TURN // GT) + NG)

            for b in range(NB):
                g = b // 4
                if b % 4 == 0 and g >= 3:
                    pe.wait_ge(s["hf"], g - 2)
                o = bank[g % 3][0:R, D * (b % 4):D * (b % 4 + 1)]
                pe.matmul(o, accT[0][:, R * b:R * (b + 1)], w2u[:, 0:D], start=True, stop=False)
                mm = pe.matmul(o, accT[1][:, R * b:R * (b + 1)], w2u[:, D:2 * D], start=False, stop=True)
                if b % 4 == 3 or b == NB - 1:
                    mm.then_inc(s["out0"], 1)

        @block.vector
        def _(dve):
            n_step = [0]

            def link(ins):
                n_step[0] += 1
                ins.then_inc(s["dsteps"], 1)
                dve.wait_ge(s["dsteps"], n_step[0])

            def signal(name, ins):
                link(ins)
                dve.sem_inc(s[name], 1)

            def divmod_r(v, t, b, r, between=lambda n: None):
                link(dve.tensor_scalar(t, v, 0.5, 1.0 / R, ALU.add, ALU.mult))
                between(1)
                link(dve.tensor_scalar(t, t, -0.5, MAGIC, ALU.add, ALU.add))
                between(1)
                link(dve.tensor_scalar(b, t, -MAGIC, None, ALU.add))
                between(1)
                link(dve.scalar_tensor_tensor(r, b, -float(R), v, ALU.mult, ALU.add))

            def floor_div(v, t, by):
                link(dve.tensor_scalar(t, v, 1.0 / by, -(by - 1) / (2.0 * by), ALU.mult, ALU.add))
                link(dve.tensor_scalar(t, t, MAGIC, -MAGIC, ALU.add, ALU.add))

            src, dst = slice(0, NT), slice(NT, 2 * NT)
            dve.wait_ge(s["coli"], 16)
            dve.memset(onesf[:, :], 1.0).then_inc(s["dsteps"], 1)
            n_step[0] += 1
            link(dve.tensor_copy(cf[:, src], col_i[:, src]))
            divmod_r(cf[:, src], ct[:, src], cb[:, src], cr[:, src])
            dve.sem_inc(s["blocks"], 1)
            n_scan = [0]

            def scan(n):
                for k in range(n_scan[0], min(n_scan[0] + n, NB + 1)):
                    dve.wait_ge(s["mask"], k + 1)
                    if k >= 2:
                        dve.wait_ge(s["prod"], k - 1)
                    dve.tensor_tensor_scan(scans[k % 2], masks[:, k, :], masks[:, k, :], 0.0,
                                           ALU.add, ALU.max).then_inc(s["scan"], 1)
                n_scan[0] += n

            link(dve.memset(fill[:, :, 0:1], -1.0))
            signal("pat", dve.memset(fill[:, :, 1:3], 0.0))
            link(dve.memset(onesb[:, :], 1.0))
            link(dve.memset(zb, 0.0))
            dve.wait_ge(s["x"], 16)
            scan(1)
            for b in range(NB):
                if b % 5 == 4:
                    scan(1)
                dve.bn_stats(bst[0:R, b, :], h0[:, b, :]).then_inc(s["dsteps"], 1)
            n_step[0] += NB
            dve.wait_ge(s["dsteps"], n_step[0])
            for b in range(NB):
                dve.bn_aggr(bmv[0:R, b, :], bst[0:R, b, :]).then_inc(s["dsteps"], 1)
            n_step[0] += NB
            dve.wait_ge(s["dsteps"], n_step[0])
            signal("stat", dve.tensor_scalar(brs[0:R, 0:NB], bmv[0:R, :, 1], EPS, None, ALU.add))
            dve.wait_ge(s["wa"], 1)
            signal("wac", dve.tensor_copy(wt[:, 2 * D:2 * D + 2], bank[2][:, 0:2]))
            scan(1)
            link(dve.tensor_copy(cf[:, dst], col_i[:, dst]))
            scan(1)
            divmod_r(cf[:, dst], ct[:, dst], cb[:, dst], cr[:, dst])
            scan(2)
            link(dve.tensor_copy(rec2[:, :, 0], cr[:, src]))
            link(dve.tensor_copy(rec2[:, :, 1], cf[:, dst]))
            scan(1)
            link(dve.tensor_scalar(ct[:, src], cb[:, src], float(NB), 1000.0, ALU.is_equal, ALU.mult))
            link(dve.tensor_tensor(cb[:, dst], cb[:, dst], ct[:, src], ALU.add))
            hb = cb[:, NT + HALF:2 * NT]
            link(dve.tensor_scalar(hb, hb, float(NB), None, ALU.add))
            link(dve.tensor_copy(srcg[:, 0:HALF], col_i[:, 0:HALF]))
            link(dve.tensor_scalar(srcg[:, HALF:NT], col_i[:, HALF:NT], float(TN), None, ALU.add))
            scan(2)
            dve.wait_ge(s["root"], 1)
            link(dve.reciprocal(brs[0:R, 0:NB], brs[0:R, 0:NB]))
            signal("stat", dve.scalar_tensor_tensor(bnm[0:R, 0:NB], bmv[0:R, :, 0], -1.0, brs[0:R, 0:NB],
                                                    ALU.mult, ALU.mult))
            dve.wait_ge(s["nati"], 16)
            dve.wait_ge(s["fill"], 16)
            link(dve.tensor_copy(nat_f[0:Q, :], nat_i[0:Q, :]))
            scan(1)
            divmod_r(nat_f[0:Q, :], nat_t[0:Q, :], nat_b[0:Q, :], nat_r[0:Q, :], scan)
            scan(1)
            dn = nat_f[0:Q, B * P:2 * B * P].rearrange("p (c e) -> p c e", c=B // GT)
            link(dve.tensor_reduce(small[0:Q, 0:2], dn, AX.X, ALU.min))
            link(dve.tensor_reduce(small[0:Q, 2:4], dn, AX.X, ALU.max))
            scan(NB + 1)
            signal("win", dve.tensor_tensor(small[0:Q, 2:4], small[0:Q, 2:4], small[0:Q, 0:2], ALU.subtract))
            dve.wait_ge(s["totals"], 1)
            tl, te, t0_ = (small[0:NB + 1, k:k + 1] for k in (32, 33, 35))
            link(dve.tensor_scalar(t0_, bank[6][0:NB + 1, 0:1], float(G0 * P - 1), None, ALU.add))
            floor_div(t0_, tl, float(G0 * P))
            signal("tiles", dve.tensor_scalar(small[0:NB + 1, 34:35], tl, float(G0 * P), None, ALU.mult))
            dve.wait_ge(s["first"], 1)
            link(dve.tensor_copy(laneoff[:, :], bank[7][:, 0:NB + 1]))
            dve.sem_inc(s["laneoff"], 1)
            link(dve.tensor_scalar(scans[1], masks[:, 0, :], laneoff[:, 0:1], None, ALU.mult))
            for k in range(1, KD):
                link(dve.scalar_tensor_tensor(scans[1], masks[:, k, :], laneoff[:, k:k + 1], scans[1],
                                              ALU.mult, ALU.add))
            dve.wait_ge(s["ends"], 1)
            link(dve.tensor_copy(te, bank[6][0:NB + 1, 1:2]))
            signal("slots", dve.tensor_scalar(starts[0:NB, :], iota[0:NB, 0:NG], te[0:NB, :], None, ALU.is_ge))
            dve.wait_ge(s["hcp"], (NB + HB - 1) // HB)
            t3 = tf[0:R, :].rearrange("p (a k) -> p a k", a=2)
            link(dve.tensor_copy(t3, hs[0:R, :, D:HW].rearrange("p b a -> p a b")))
            for p_ in range(3):
                part = tb[0:R, :, NB * p_:NB * (p_ + 1)]
                link(dve.tensor_copy(part, t3))
                if p_ < 2:
                    link(dve.tensor_tensor(t3, t3, part, ALU.subtract))
            dve.wait_ge(s["rank"], NB + 1 + NB + 1 - KD)
            for q_ in range(2):
                w = slice(HALF * q_, HALF * (q_ + 1))
                link(dve.scalar_tensor_tensor(scans[0][:, w], bank[4 + q_][:, 0:HALF], -1.0, scans[1][:, w],
                                              ALU.add, ALU.add))
            floor_div(scans[0], scans[1], float(P))
            link(dve.scalar_tensor_tensor(scans[0], scans[1], -float(P), scans[0], ALU.mult, ALU.add))
            link(dve.scalar_tensor_tensor(posi[:, :], scans[0], float(SW), scans[1], ALU.mult, ALU.add))
            dve.wait_ge(s["wcol"], 16)
            dve.wait_ge(s["slots"], 2)
            link(dve.tensor_scalar(offs[0:1, :], bank[7][0:1, 0:NG], float(GW), None, ALU.mult))
            link(dve.tensor_copy(low[:, 0, :], bank[7][0:R, 0:NG]))
            dve.sem_inc(s["ready"], 1)

            def logits(i, c, first):
                dve.wait_ge(s["sumd"], c16(i, c))
                if not first:
                    dve.wait_ge(s_sc[c], i * (16 * B))
                ps = bank[6][:, B * c:B * (c + 1)]
                dve.tensor_scalar(lk, ps, SLOPE, None, ALU.mult).then_inc(s["lks"], 1)
                dve.wait_ge(s["lks"], (C * i + c) * 2 + 1)
                dve.tensor_tensor(lk, ps, lk, ALU.max).then_inc(s["lks"], 1)
                dve.wait_ge(s["lks"], (C * i + c) * 2 + 2)
                dve.tensor_tensor(recr[:, B * c:B * (c + 1), 2], lk, wcol[:, bass.ds(i * TURN + B * c, B)],
                                  ALU.mult).then_inc(s["logd"], 1)

            def own_block(i, m):
                pr = i * (TURN // 2) + m
                dve.wait_ge(s["blkb"], pr + 1)
                dve.wait_ge(s["vcpd"], pr + 1)
                dve.scalar_tensor_tensor(msk[m % 2][0:3 * NB, :], bank[2 + m % 2][0:3 * NB, :],
                                         iota_pb[0:3 * NB, :], vcp[m % 2][0:3 * NB, :],
                                         ALU.is_equal, ALU.mult).then_inc(s["mskd"], 1)

            def logit_turn(i, first, second=False):
                for m in range(TURN // 2):
                    c, j = m // (B // 2), m % (B // 2)
                    pr = i * (TURN // 2) + m
                    t0 = i * TURN + B * c
                    dve.wait_ge(s["rowb"], pr + 1)
                    if not (first and m < 2):
                        dve.wait_ge(s["vald"], pr - 1)
                    dve.tensor_scalar(oht[m % 2][0:R, :], bank[m % 2][0:R, :], iota_p[0:R, :], None,
                                      ALU.is_equal).then_inc(s["ohtd"], 1)
                    if j == 2:
                        if not first:
                            dve.wait_ge(s["cntd"], C * i + (c + 1 - C))
                        dve.tensor_tensor(
                            ohb[c], iota[:, 0:2 * NB].rearrange("p (o k) -> p o k", o=1).to_broadcast([P, B, 2 * NB]),
                            cb[:, bass.ds(NT + t0, B)].rearrange("p (b o) -> p b o", o=1).to_broadcast([P, B, 2 * NB]),
                            ALU.is_equal).then_inc(s["ohb"], 1)
                    if m:
                        own_block(i, m - 1)
                    elif not first:
                        own_block(i - 1, TURN // 2 - 1)
                    if j == 1 and c:
                        logits(i, c - 1, first)
                    elif j == 1 and not first:
                        logits(i - 1, C - 1, second)
            logit_turn(0, True)
            logit_turn(1, False, True)
            with dve.Fori(2, 2 * HT) as i:
                logit_turn(i, False)
            own_block(2 * HT - 1, TURN // 2 - 1)
            logits(2 * HT - 1, C - 1, False)

            dve.wait_ge(s["counted"], 1)
            signal("cntc", dve.tensor_copy(small[0:R, 64:64 + 2 * NB], bank[7][0:R, 0:2 * NB]))
            dve.wait_ge(s["cntc"], 2)
            signal("cntp", dve.tensor_copy(mcnt, bank[6][0:2 * NB, 128:128 + R]))
            dve.wait_ge(s["winr"], 32)
            link(dve.tensor_tensor(rel[:, :].rearrange("p (g k) -> p g k", k=GT),
                                   cf[:, dst].rearrange("p (g k) -> p g k", k=GT),
                                   winb.rearrange("p (g o) -> p g o", o=1).to_broadcast([P, NT // GT, GT]),
                                   ALU.subtract))
            link(dve.tensor_copy(base[:, :], brow[0:1, 0:NT // GT]))
            sp_, sq1 = small[0:1, 40:41], small[0:1, 41:42]
            link(dve.tensor_reduce(sp_, brow[0:1, NT // GT:2 * NT // GT], AX.X, ALU.max))
            floor_div(sp_, sq1, float(WIN))
            link(dve.tensor_scalar(npass[:, :], sq1, 1.0, None, ALU.add))
            link(dve.tensor_tensor(newb[:, 1:NG], low[:, 0, 1:NG], low[:, 0, 0:NG - 1], ALU.not_equal))
            link(dve.tensor_scalar(newb[:, 1:NG], newb[:, 1:NG], 6e38 / 2, -1.5e38, ALU.mult, ALU.add))
            link(dve.memset(newb[:, 0:1], 1.5e38))
            link(dve.memset(newb[:, NG:NG + 1], 1.5e38))
            dve.wait_ge(s["rfill"], 2 * HT * C)
            dve.wait_ge(s["cntw"], 16)
            for c in range(C):
                dve.wait_ge(s_sc[c], 16 * B * 2 * HT)
            signal("ones", dve.memset(ring[:, :, D:GW], 1.0))
            dve.wait_ge(s["srtl"], 16)
            signal("sfar", dve.tensor_copy(sdst[:, :], srt[:, :, 1]))
            lg = srt[:, :, 2].rearrange("p (t k) -> p t k", k=TURN)
            link(dve.tensor_scalar(lpart[:, :, 0, :], lg, -1.0, None, ALU.mult))
            link(dve.scalar_tensor_tensor(lrest, lg, -1.0, lpart[:, :, 0, :], ALU.mult, ALU.subtract))
            link(dve.tensor_copy(lpart[:, :, 1, :], lrest))
            signal("lpart", dve.tensor_tensor(lpart[:, :, 2, :], lrest, lpart[:, :, 1, :], ALU.subtract))
            for g in range(ST // 4):
                dve.wait_ge(s["ltr"], g + 1)
                dve.tensor_copy(lrow[0:3 * TURN, 4 * P * g:4 * P * (g + 1)],
                                bank[g % 6][0:3 * TURN, :]).then_inc(s["lrow"], 1)
            link(dve.memset(zacc[:, :], 0.0))

            def lowest(T, c):
                for q_ in range(2):
                    dve.wait_ge(s["mtr"], (C * T + c) * 2 + (q_ + 1))
                    dve.tensor_reduce(low[:, 0, bass.ds(T * (TURN // G0) + (B * c // G0 + 2 * q_), 2)],
                                      bank[2 * c + q_][0:R, :].rearrange("p (g e) -> p g e", g=2), AX.X,
                                      ALU.min).then_inc(s["lowd"], 1)

            def low_turn(T, first):
                for c in range(C):
                    if not first:
                        dve.wait_ge(s["mtr"], (C * T + c) * 2 + (2 - 2 * C))
                    for k in range(B * c + BA, B * (c + 1)):
                        row = srt[:, bass.ds(T * TURN + k, 1), 0:1].to_broadcast([P, 1, R])
                        dve.tensor_tensor(sqb[:, k:k + 1, :], iota[:, 0:R].rearrange("p (o r) -> p o r", o=1), row,
                                          ALU.not_equal).then_inc(s["sqd"], 1)
                    if c:
                        lowest(T, c - 1)
                    elif not first:
                        lowest(T - 1, C - 1)
            turns(dve, ST, low_turn)
            lowest(ST - 1, C - 1)
            dve.wait_ge(s["lowd"], NG // 2)
            link(dve.tensor_tensor_scan(low[:, 1, :], newb[:, 0:NG], low[:, 0, :], 3e38, ALU.max, ALU.min))
            link(dve.tensor_tensor_scan(low[:, 2, ::-1], newb[:, 1:NG + 1][:, ::-1], low[:, 0, ::-1], 3e38,
                                        ALU.max, ALU.min))
            link(dve.tensor_tensor(low[:, 0, :], low[:, 1, :], low[:, 2, :], ALU.min))
            link(dve.tensor_scalar(low[:, 0, :], low[:, 0, :], NOMAX, -1.0, ALU.min, ALU.mult))
            for p_ in range(3):
                link(dve.tensor_copy(guard[:, p_, :], low[:, 0, :]))
                if p_ < 2:
                    link(dve.tensor_tensor(low[:, 0, :], low[:, 0, :], guard[:, p_, :], ALU.subtract))
            dve.sem_inc(s["guards"], 1)

            def add_sums(T, c, first):
                for g in range(B // G0 * c, B // G0 * (c + 1)):
                    o = dve.value_load(offs[0:1, bass.ds(T * (TURN // G0) + g, 1)], min_val=0, max_val=NB * GW)
                    dve.wait_ge(s["pvd"], T * (TURN // G0) + (g + 1))
                    if not (first and g == 0):
                        dve.wait_ge(s["fld"], T * (TURN // G0) + g)
                    z = zacc[0:R, bass.ds(o, GW)]
                    dve.tensor_tensor(z, z, bank[3 + g % 4][0:R, 0:GW], ALU.add).then_inc(s["fld"], 1)

            def soft_turn(T, first):
                for c in range(C):
                    if not first:
                        dve.wait_ge(s["xd"], T * (TURN // 4) + (2 * (c + 1) - TURN // 4))
                    dve.tensor_copy(gring[:, c, :, :], guard[:, :, bass.ds(T * (TURN // G0) + B // G0 * c, B // G0)]
                                    ).then_inc(s["grd"], 1)
                    if c:
                        add_sums(T, c - 1, first)
                    elif not first:
                        add_sums(T - 1, C - 1, False)
            turns(dve, ST, soft_turn)
            add_sums(ST - 1, C - 1, False)
            dve.wait_ge(s["fld"], NG)
            dve.sem_inc(s["zdone"], 1)

            z3 = zacc[0:R, 0:NB * GW].rearrange("p (b w) -> p b w", w=GW)
            none, dsum, dinv = (den[0:R, NB * q_:NB * (q_ + 1)] for q_ in range(3))
            link(dve.tensor_scalar(none, z3[:, :, D], 0.0, None, ALU.is_equal))
            link(dve.memset(padrow[:, :], -1e30))
            dve.sem_inc(s["none"], 1)
            link(dve.tensor_tensor(dsum, z3[:, :, D], none, ALU.add))
            link(dve.reciprocal(dinv, dsum))

            def bc(v, d):
                return v.rearrange("p (b o) -> p b o", o=1).to_broadcast([R, CH, d])

            def chunk(v, k):
                return v[:, CH * D * k:CH * D * (k + 1)]

            def by_block(v):
                return v.rearrange("p (b d) -> p b d", d=D)

            def stats(k, v):
                for b in range(CH * k, CH * (k + 1)):
                    dve.bn_stats(st2[0:R, b, :], v(b)).then_inc(s["dsteps"], 1)
                n_step[0] += CH
                dve.wait_ge(s["dsteps"], n_step[0])
                for b in range(CH * k, CH * (k + 1)):
                    dve.bn_aggr(mv2[0:R, b, :], st2[0:R, b, :]).then_inc(s["dsteps"], 1)
                n_step[0] += CH
                dve.wait_ge(s["dsteps"], n_step[0])

            def ratio(k):
                bl = slice(CH * k, CH * (k + 1))
                link(dve.tensor_tensor(by_block(chunk(ya, k)), z3[:, bl, 0:D], bc(dinv[:, bl], D), ALU.mult))
                dve.wait_ge(s["hn"], 2 * (k + 1))
                link(dve.tensor_tensor(chunk(ya, k), chunk(ya, k), chunk(yb, k), ALU.add))
                stats(k, lambda b: ya[:, D * b:D * (b + 1)])

            def elu(k):
                dve.wait_ge(s["exps"], k + 1)
                dve.wait_ge(s["xm"], k + 1)
                link(dve.scalar_tensor_tensor(chunk(yb, k), chunk(yb, k), 1.0, chunk(xagain, k), ALU.min, ALU.add))
                link(dve.scalar_tensor_tensor(h0[:, CH * k:CH * (k + 1), :].rearrange("p b d -> p (b d)"),
                                              chunk(ya, k), 0.0, chunk(yb, k), ALU.max, ALU.add))
                stats(k, lambda b: h0[:, b, :])
                b = slice(CH * k, CH * (k + 1))
                signal("var2", dve.tensor_scalar(rs2[0:R, b], mv2[0:R, b, 1], EPS, None, ALU.add))

            def scale2(n, b):
                dve.wait_ge(s["dev2"], n)
                link(dve.reciprocal(rs2[0:R, b], rs2[0:R, b]))
                signal("root2", dve.scalar_tensor_tensor(nm2[0:R, b], mv2[0:R, b, 0], -1.0, rs2[0:R, b],
                                                         ALU.mult, ALU.mult))

            def times_gamma(k):
                y = by_block(chunk(ya, k))
                dve.wait_ge(s["norm1"], CH * (k + 1))
                signal("gam", dve.tensor_tensor(
                    y, y, gbc[0:R, 0:D].rearrange("p (o d) -> p o d", o=1).to_broadcast([R, CH, D]), ALU.mult))

            for k in range(NB // CH):
                ratio(k)
            signal("root1", dve.tensor_scalar(rs1[0:R, 0:NB], mv2[0:R, :, 1], EPS, None, ALU.add))
            dve.wait_ge(s["root1"], 2)
            link(dve.reciprocal(rs1[0:R, 0:NB], rs1[0:R, 0:NB]))
            signal("root1", dve.scalar_tensor_tensor(nm1[0:R, 0:NB], mv2[0:R, :, 0], -1.0, rs1[0:R, 0:NB],
                                                     ALU.mult, ALU.mult))
            dve.wait_ge(s["wl1"], 16 * 19)
            times_gamma(0)
            times_gamma(1)
            for k in range(NB // CH):
                if k + 2 < NB // CH:
                    times_gamma(k + 2)
                elu(k)
                if k == 2:
                    scale2(1, slice(0, 3 * CH))
            scale2(2, slice(3 * CH, NB))
            for q_ in range(NPA, (NB + 1) // 2):
                table_out(dve, dve.tensor_copy, q_)
            dve.wait_ge(s["cm"], 1)
            link(dve.tensor_copy(wt[0:1, 5 * D:7 * D], bank[6][0:1, 0:2 * D]))
            link(dve.tensor_copy(w2u[:, 0:2 * D], bank[7][:, 0:2 * D]))
            link(dve.tensor_copy(u3[0:2, :], bank[7][0:2, 2 * D:3 * D]))
            link(dve.tensor_scalar(small[:, 3:4], small[:, 3:4], 1.0, None, ALU.add))
            link(dve.tensor_scalar(w2u[:, 2 * D:3 * D], wt[:, 4 * D:5 * D], small[:, 3:4], None, ALU.mult))
            dve.sem_inc(s["u3d"], 1)
            link(dve.memset(accT[0], 0.0))
            link(dve.memset(accT[1], 0.0))

            passes = dve.value_load(npass[0:1, 0:1], min_val=1, max_val=NPASS)
            with dve.Fori(0, passes) as kp:
                for h in range(2):
                    def flush(nb, i, c, h):
                        for g in range(B // GT):
                            t = i * (TURN // GT) + ((h * HALF + B * c) // GT + g)
                            o = dve.value_load(base[0:1, bass.ds(t, 1)], min_val=0, max_val=N)
                            dve.wait_ge(s["pso"], nb * 2 + (g + 1))
                            dve.wait_ge(s["fld"], nb * 2 + (NG + g))
                            w = accT[h][:, bass.ds(o, WIN)]
                            dve.tensor_tensor(w, w, bank[6 + g][:, 0:WIN], ALU.add).then_inc(s["fld"], 1)

                    def msg_turn(i, first, h=h, last_of=None):
                        tt = kp * (2 * HT) + (h * HT + i)
                        for c in range(C):
                            nb = tt * C + c
                            t0 = i * TURN + (h * HALF + B * c)
                            if not first:
                                dve.wait_ge(s["pso"], nb * 2 + (2 - 2 * C))
                            dve.tensor_tensor(oh1[:, c, :].rearrange("p (k w) -> p k w", k=B),
                                              iota[:, 0:WIN].rearrange("p (o w) -> p o w", o=1).to_broadcast([P, B, WIN]),
                                              rel[:, bass.ds(t0, B)].rearrange("p (k o) -> p k o", o=1).to_broadcast([P, B, WIN]),
                                              ALU.is_equal).then_inc(s["ohd"], 1)
                            dve.wait_ge(s["ea"], nb + 1)
                            dve.wait_ge(s_g1[c], tt * (16 * B) + 16 * B)
                            for g in range(2):
                                w = slice(512 * g, 512 * (g + 1))
                                dve.tensor_tensor(pre[:, c, w], bank[2 * c + g][:, :], g1[:, c, w],
                                                  ALU.add).then_inc(s["addh"], 1)
                            if c:
                                flush(nb - 1, i, c - 1, h)
                            elif last_of is not None:
                                flush(nb - 1, HT - 1, C - 1, last_of)
                            elif not first:
                                flush(nb - 1, i - 1, C - 1, h)
                    if h == 0:
                        turns(dve, HT, msg_turn)
                    else:
                        msg_turn(0, False, last_of=0)
                        with dve.Fori(1, HT) as i:
                            msg_turn(i, False)
                flush(kp * (2 * HT * C) + (2 * HT * C - 1), HT - 1, C - 1, 1)
                dve.wait_ge(s["fld"], (kp + 1) * (2 * HT * TURN // GT) + NG)
                dve.tensor_scalar(rel[:, :], rel[:, :], -float(WIN), None, ALU.add).then_inc(s["nextw"], 1)
                dve.tensor_scalar(base[:, :], base[:, :], float(WIN), float(N), ALU.add, ALU.min).then_inc(s["nextw"], 1)
                dve.wait_ge(s["nextw"], kp * 2 + 2)

            for g in range((NB + 3) // 4):
                b0, b1 = 4 * g, min(4 * g + 4, NB)
                w = D * (b1 - b0)
                q = xagain[:, D * b0:D * b1]
                dve.wait_ge(s["out0"], g + 1)
                dve.tensor_tensor(q, q, bank[g % 3][0:R, 0:w], ALU.add).then_inc(s["hf"], 1)
                dve.wait_ge(s["hf"], g + 1)
                x1 = h0[:, b0:b1, :].rearrange("p b d -> p (b d)")
                dve.scalar_tensor_tensor(x1, q, 0.0, x1, ALU.max, ALU.add).then_inc(s["outd"], 1)


def _lay(inputs):
    import numpy as np

    def slots(v, pad):
        halves = [v[:EH[0]], v[EH[0]:]]
        room = HT * TURN * P
        if pad is None:
            return np.concatenate([np.pad(x, (0, room - len(x)), mode="edge") for x in halves])
        return np.concatenate([np.pad(x, (0, room - len(x)), constant_values=pad) for x in halves])

    g = {k: np.asarray(v) for k, v in inputs.items()}
    src, dst = slots(g["src"], N), slots(g["dst"], None)
    w = slots(g["edge_weight"], 0)
    nat = np.concatenate([src.reshape(Q, B * P), dst.reshape(Q, B * P)], 1)
    col = np.concatenate([src.reshape(NT, P).T, dst.reshape(NT, P).T], 1)
    ea = g["edge_attr_16"].T
    eat = np.zeros((EA + 1, NT * P), ea.dtype)
    eat[0] = 1
    eat[1:, :EH[0]] = ea[:, :EH[0]]
    eat[1:, HT * TURN * P:HT * TURN * P + EH[1]] = ea[:, EH[0]:]
    cst = np.zeros((P, C_W), np.float32)
    cst[:, C_ID:C_ID + P] = np.eye(P)
    cst[:, C_TRI:C_TRI + P] = np.triu(np.ones((P, P)), 1)
    cst[:, C_IOTA:C_IOTA + NG] = np.arange(NG)
    cst[:, C_P] = np.arange(P)
    cst[:, C_PB] = np.arange(P) % NB
    cst[:NB + 1, C_INC:C_S3] = np.triu(np.ones((NB + 1, NB + 1)))
    cst[:3 * TURN, C_S3:] = np.tile(np.eye(TURN), (3, 1))
    return {
        "cst": cst, "nat": nat, "col": col, "w": w.reshape(NT, P).T, "eaT": eat, "x": g["x"],
        "W": g["L0_gnn_W"], "WT": g["L0_gnn_W"].T, "as": g["L0_gnn_a_src"], "ad": g["L0_gnn_a_dst"],
        "gamma": g["L0_gnn_ln_gamma"], "beta": g["L0_gnn_ln_beta"], "req": g["L1_gnn_req_emb"],
        "W1f": g["L1_gnn_W1f"], "W1b": g["L1_gnn_W1b"], "b1f": g["L1_gnn_b1f"], "b1b": g["L1_gnn_b1b"],
        "W2fT": g["L1_gnn_W2f"].T, "W2bT": g["L1_gnn_W2b"].T, "b2f": g["L1_gnn_b2f"], "b2b": g["L1_gnn_b2b"],
        "Wu": g["L1_gnn_Wu"], "bu": g["L1_gnn_bu"], "eps": g["L1_gnn_eps"],
    }


def kernel(**inputs):
    import numpy as _np
    import concourse.bacc as _bacc
    from concourse import mybir as _mybir
    from concourse.bass_utils import run_bass_kernel_spmd as _run

    nc = _bacc.Bacc("TRN2", target_bir_lowering=False, num_devices=1)
    arrays, args = {}, {}
    for name, v in _lay(inputs).items():
        v = _np.ascontiguousarray(v)
        arrays[f"in_{name}"] = v
        args[name] = nc.dram_tensor(f"in_{name}", v.shape, _mybir.dt.from_np(v.dtype), kind="ExternalInput").ap()
    out = nc.dram_tensor("out_x", (N, D), F32, kind="ExternalOutput").ap()
    scratch = {
        "rec": nc.dram_tensor("scr_rec", (P * SW, 3), F32).ap(),
        "H": nc.dram_tensor("scr_H", (N, D), F32).ap(),
        "PP": nc.dram_tensor("scr_PP", (2 * TN, D), F32).ap(),
        "base": nc.dram_tensor("scr_base", (2, NT // GT), F32).ap(),
        "cnt": nc.dram_tensor("scr_cnt", (2 * N,), F32).ap(),
    }
    build(nc, args, out, scratch)
    r = _run(nc, [arrays], core_ids=[0])
    return r.results[0]["out_x"]
```
